# Optimizing a Trainium2 kernel written in Bass

```python
import numpy as np
import jax
import jax.numpy as jnp

def _softmax(x, axis=-1):
    return jax.nn.softmax(x, axis=axis)

def _gelu(x):
    return jax.nn.gelu(x, approximate=True)

def _silu(x):
    return jax.nn.silu(x)

def _sigmoid(x):
    return jax.nn.sigmoid(x)

def _layernorm(x, axis=-1, eps=1e-05):
    m = jnp.mean(x, axis=axis, keepdims=True)
    v = jnp.var(x, axis=axis, keepdims=True)
    return (x - m) / jnp.sqrt(v + eps)

def _scatter_add(tgt, idx, src, axis=0):
    return tgt.at[idx].add(src)

def _segment_sum(src, seg, n):
    return jax.ops.segment_sum(src, seg, n)
kernel_name = 'mk_flamingo_gated_d1_seqx_r4_073d47'

def setup_inputs(seed: int=0):
    np.random.seed(seed)
    _w = jnp.asarray

    def _rec_inputs():
        import jax
        import jax.numpy as jnp
        _rk = jax.random.key(seed)
        x = -0.0002928 + 1 * jax.random.normal(jax.random.fold_in(_rk, 1), (32, 128, 256), jnp.float32)
        _lenS = 128 - jax.random.randint(jax.random.fold_in(_rk, 7), (32,), 0, max(1, 128 // 4) + 1, jnp.int32)
        _lenS2 = 128 - jax.random.randint(jax.random.fold_in(_rk, 8), (32,), 0, max(1, 128 // 4) + 1, jnp.int32)
        _ctx_1024P = jax.random.normal(jax.random.fold_in(_rk, 11), (32, 16, 256), jnp.float32)
        _ctx_1024c = jax.random.dirichlet(jax.random.fold_in(_rk, 511), 0.3 * jnp.ones((16,), jnp.float32), (32, 128))
        _ctx_1024t = jnp.einsum('bsk,bkd->bsd', _ctx_1024c, _ctx_1024P)
        _ctx_1024t = _ctx_1024t * jax.lax.rsqrt(jnp.mean(jnp.square(_ctx_1024t)) + 1e-12) * 0.953939
        ctx_1024 = -1.39393e-06 + 0.999914 * (_ctx_1024t + 0.3 * jax.random.normal(jax.random.fold_in(_rk, 611), (32, 128, 256), jnp.float32))
        _g = jax.random.normal(jax.random.fold_in(_rk, 9001), (2, 1), jnp.float32)
        _g = jnp.sign(_g) * jnp.maximum(jnp.abs(_g), 1.0) + (_g == 0) * 1.0
        g_xattn = _g[0]
        g_ffn = _g[1]
        return (x, ctx_1024, g_xattn, g_ffn)
    x, ctx_1024, g_xattn, g_ffn = _rec_inputs()

    def _L0_xattn_setup():
        import jax, jax.numpy as jnp
        import numpy as np
        B, S, D, NH = (2, 512, 256, 8)
        DH = D // NH
        EPS = 1e-06
        LN_EPS = 1e-05

        def _mlstm_cell(q, k, v, igate_w, igate_b, fgate_w, fgate_b, ln_scale):
            Slen = q.shape[0]
            ifg = jnp.concatenate([q, k, v], axis=-1)
            ig = (ifg @ igate_w.T + igate_b).T
            fg = (ifg @ fgate_w.T + fgate_b).T
            qh = q.reshape(Slen, NH, DH).transpose(1, 0, 2)
            kh = k.reshape(Slen, NH, DH).transpose(1, 0, 2)
            vh = v.reshape(Slen, NH, DH).transpose(1, 0, 2)
            log_f = jax.nn.log_sigmoid(fg)
            cs = jnp.cumsum(log_f, axis=1)
            fg_mat = cs[:, :, None] - cs[:, None, :]
            mask = jnp.tril(jnp.ones((Slen, Slen), dtype=bool))
            log_fg_mat = jnp.where(mask, fg_mat, -jnp.inf)
            log_D = log_fg_mat + ig[:, None, :]
            max_log_D = jnp.max(log_D, axis=-1, keepdims=True)
            D_mat = jnp.exp(log_D - max_log_D)
            qk = jnp.einsum('hsd,htd->hst', qh, kh) / np.sqrt(DH)
            C = qk * D_mat
            normalizer = jnp.maximum(jnp.abs(C.sum(axis=-1, keepdims=True)), jnp.exp(-max_log_D))
            h = jnp.einsum('hst,htd->hsd', C / (normalizer + EPS), vh)
            h = h.transpose(1, 0, 2).reshape(Slen, D)
            mu = h.mean(axis=-1, keepdims=True)
            var = h.var(axis=-1, keepdims=True)
            return (h - mu) / jnp.sqrt(var + LN_EPS) * ln_scale
        key = jax.random.key(seed)
        ks = jax.random.split(key, 8)
        rnd = lambda k, sh, s=1.0: jax.random.normal(k, sh, dtype=jnp.float32) * s
        return {'q': rnd(ks[0], (B, S, D)), 'k': rnd(ks[1], (B, S, D)), 'v': rnd(ks[2], (B, S, D)), 'igate_w': rnd(ks[3], (NH, 3 * D), 0.02), 'igate_b': jnp.linspace(3.0, 6.0, NH, dtype=jnp.float32), 'fgate_w': rnd(ks[4], (NH, 3 * D), 0.02), 'fgate_b': rnd(ks[5], (NH,), 0.3162278), 'ln_scale': jnp.ones((D,), dtype=jnp.float32)}
    _L0_xattn_all = _L0_xattn_setup()
    _L0_xattn_in = {k: v for k, v in _L0_xattn_all.items() if k in ('igate_w', 'igate_b', 'fgate_w', 'fgate_b', 'ln_scale')}
    del _L0_xattn_all

    def _L0_ffn_setup():
        import math
        import jax, jax.numpy as jnp
        import numpy as np
        K = 2
        CAP_FACTOR = 1.0
        EPS = 1e-09
        key = jax.random.key(seed)
        ks = jax.random.split(key, 6)
        B, S, D, H, E = (4, 512, 256, 1024, 8)
        x = jax.random.normal(ks[0], (B, S, D), jnp.float32)
        wg = jax.random.normal(ks[1], (D, E), jnp.float32) * 0.02
        w1 = jax.random.normal(ks[2], (E, D, H), jnp.float32) * 0.02
        b1 = jnp.zeros((E, H), jnp.float32)
        w2 = jax.random.normal(ks[3], (E, H, D), jnp.float32) * 0.02
        b2 = jnp.zeros((E, D), jnp.float32)
        return {'x': x, 'wg': wg, 'w1': w1, 'b1': b1, 'w2': w2, 'b2': b2}
    _L0_ffn_all = _L0_ffn_setup()
    _L0_ffn_in = {k: v for k, v in _L0_ffn_all.items() if k in ('wg', 'w1', 'b1', 'w2', 'b2')}
    del _L0_ffn_all
    return {'x': x, 'ctx_1024': ctx_1024, 'g_xattn': g_xattn, 'g_ffn': g_ffn, 'L0_xattn_igate_w': _L0_xattn_in['igate_w'], 'L0_xattn_igate_b': _L0_xattn_in['igate_b'], 'L0_xattn_fgate_w': _L0_xattn_in['fgate_w'], 'L0_xattn_fgate_b': _L0_xattn_in['fgate_b'], 'L0_xattn_ln_scale': _L0_xattn_in['ln_scale'], 'L0_ffn_wg': _L0_ffn_in['wg'], 'L0_ffn_w1': _L0_ffn_in['w1'], 'L0_ffn_b1': _L0_ffn_in['b1'], 'L0_ffn_w2': _L0_ffn_in['w2'], 'L0_ffn_b2': _L0_ffn_in['b2']}

def reference(x, ctx_1024, g_xattn, g_ffn, L0_xattn_igate_w, L0_xattn_igate_b, L0_xattn_fgate_w, L0_xattn_fgate_b, L0_xattn_ln_scale, L0_ffn_wg, L0_ffn_w1, L0_ffn_b1, L0_ffn_w2, L0_ffn_b2):
    import jax
    import jax.numpy as jnp

    def _L0_xattn_ref(q, k, v, igate_w, igate_b, fgate_w, fgate_b, ln_scale):
        import jax, jax.numpy as jnp
        import numpy as np
        B, S, D, NH = (2, 512, 256, 8)
        DH = D // NH
        EPS = 1e-06
        LN_EPS = 1e-05

        def _mlstm_cell(q, k, v, igate_w, igate_b, fgate_w, fgate_b, ln_scale):
            Slen = q.shape[0]
            ifg = jnp.concatenate([q, k, v], axis=-1)
            ig = (ifg @ igate_w.T + igate_b).T
            fg = (ifg @ fgate_w.T + fgate_b).T
            qh = q.reshape(Slen, NH, DH).transpose(1, 0, 2)
            kh = k.reshape(Slen, NH, DH).transpose(1, 0, 2)
            vh = v.reshape(Slen, NH, DH).transpose(1, 0, 2)
            log_f = jax.nn.log_sigmoid(fg)
            cs = jnp.cumsum(log_f, axis=1)
            fg_mat = cs[:, :, None] - cs[:, None, :]
            mask = jnp.tril(jnp.ones((Slen, Slen), dtype=bool))
            log_fg_mat = jnp.where(mask, fg_mat, -jnp.inf)
            log_D = log_fg_mat + ig[:, None, :]
            max_log_D = jnp.max(log_D, axis=-1, keepdims=True)
            D_mat = jnp.exp(log_D - max_log_D)
            qk = jnp.einsum('hsd,htd->hst', qh, kh) / np.sqrt(DH)
            C = qk * D_mat
            normalizer = jnp.maximum(jnp.abs(C.sum(axis=-1, keepdims=True)), jnp.exp(-max_log_D))
            h = jnp.einsum('hst,htd->hsd', C / (normalizer + EPS), vh)
            h = h.transpose(1, 0, 2).reshape(Slen, D)
            mu = h.mean(axis=-1, keepdims=True)
            var = h.var(axis=-1, keepdims=True)
            return (h - mu) / jnp.sqrt(var + LN_EPS) * ln_scale
        return jax.vmap(lambda qq, kk, vv: _mlstm_cell(qq, kk, vv, igate_w, igate_b, fgate_w, fgate_b, ln_scale))(q, k, v)

    def _L0_ffn_ref(x, wg, w1, b1, w2, b2):
        import math
        import jax, jax.numpy as jnp
        import numpy as np
        K = 2
        CAP_FACTOR = 1.0
        EPS = 1e-09
        B, S, D = x.shape
        E = wg.shape[1]
        xt = x.reshape(-1, D)
        N = xt.shape[0]
        cap = int(math.ceil(CAP_FACTOR * K * N / E))
        logits = xt.astype(jnp.float32) @ wg.astype(jnp.float32)
        scores = jax.nn.softmax(logits, axis=-1)
        gvals, gidx = jax.lax.top_k(scores, K)
        gvals = gvals / jnp.clip(gvals.sum(-1, keepdims=True), EPS)
        offset = jnp.zeros((E,), jnp.int32)
        pos_l, keep_l = ([], [])
        for kk in range(K):
            m = jax.nn.one_hot(gidx[:, kk], E, dtype=jnp.int32)
            loc = jnp.cumsum(m, axis=0) - 1 + offset[None, :]
            offset = offset + m.sum(axis=0)
            pos = jnp.take_along_axis(loc, gidx[:, kk:kk + 1], axis=1)[:, 0]
            keep = pos < cap
            pos_l.append(jnp.where(keep, pos, 0))
            keep_l.append(keep)
        pos = jnp.stack(pos_l, axis=1)
        keep = jnp.stack(keep_l, axis=1)
        gvals = gvals * keep
        e_flat = gidx.reshape(-1)
        p_flat = pos.reshape(-1)
        kmask = keep.reshape(-1).astype(x.dtype)
        x_rep = jnp.repeat(xt, K, axis=0)
        disp = jnp.zeros((E, cap, D), x.dtype).at[e_flat, p_flat].add(x_rep * kmask[:, None])
        h = jax.nn.gelu(jnp.einsum('ecd,edh->ech', disp, w1) + b1[:, None, :], approximate=False)
        y = jnp.einsum('ech,ehd->ecd', h, w2) + b2[:, None, :]
        yk = y[e_flat, p_flat]
        w = gvals.reshape(-1).astype(x.dtype)
        out = (yk * w[:, None]).reshape(N, K, D).sum(axis=1)
        return out.reshape(B, S, D)
    x = x + jnp.tanh(g_xattn[0]) * _L0_xattn_ref(_layernorm(x, axis=-1), ctx_1024, ctx_1024, L0_xattn_igate_w, L0_xattn_igate_b, L0_xattn_fgate_w, L0_xattn_fgate_b, L0_xattn_ln_scale)
    x = x + jnp.tanh(g_ffn[0]) * _L0_ffn_ref(_layernorm(x, axis=-1), L0_ffn_wg, L0_ffn_w1, L0_ffn_b1, L0_ffn_w2, L0_ffn_b2)
    return x

_drawn_inputs = setup_inputs


def setup_inputs(seed=0):
    import zlib

    import numpy as np

    out = dict(_drawn_inputs(seed))
    spreads = {'L0_xattn_ln_scale': (1.0, 0.2), 'L0_ffn_b1': (0.0, 0.456), 'L0_ffn_b2': (0.0, 0.1)}
    factors = {}
    for name, (base, spread) in spreads.items():
        noise = np.random.default_rng([zlib.crc32(name.encode()), seed]).standard_normal(out[name].shape)
        drawn = base * np.exp(spread * noise) if base else spread * noise
        out[name] = jnp.asarray(drawn.astype(out[name].dtype))
    for name, factor in factors.items():
        out[name] = (out[name] * factor).astype(out[name].dtype)
    return out
```

```python
from contextlib import ExitStack

import concourse.bass as bass
from concourse import mybir

F32 = mybir.dt.float32
F32R = mybir.dt.float32r
BF16 = mybir.dt.bfloat16
I32 = mybir.dt.int32
U32 = mybir.dt.uint32
ALU = mybir.AluOpType
ACT = mybir.ActivationFunctionType
AX_X = mybir.AxisListType.X

P = 128
LN_EPS = 1e-5
NORM_EPS = 1e-6
GATE_EPS = 1e-9
MASKED = -1.0e30
LOWEST = -3.0e38


def flamingo_block(nc, x, ctx_in, g_xattn, g_ffn, igate_w, igate_b, fgate_w, fgate_b, ln_scale,
                   wg, w1, b1, w2, b2, out):
    B, S, D = x.shape
    HEADS = igate_w.shape[0]
    DH = D // HEADS
    DC = D // P
    E, _, HID = w1.shape
    HC = HID // P
    TOP = 2
    N = B * S
    CAP = -(-TOP * N // E)
    assert S == P and HEADS * DH == D and CAP % P == 0 and B % 16 == 0

    GB = 4
    GROUPS = B // GB
    GW = GB * S
    PAIR_TILES = B * HEADS // P
    BT = B // PAIR_TILES
    PARTS = 3
    KA = PARTS * HEADS
    VW = DH + 1
    VWIN = 3 * VW
    LPAD = 96
    SLOT_TILES = CAP // P
    KT = TOP * B
    UNITS = 2 * E
    UT = SLOT_TILES // 2
    UW = UT * P

    gates_dram = nc.dram_tensor("gates_scratch", [2 * HEADS, N], F32, kind="Internal").ap()
    a_dram = nc.dram_tensor("a_scratch", [B, PARTS, HEADS, S], BF16, kind="Internal").ap()
    m_dram = nc.dram_tensor("m_scratch", [B, PARTS, HEADS, S], BF16, kind="Internal").ap()
    xn_dram = nc.dram_tensor("xn_scratch", [N, D], F32, kind="Internal").ap()
    acc_dram = nc.dram_tensor("acc_scratch", [N + CAP, D], F32, kind="Internal").ap()

    x_rows = x.rearrange("b s d -> (b s) d")
    ctx_rows = ctx_in.rearrange("b s d -> (b s) d")
    out_rows = out.rearrange("b s d -> (b s) d")

    with ExitStack() as keep:
        def sb(name, shape, dt=F32, stack=keep):
            return stack.enter_context(nc.sbuf_tensor(name, shape, dt))

        def sem(name):
            return keep.enter_context(nc.semaphore(name))

        ident = sb("ident", [P, P])
        ident_bf = sb("ident_bf", [P, P], BF16)
        ones_bf = sb("ones_bf", [P, P], BF16)
        tri_bf = sb("tri_bf", [P, P], BF16)
        w_raw1 = sb("w_raw1", [P, DC, HID])
        w_raw2 = sb("w_raw2", [P, HC, D])
        b1_rows = sb("b1_rows", [E * HC, P])
        b1_cols = sb("b1_cols", [P, E * HC])
        b2_all = sb("b2_all", [P, E, D])
        gx = sb("gx", [P, 2])
        tanh_g = sb("tanh_g", [P, 2])
        logits = sb("logits", [P, B, E])
        slot_w = sb("slot_w", [P, E * SLOT_TILES])
        gather_idx = sb("gather_idx", [P, E * SLOT_TILES], U32)
        scatter_idx = sb("scatter_idx", [P, E * SLOT_TILES], U32)

        att = ExitStack()
        qT = sb("qT", [P, DC, N], stack=att)
        kT = sb("kT", [P, DC, N], stack=att)
        cell = ExitStack()
        x_in = sb("x_in", [P, 2, GB, D], stack=cell)
        c_in = sb("c_in", [P, 2, GB, D], stack=cell)
        q_rows = sb("q_rows", [P, 2, GB, D], stack=cell)
        g_stats = sb("g_stats", [P, GB, 6], stack=cell)
        g_mv = sb("g_mv", [P, 2, GB, 2], stack=cell)
        g_var = sb("g_var", [P, GB], stack=cell)
        g_rstd = sb("g_rstd", [P, 2, GB], stack=cell)
        gate_rows = sb("gate_rows", [2 * HEADS, 3 * D], stack=cell)
        gate_wT = sb("gate_wT", [P, 3 * DC, 2 * HEADS], stack=cell)
        gate_wk = sb("gate_wk", [P, DC, 2 * HEADS], stack=cell)
        gate_b = sb("gate_b", [2 * HEADS, 1], stack=cell)
        gates_sb = sb("gates_sb", [2 * HEADS, 2, GW], stack=cell)
        neg_half = sb("neg_half", [P, GB], stack=cell)
        PW = PAIR_TILES * S
        ig_p = sb("ig_p", [P, PAIR_TILES, S], stack=cell)
        fg_p = sb("fg_p", [P, PAIR_TILES, S], stack=cell)
        fa = sb("fa", [P, PW], stack=cell)
        fe = sb("fe", [P, PW], stack=cell)
        fl = sb("fl", [P, PW], stack=cell)
        logf = sb("logf", [P, PW], stack=cell)
        cs = sb("cs", [P, PW], stack=cell)
        av = sb("av", [P, PW], stack=cell)
        mv = sb("mv", [P, PW], stack=cell)
        msum = sb("msum", [P, PW], stack=cell)
        nm = sb("nm", [P, PW], stack=cell)
        res1 = sb("res1", [P, 2, PW], stack=cell)
        negm = sb("negm", [P, PW], stack=cell)
        parts = sb("parts", [P, 2, PARTS, PW], BF16, stack=cell)
        ones_row = sb("ones_row", [P, S], stack=cell)
        zero_row = sb("zero_row", [P, S], stack=cell)
        nmT = sb("nmT", [P, B * HEADS], stack=cell)
        mask_bf = sb("mask_bf", [P, 4, S], BF16, stack=cell)
        z_lhs = sb("z_lhs", [P, 2, S], BF16, stack=cell)
        z_rhs = sb("z_rhs", [P, 2, HEADS * S], BF16, stack=cell)
        sel_f = sb("sel_f", [P, HEADS, S], BF16, stack=cell)
        k_st = sb("k_st", [P, 2, DC, S], stack=cell)
        q_bd = sb("q_bd", [P, 2, DC, 4 * S], stack=cell)
        x_c = sb("x_c", [P, 2, D], stack=cell)
        c_c = sb("c_c", [P, 2, D], stack=cell)
        v_ext = sb("v_ext", [P, 2, (HEADS + 2) * VW], stack=cell)
        decay = sb("decay", [P, 2, HEADS * S], stack=cell)
        cT = sb("cT", [P, 2, HEADS * S], stack=cell)
        den = sb("den", [P, HEADS], stack=cell)
        den2 = sb("den2", [P, HEADS], stack=cell)
        rden = sb("rden", [P, HEADS], stack=cell)
        hn = sb("hn", [P, HEADS, DH], stack=cell)
        h_st = sb("h_st", [P, 6], stack=cell)
        h_mv = sb("h_mv", [P, 2, 2], stack=cell)
        h_var = sb("h_var", [P, 1], stack=cell)
        h_rstd = sb("h_rstd", [P, 2, 1], stack=cell)
        h_sc = sb("h_sc", [P, 2, D], stack=cell)
        ls = sb("ls", [P, D], stack=cell)
        ls_t = sb("ls_t", [P, D], stack=cell)
        x1 = sb("x1", [P, 2, D], stack=cell)
        x_st = sb("x_st", [P, 6], stack=cell)
        x_mv = sb("x_mv", [P, 2, 2], stack=cell)
        x_var = sb("x_var", [P, 1], stack=cell)
        x_rstd = sb("x_rstd", [P, 2, 1], stack=cell)
        xn = sb("xn", [P, 2, D], stack=cell)
        xnT = sb("xnT", [P, DC, S], stack=cell)
        wg_sb = sb("wg_sb", [P, DC, E], stack=cell)
        wg_pad = sb("wg_pad", [P, DC, LPAD // E, E], stack=cell)
        cell.close()
        route = ExitStack()

        def rt(name, shape, dt=F32):
            return sb(name, shape, dt, stack=route)

        rmax = rt("rmax", [P, B])
        rz = rt("rz", [P, B, E])
        rexp = rt("rexp", [P, B, E])
        rsum = rt("rsum", [P, B])
        rrec = rt("rrec", [P, B])
        score = rt("score", [P, B, E])
        best = rt("best", [P, TOP, B])
        req = rt("req", [P, B, E])
        rkey = rt("rkey", [P, B, E])
        kmax = rt("kmax", [P, TOP, B])
        score2 = rt("score2", [P, B, E])
        chosen = rt("chosen", [P, B, E])
        rank = rt("rank", [P, B, E])
        onehot = rt("onehot", [P, E, TOP, B], BF16)
        reset = rt("reset", [P, E, KT])
        gsum = rt("gsum", [P, B])
        gclip = rt("gclip", [P, B])
        grec = rt("grec", [P, B])
        gval = rt("gval", [P, TOP, B])
        gw_t = rt("gw_t", [P, KT])
        before = rt("before", [P, E * KT])
        loc0 = rt("loc0", [P, E * KT])
        loc = rt("loc", [P, E, KT])
        locsel = rt("locsel", [P, E, KT])
        pos = rt("pos", [P, KT])
        pos_i = rt("pos_i", [P, KT], I32)
        row_i = rt("row_i", [P, KT], I32)
        col_i = rt("col_i", [P, KT], I32)
        row_f = rt("row_f", [P, KT])
        col_f = rt("col_f", [P, KT])
        col_b = rt("col_b", [P, KT])
        col_s = rt("col_s", [P, KT])
        token1 = rt("token1", [P, TOP, B])
        token_i = rt("token_i", [P, TOP, B], I32)
        iota_i = rt("iota_i", [P, P], I32)
        iota_f = rt("iota_f", [P, P])
        colhot = rt("colhot", [P, KT, E * SLOT_TILES])
        dump_i = rt("dump_i", [P, E, SLOT_TILES], I32)
        dump = rt("dump", [P, E * SLOT_TILES])
        slot_t = rt("slot_t", [P, E * SLOT_TILES])
        empty = rt("empty", [P, E * SLOT_TILES])
        dumped = rt("dumped", [P, E * SLOT_TILES])
        rowhot = qT[:].rearrange("p c n -> p (c n)").rearrange("p (k r) -> p k r", r=P)
        colval = kT[:].rearrange("p c n -> p (c n)").rearrange("p (k r) -> p k r", r=P)
        route.close()
        att.close()
        w1h = sb("w1h", [P, 2, DC, HID], F32R)
        w1l = sb("w1l", [P, 2, DC, HID], F32R)
        w2h = sb("w2h", [P, 2, HC, D], F32R)
        w2l = sb("w2l", [P, 2, HC, D], F32R)
        xg = sb("xg", [P, 2, UT, D])
        g_ix = sb("g_ix", [P, 2, UT], U32)
        s_ix = sb("s_ix", [P, 2, UT], U32)
        xh = sb("xh", [P, 2, DC, UW], F32R)
        xl = sb("xl", [P, 2, DC, UW], F32R)
        hf = sb("hf", [P, 3, UW])
        hh = sb("hh", [P, 2, HC, UW], F32R)
        hl = sb("hl", [P, 2, HC, UW], F32R)
        y_b = sb("y_b", [P, 2, UT, D])
        y_w = sb("y_w", [P, 2, UT, D])

        ps = keep.enter_context(nc.psum_tensor("ps", [P, 8, 512], F32))

        waited = sem("waited")
        const_ready = sem("const_ready")
        misc_ld = sem("misc_ld")
        w_ld = sem("w_ld")
        x_ld = [sem("x_ld0"), sem("x_ld1")]
        c_ld = [sem("c_ld0"), sem("c_ld1")]
        wT_done = sem("wT_done")
        wT_copied = sem("wT_copied")
        wk_ready = sem("wk_ready")
        stats_done = sem("stats_done")
        g_seq = sem("g_seq")
        rstd_seq = sem("rstd_seq")
        rstd_done = sem("rstd_done")
        q_done = sem("q_done")
        kT_ps = sem("kT_ps")
        qT_ps = sem("qT_ps")
        kT_done = sem("kT_done")
        qT_done = sem("qT_done")
        gate_ps = sem("gate_ps")
        gate_done = sem("gate_done")
        gate_st = [sem("gate_st0"), sem("gate_st1")]
        pair_ld = sem("pair_ld")
        sc_v = sem("sc_v")
        sc_a = sem("sc_a")
        nmT_ps = sem("nmT_ps")
        nmT_done = sem("nmT_done")
        part_st = sem("part_st")
        tg_done = sem("tg_done")
        const_v = sem("const_v")
        pe_ld = [sem("pe_ld0"), sem("pe_ld1")]
        xc_ld = [sem("xc_ld0"), sem("xc_ld1")]
        v_ready = sem("v_ready")
        z_ps = sem("z_ps")
        s_ps = sem("s_ps")
        exp_done = sem("exp_done")
        cT_done = sem("cT_done")
        h_ps = sem("h_ps")
        p1_seq = sem("p1_seq")
        hn_done = sem("hn_done")
        h_stat = sem("h_stat")
        h_pool = sem("h_pool")
        h_rs = sem("h_rs")
        hsc_done = sem("hsc_done")
        x1_done = sem("x1_done")
        x1_seq = sem("x1_seq")
        x_stat = sem("x_stat")
        x_pool = sem("x_pool")
        x_rs = sem("x_rs")
        xn_done = sem("xn_done")
        xnT_ps = sem("xnT_ps")
        xnT_done = sem("xnT_done")
        lg_ps = sem("lg_ps")
        lg_done = sem("lg_done")
        x1_st = [sem("x1_st0"), sem("x1_st1")]
        xn_st = [sem("xn_st0"), sem("xn_st1")]
        dump_st = sem("dump_st")
        rt_v = sem("rt_v")
        rt_a = sem("rt_a")
        rt_p = sem("rt_p")
        rt_c = sem("rt_c")
        count_ps = sem("count_ps")
        cv_id = sem("cv_id")
        cv_w = sem("cv_w")
        rh_done = sem("rh_done")
        slot_ps = sem("slot_ps")
        slots_done = sem("slots_done")
        w1h_done = sem("w1h_done")
        w1l_done = sem("w1l_done")
        w2h_done = sem("w2h_done")
        w2l_done = sem("w2l_done")
        ix_done = sem("ix_done")
        xg_ld = [sem("xg_ld0"), sem("xg_ld1")]
        xT_ps = sem("xT_ps")
        xh_done = sem("xh_done")
        xl_done = sem("xl_done")
        g1_ps = sem("g1_ps")
        gelu_done = sem("gelu_done")
        hh_done = sem("hh_done")
        hl_done = sem("hl_done")
        y_ps = sem("y_ps")
        yb_done = sem("yb_done")
        yw_done = sem("yw_done")
        six_done = sem("six_done")
        y_st = sem("y_st")
        out_st = sem("out_st")

        LAST_G = GROUPS
        MISC = 9
        CONSTS = 9
        NJ = 4

        block = keep.enter_context(nc.Block())

        @block.sync
        def _(sp):
            sp.dma_start(gate_rows[0:HEADS, :], igate_w).then_inc(misc_ld, 16)
            sp.dma_start(gate_rows[HEADS:2 * HEADS, :], fgate_w).then_inc(misc_ld, 16)
            sp.dma_start(gate_b[0:HEADS, :], igate_b.rearrange("(h a) -> h a", a=1)).then_inc(misc_ld, 16)
            sp.dma_start(gate_b[HEADS:2 * HEADS, :], fgate_b.rearrange("(h a) -> h a", a=1)).then_inc(misc_ld, 16)

            def load_group(g, k):
                if not isinstance(g, int) or g >= 2:
                    sp.wait_ge(q_done, 4 * (g - 1))
                    sp.sem_inc(waited, 1)
                    sp.wait_ge(kT_ps, 2 * (g - 1))
                    sp.sem_inc(waited, 1)
                sp.dma_start(x_in[:, k], x_rows[bass.ds(g * GW, GW)].rearrange("(b p) d -> p b d", p=P)).then_inc(x_ld[k], 16)
                sp.dma_start(c_in[:, k], ctx_rows[bass.ds(g * GW, GW)].rearrange("(b p) d -> p b d", p=P)).then_inc(c_ld[k], 16)

            load_group(0, 0)
            load_group(1, 1)
            sp.dma_start(ls[:], ln_scale.rearrange("(a d) -> a d", a=1).broadcast_to([P, D])).then_inc(misc_ld, 16)
            sp.dma_start(gx[:, 0:1], g_xattn.rearrange("(a d) -> a d", a=1).broadcast_to([P, 1])).then_inc(misc_ld, 16)
            sp.dma_start(gx[:, 1:2], g_ffn.rearrange("(a d) -> a d", a=1).broadcast_to([P, 1])).then_inc(misc_ld, 16)
            sp.dma_start(b1_rows[:], b1.rearrange("e (m p) -> (e m) p", p=P)).then_inc(misc_ld, 16)
            sp.dma_start(wg_sb[:], wg.rearrange("(c p) e -> p c e", p=P)).then_inc(misc_ld, 16)

            def store_gates(g, k):
                sp.wait_ge(gate_done, g + 1)
                sp.dma_start(gates_dram[:, bass.ds(g * GW, GW)], gates_sb[:, k, :]).then_inc(gate_st[k], 16)

            with sp.Fori(1, GROUPS // 2) as i:
                for k in range(2):
                    load_group(2 * i + k, k)
                    store_gates(2 * i - 2 + k, k)
            sp.dma_start(b2_all[:], b2.rearrange("(a e) d -> a e d", a=1).broadcast_to([P, E, D])).then_inc(w_ld, 16)
            sp.dma_start(w_raw1[:], w1[0].rearrange("(c p) h -> p c h", p=P)).then_inc(w_ld, 16)
            sp.dma_start(w_raw2[:], w2[0].rearrange("(k p) d -> p k d", p=P)).then_inc(w_ld, 16)
            for g in (GROUPS - 2, GROUPS - 1):
                store_gates(g, g % 2)

            for k in range(2):
                sp.wait_ge(gate_st[k], 16 * (GROUPS // 2))
            pairs = gates_dram.rearrange("h (b s) -> b h s", s=S)
            for t in range(PAIR_TILES):
                sp.dma_start(fg_p[:, t], pairs[t * BT:(t + 1) * BT, HEADS:2 * HEADS]).then_inc(pair_ld, 16)
            for t in range(PAIR_TILES):
                sp.dma_start(ig_p[:, t], pairs[t * BT:(t + 1) * BT, 0:HEADS]).then_inc(pair_ld, 16)

            def load_x(b, k):
                if not isinstance(b, int) or b >= 2:
                    sp.wait_ge(x1_done, b - 1)
                    sp.wait_ge(v_ready, b - 1)
                sp.dma_start(x_c[:, k], x_rows[bass.ds(b * S, S)]).then_inc(xc_ld[k], 16)
                sp.dma_start(c_c[:, k], ctx_rows[bass.ds(b * S, S)]).then_inc(xc_ld[k], 16)

            def load_pe(b, k):
                if not isinstance(b, int) or b >= 2:
                    sp.wait_ge(s_ps, b - 1)
                sp.dma_start(k_st[:, k], kT[:, :, bass.ds(b * S, S)]).then_inc(pe_ld[k], 16)
                for j in range(NJ):
                    sp.dma_start(q_bd[j * DH:(j + 1) * DH, k, :, j * S:(j + 1) * S],
                                 qT[j * DH:(j + 1) * DH, :, bass.ds(b * S, S)]).then_inc(pe_ld[k], 16)
                sp.dma_start(z_lhs[PARTS:PARTS + KA, k], a_dram[bass.ds(b, 1)].rearrange("b j h s -> (b j h) s")).then_inc(pe_ld[k], 16)
                sp.dma_start(z_rhs[0:PARTS, k], m_dram[bass.ds(b, 1)].rearrange("b j h s -> (b j) (h s)")).then_inc(pe_ld[k], 16)

            def store_rows(b, k):
                sp.wait_ge(x1_done, b + 1)
                sp.dma_start(acc_dram[bass.ds(b * S, S)], x1[:, k]).then_inc(x1_st[k], 16)
                sp.wait_ge(xn_done, b + 1)
                sp.dma_start(xn_dram[bass.ds(b * S, S)], xn[:, k]).then_inc(xn_st[k], 16)

            for n, dst in ((0, a_dram), (1, m_dram)):
                sp.wait_ge(sc_v, 13 + 4 * n)
                for j in range(PARTS):
                    for t in range(PAIR_TILES):
                        sp.dma_start(dst[t * BT:(t + 1) * BT, j], parts[:, n, j, t * S:(t + 1) * S]).then_inc(part_st, 16)
            sp.wait_ge(qT_done, LAST_G)
            sp.wait_ge(kT_done, 2 * LAST_G)
            sp.wait_ge(const_ready, CONSTS)
            sp.wait_ge(nmT_done, 1)
            sp.wait_ge(part_st, 16 * 2 * PARTS * PAIR_TILES)
            for b in range(2):
                load_x(b, b)
                load_pe(b, b)
            sp.wait_ge(const_v, 2)
            sp.dma_start(acc_dram[N:N + CAP].rearrange("(p j) d -> p (j d)", p=P), decay[:].rearrange("p a b -> p (a b)")).then_inc(dump_st, 16)
            sp.wait_ge(dump_st, 16)

            load_pe(2, 0)
            load_pe(3, 1)
            load_x(2, 0)
            store_rows(0, 0)
            with sp.Fori(2, B // 2) as i:
                for k in range(2):
                    load_pe(2 * i + k, k)
                    load_x(2 * i + k - 1, 1 - k)
                    store_rows(2 * i + k - 3, 1 - k)
            load_x(B - 1, 1)
            for b in (B - 3, B - 2, B - 1):
                store_rows(b, b % 2)

            with sp.Fori(1, E) as e:
                sp.wait_ge(w1h_done, e)
                sp.wait_ge(w1l_done, e)
                sp.dma_start(w_raw1[:], w1[bass.ds(e, 1)].rearrange("e (c p) h -> p (e c) h", p=P)).then_inc(w_ld, 16)
                sp.wait_ge(w2h_done, e)
                sp.wait_ge(w2l_done, e)
                sp.dma_start(w_raw2[:], w2[bass.ds(e, 1)].rearrange("e (k p) d -> p (e k) d", p=P)).then_inc(w_ld, 16)

            sp.wait_ge(y_st, 16 * E * SLOT_TILES)
            for q in range(4):
                rows = slice(q * N // 4, (q + 1) * N // 4)
                sp.dma_start(out_rows[rows], acc_dram[rows]).then_inc(out_st, 16)
            sp.wait_ge(out_st, 16 * 4)

        @block.gpsimd
        def _(pool):
            nc.gpsimd.memset(ident[:], 0.0).then_inc(rt_c, 1)
            nc.gpsimd.memset(tri_bf[:], 1.0).then_inc(rt_c, 1)
            nc.gpsimd.memset(mask_bf[:], 0.0).then_inc(rt_c, 1)
            nc.gpsimd.memset(z_rhs[:], 0.0).then_inc(rt_c, 1)
            nc.gpsimd.memset(sel_f[:], 1.0).then_inc(rt_c, 1)
            nc.gpsimd.memset(neg_half[:], -0.5).then_inc(const_ready, 1)
            pool.wait_ge(rt_c, 5)
            nc.gpsimd.affine_select(out=ident[:], in_=ident[:], compare_op=ALU.not_equal, fill=1.0, base=0,
                                    pattern=[[-1, P]], channel_multiplier=1).then_inc(const_ready, 1)
            pool.wait_ge(const_ready, 2)
            nc.gpsimd.tensor_copy(ident_bf[:], ident[:]).then_inc(const_ready, 1)
            nc.gpsimd.affine_select(out=tri_bf[:], in_=tri_bf[:], compare_op=ALU.is_ge, fill=0.0, base=0,
                                    pattern=[[1, P]], channel_multiplier=-1).then_inc(const_ready, 1)
            nc.gpsimd.affine_select(out=mask_bf[:], in_=mask_bf[:], compare_op=ALU.is_ge, fill=MASKED, base=0,
                                    pattern=[[0, 4], [1, S]], channel_multiplier=-1).then_inc(const_ready, 1)
            nc.gpsimd.memset(z_lhs[:], 0.0).then_inc(rt_c, 1)
            nc.gpsimd.memset(v_ext[:], 1.0).then_inc(const_ready, 1)
            for j in range(PARTS):
                pool.wait_ge(rt_c, 6 + j)
                nc.gpsimd.affine_select(out=sel_f[:], in_=sel_f[:], compare_op=ALU.not_equal, fill=0.0,
                                        base=-(PARTS + j * HEADS), pattern=[[-1, HEADS], [0, S]],
                                        channel_multiplier=1).then_inc(rt_c, 1)
            pool.wait_ge(rt_c, 9)
            for k in range(2):
                nc.gpsimd.tensor_scalar(z_rhs[:, k].rearrange("p (h s) -> p h s", h=HEADS), sel_f[:], -1.0, 1.0,
                                        ALU.mult, ALU.add).then_inc(const_ready, 1)
            nc.gpsimd.memset(z_lhs[0:PARTS], 1.0).then_inc(const_ready, 1)

            def group_rstd(g, k):
                pool.wait_ge(stats_done, g + 1)
                if not isinstance(g, int) or g >= 1:
                    pool.wait_ge(rstd_done, g)
                if not isinstance(g, int) or g >= 2:
                    pool.wait_ge(q_done, GB * (g - 1))
                pool.sem_inc(waited, 1)
                nc.gpsimd.tensor_scalar(g_var[:], g_mv[:, k, :, 1], LN_EPS, None, ALU.add).then_inc(rstd_seq, 1)
                pool.wait_ge(rstd_seq, g + 1)
                nc.gpsimd.tensor_tensor(g_rstd[:, k], g_var[:], neg_half[:], ALU.pow).then_inc(rstd_done, 1)

            for g in range(4):
                group_rstd(g, g % 2)
            with pool.Fori(2, GROUPS // 2) as i:
                for k in range(2):
                    group_rstd(2 * i + k, k)

            def values(b, k):
                pool.wait_ge(xc_ld[k], 32 * ((b - k) // 2) + 32 if isinstance(b, int) else 16 * (b - k) + 32)
                if not isinstance(b, int) or b >= 2:
                    pool.wait_ge(h_ps, b - 1)
                pool.sem_inc(waited, 1)
                nc.gpsimd.tensor_copy(v_ext[:, k, 0:HEADS * VW].rearrange("p (h e) -> p h e", e=VW)[:, :, 0:DH],
                                      c_c[:, k].rearrange("p (h e) -> p h e", e=DH)).then_inc(v_ready, 1)

            def head_rstd(b, k):
                pool.wait_ge(h_stat, b + 1)
                if not isinstance(b, int) or b >= 1:
                    pool.wait_ge(h_rs, b)
                if not isinstance(b, int) or b >= 2:
                    pool.wait_ge(x1_done, b - 1)
                pool.sem_inc(waited, 1)
                nc.gpsimd.tensor_scalar(h_var[:], h_mv[:, k, 1:2], LN_EPS, None, ALU.add).then_inc(h_pool, 1)
                pool.wait_ge(h_pool, b + 1)
                nc.gpsimd.tensor_tensor(h_rstd[:, k], h_var[:], neg_half[:, 0:1], ALU.pow).then_inc(h_rs, 1)

            def row_rstd(b, k):
                pool.wait_ge(x_stat, b + 1)
                if not isinstance(b, int) or b >= 1:
                    pool.wait_ge(x_rs, b)
                if not isinstance(b, int) or b >= 2:
                    pool.wait_ge(xn_done, b - 1)
                pool.sem_inc(waited, 1)
                nc.gpsimd.tensor_scalar(x_var[:], x_mv[:, k, 1:2], LN_EPS, None, ALU.add).then_inc(x_pool, 1)
                pool.wait_ge(x_pool, b + 1)
                nc.gpsimd.tensor_tensor(x_rstd[:, k], x_var[:], neg_half[:, 0:1], ALU.pow).then_inc(x_rs, 1)

            for b in range(4):
                values(b, b % 2)
                if b >= 1:
                    head_rstd(b - 1, (b - 1) % 2)
                    row_rstd(b - 1, (b - 1) % 2)
            with pool.Fori(2, B // 2) as i:
                for k in range(2):
                    values(2 * i + k, k)
                    head_rstd(2 * i + k - 1, 1 - k)
                    row_rstd(2 * i + k - 1, 1 - k)
            head_rstd(B - 1, 1)
            row_rstd(B - 1, 1)

            pool.wait_ge(xn_done, B)
            pool.wait_ge(lg_done, B)
            for k in range(2):
                pool.wait_ge(xn_st[k], 16 * (B // 2))
                pool.wait_ge(x1_st[k], 16 * (B // 2))
            nc.gpsimd.iota(iota_i[:], pattern=[[1, P]], base=0, channel_multiplier=0).then_inc(rt_p, 1)
            nc.gpsimd.iota(token_i[:], pattern=[[0, TOP], [S, B]], base=1, channel_multiplier=1).then_inc(rt_p, 1)
            nc.gpsimd.iota(dump_i[:], pattern=[[0, E], [1, SLOT_TILES]], base=N + 1, channel_multiplier=SLOT_TILES).then_inc(rt_p, 1)
            for e in range(E):
                nc.gpsimd.memset(rank[:, :, e:e + 1], float(E - e)).then_inc(rt_p, 1)
            nc.gpsimd.memset(reset[:], 1.0).then_inc(rt_p, 1)
            pool.wait_ge(rt_p, 12)
            nc.gpsimd.memset(reset[:, :, 0:1], 0.0).then_inc(rt_p, 1)
            nc.gpsimd.tensor_copy(iota_f[:], iota_i[:]).then_inc(rt_p, 1)
            nc.gpsimd.tensor_copy(token1[:], token_i[:]).then_inc(rt_p, 1)
            nc.gpsimd.tensor_copy(dump[:], dump_i[:].rearrange("p e j -> p (e j)")).then_inc(rt_p, 1)

            for q in range(4):
                pool.wait_ge(rt_v, 33 + q)
                ks = slice(q * KT // 4, (q + 1) * KT // 4)
                nc.gpsimd.tensor_tensor(colval[:, ks, E * SLOT_TILES:],
                                        colhot[:, ks, :], gw_t[:, ks].unsqueeze(2).broadcast_to([P, KT // 4, E * SLOT_TILES]),
                                        ALU.mult).then_inc(cv_w, 1)

            pool.wait_ge(slots_done, 3)
            for k in range(2):
                pool.wait_ge(xn_st[k], 16 * (B // 2))
            pool.wait_ge(dump_st, 16)

            def gather(u, k):
                if not isinstance(u, int) or u >= 2:
                    pool.wait_ge(xT_ps, 2 * (u - 1))
                    pool.wait_ge(xg_ld[k], 8 * UT * (u - k))
                pool.sem_inc(waited, 1)
                nc.gpsimd.tensor_copy(g_ix[:, k], gather_idx[:, bass.ds(u * UT, UT)]).then_inc(ix_done, 1)
                pool.wait_ge(ix_done, u + 1)
                pool.sem_inc(waited, 1)
                for j in range(UT):
                    nc.gpsimd.indirect_dma_start(xg[:, k, j], None, xn_dram,
                                                 bass.IndirectOffsetOnAxis(ap=g_ix[:, k, j:j + 1], axis=0)).then_inc(xg_ld[k], 16)

            def scatter(u, k):
                if not isinstance(u, int) or u >= 1:
                    pool.wait_ge(y_st, 16 * UT * u)
                pool.sem_inc(waited, 1)
                nc.gpsimd.tensor_copy(s_ix[:, k], scatter_idx[:, bass.ds(u * UT, UT)]).then_inc(six_done, 1)
                pool.wait_ge(six_done, u + 1)
                for j in range(UT):
                    pool.wait_ge(yw_done, UT * u + j + 1)
                    pool.sem_inc(waited, 1)
                    nc.gpsimd.indirect_dma_start(acc_dram, bass.IndirectOffsetOnAxis(ap=s_ix[:, k, j:j + 1], axis=0),
                                                 y_w[:, k, j], None, compute_op=ALU.add).then_inc(y_st, 16)

            for u in range(4):
                gather(u, u % 2)
                if u >= 3:
                    scatter(u - 3, (u - 3) % 2)
            with pool.Fori(2, UNITS // 2) as i:
                for k in range(2):
                    gather(2 * i + k, k)
                    scatter(2 * i + k - 3, 1 - k)
            for u in range(UNITS - 3, UNITS):
                scatter(u, u % 2)
            pool.wait_ge(y_st, 16 * E * SLOT_TILES)

        @block.scalar
        def _(act):
            act.wait_ge(wT_done, 1)
            nc.scalar.copy(gate_wT[:], ps[:, 0, 0:3 * DC * 2 * HEADS].rearrange("p (c g) -> p c g", g=2 * HEADS)).then_inc(wT_copied, 1)
            nc.scalar.copy(b1_cols[:], ps[:, 1, 0:E * HC]).then_inc(wT_copied, 1)
            act.wait_ge(misc_ld, 16 * MISC)
            nc.scalar.activation(tanh_g[:], gx[:], ACT.Tanh).then_inc(tg_done, 1)

            def copy_kT(g):
                for c in range(DC):
                    act.wait_ge(kT_ps, DC * g + c + 1)
                    nc.scalar.copy(kT[:, c, bass.ds(g * GW, GW)], ps[:, c, :]).then_inc(kT_done, 1)

            def copy_gates(g, k):
                act.wait_ge(gate_ps, g + 1)
                if not isinstance(g, int) or g >= 2:
                    act.wait_ge(gate_st[k], 8 * (g - k))
                nc.scalar.activation(gates_sb[:, k], ps[0:2 * HEADS, 4, :], ACT.Identity, bias=gate_b[:, 0:1]).then_inc(gate_done, 1)

            for g in range(4):
                copy_kT(g)
                if g >= 2:
                    copy_gates(g - 2, g % 2)
            with act.Fori(2, GROUPS // 2) as i:
                for k in range(2):
                    copy_kT(2 * i + k)
                    copy_gates(2 * i + k - 2, k)
            for g in (GROUPS - 2, GROUPS - 1):
                copy_gates(g, g % 2)

            act.wait_ge(sc_v, 1)
            nc.scalar.activation(fe[:], fa[:], ACT.Exp).then_inc(sc_a, 1)
            act.wait_ge(sc_a, 1)
            nc.scalar.activation(fl[:], fe[:], ACT.Ln, bias=1.0).then_inc(sc_a, 1)
            act.wait_ge(sc_v, 9)
            nc.scalar.activation(nm[:], msum[:], ACT.Exp, scale=-1.0).then_inc(sc_a, 1)

            def decays(b, k):
                act.wait_ge(z_ps, b + 1)
                if not isinstance(b, int):
                    act.wait_ge(cT_done, b - 1)
                elif b >= 2:
                    act.wait_ge(cT_done, b - 1)
                else:
                    act.wait_ge(dump_st, 16)
                nc.scalar.activation(decay[:, k], ps[:, 0:2, :].rearrange("p a b -> p (a b)"), ACT.Exp).then_inc(exp_done, 1)

            def copy_xnT(b):
                act.wait_ge(xnT_ps, b + 1)
                if not isinstance(b, int) or b >= 1:
                    act.wait_ge(lg_ps, b)
                nc.scalar.copy(xnT[:], ps[:, 6, 0:DC * S].rearrange("p (c s) -> p c s", s=S)).then_inc(xnT_done, 1)

            def copy_logits(b):
                act.wait_ge(lg_ps, b + 1)
                nc.scalar.copy(logits[:, bass.ds(b, 1)].rearrange("p a e -> p (a e)"), ps[:, 7, 0:E]).then_inc(lg_done, 1)

            for b in range(4):
                decays(b, b % 2)
                if b >= 3:
                    copy_xnT(b - 3)
                    copy_logits(b - 3)
            with act.Fori(2, B // 2) as i:
                for k in range(2):
                    decays(2 * i + k, k)
                    copy_xnT(2 * i + k - 3)
                    copy_logits(2 * i + k - 3)
            for b in range(B - 3, B):
                copy_xnT(b)
                copy_logits(b)

            act.wait_ge(rt_v, 2)
            nc.scalar.activation(rexp[:], rz[:], ACT.Exp).then_inc(rt_a, 1)

            def split_w(e, k):
                act.wait_ge(w_ld, 32 * e + 48)
                if not isinstance(e, int) or e >= 2:
                    act.wait_ge(g1_ps, 2 * HC * (e - 1))
                nc.scalar.copy(w1h[:, k], w_raw1[:]).then_inc(w1h_done, 1)
                if not isinstance(e, int) or e >= 2:
                    act.wait_ge(y_ps, 2 * 2 * (e - 1))
                nc.scalar.copy(w2h[:, k], w_raw2[:]).then_inc(w2h_done, 1)

            def round_x(u, k):
                for c in range(DC):
                    act.wait_ge(xT_ps, DC * u + c + 1)
                    if not isinstance(u, int) or u >= 2:
                        act.wait_ge(g1_ps, HC * (u - 1))
                    nc.scalar.copy(xh[:, k, c], ps[:, c, :]).then_inc(xh_done, 1)

            def gelu(u, par):
                for m in range(HC):
                    act.wait_ge(g1_ps, HC * u + m + 1)
                    slot = (HC * par + m) % 3
                    if not isinstance(u, int) or HC * u + m >= 3:
                        act.wait_ge(hl_done, HC * u + m - 2)
                    b1_c = HC * (u // 2) + m if isinstance(u, int) else None
                    bias = b1_cols[:, b1_c:b1_c + 1] if b1_c is not None else b1_cols[:, bass.ds(b1_at[0] + m, 1)]
                    nc.scalar.activation(hf[:, slot], ps[:, 2 + (HC * par + m) % 3, :], ACT.Gelu, bias=bias).then_inc(gelu_done, 1)

            def weigh_y(u, k):
                for j in range(UT):
                    if j % 2 == 0:
                        act.wait_ge(yb_done, 2 * u + j // 2 + 1)
                    if not isinstance(u, int) or u >= 2:
                        act.wait_ge(y_st, 16 * UT * (u - 1))
                    scale = slot_w[:, bass.ds(u * UT + j, 1)]
                    nc.scalar.mul(y_w[:, k, j], y_b[:, k, j], scale).then_inc(yw_done, 1)

            b1_at = [0]
            act.wait_ge(slot_ps, 1)
            act.wait_ge(slots_done, 3)
            for s in range(UNITS + 2):
                if s < UNITS and s % 2 == 0:
                    split_w(s // 2, (s // 2) % 2)
                if s < UNITS:
                    round_x(s, s % 2)
                if 1 <= s <= UNITS:
                    gelu(s - 1, (s - 1) % 3)
                if s >= 2:
                    weigh_y(s - 2, s % 2)

        @block.tensor
        def _(pe):
            pe.wait_ge(misc_ld, 16 * MISC)
            pe.wait_ge(const_ready, CONSTS)
            for c in range(3 * DC):
                nc.tensor.transpose(ps[:, 0, c * 2 * HEADS:(c + 1) * 2 * HEADS], gate_rows[:, c * P:(c + 1) * P],
                                    ident[0:2 * HEADS, 0:2 * HEADS])
            nc.tensor.transpose(ps[:, 1, 0:E * HC], b1_rows[:], ident[0:E * HC, 0:E * HC]).then_inc(wT_done, 1)
            pe.wait_ge(wT_copied, 2)
            pe.wait_ge(wk_ready, 1)

            def turn_ctx(g, k):
                pe.wait_ge(c_ld[k], 16 * ((g - k) // 2) + 16 if isinstance(g, int) else 8 * (g - k) + 16)
                for c in range(DC):
                    if not isinstance(g, int) or g >= 1:
                        pe.wait_ge(kT_done, DC * (g - 1) + c + 1)
                    for b in range(GB):
                        last = nc.tensor.transpose(ps[:, c, b * S:(b + 1) * S], c_in[:, k, b, c * P:(c + 1) * P], ident[:])
                    last.then_inc(kT_ps, 1)

            def turn_q(g, k):
                pe.wait_ge(q_done, GB * (g + 1))
                if not isinstance(g, int) or g >= 1:
                    pe.wait_ge(qT_done, g)
                for c in range(DC):
                    for b in range(GB):
                        last = nc.tensor.transpose(ps[:, 2 + c, b * S:(b + 1) * S], q_rows[:, k, b, c * P:(c + 1) * P], ident[:])
                last.then_inc(qT_ps, 1)

            def gates(g):
                pe.wait_ge(qT_done, g + 1)
                pe.wait_ge(kT_done, DC * (g + 1))
                if not isinstance(g, int) or g >= 1:
                    pe.wait_ge(gate_done, g)
                for c in range(DC):
                    nc.tensor.matmul(ps[0:2 * HEADS, 4, :], gate_wT[:, c], qT[:, c, bass.ds(g * GW, GW)], start=(c == 0), stop=False)
                for c in range(DC):
                    last = nc.tensor.matmul(ps[0:2 * HEADS, 4, :], gate_wk[:, c], kT[:, c, bass.ds(g * GW, GW)], start=False, stop=(c == DC - 1))
                last.then_inc(gate_ps, 1)

            for g in range(4):
                turn_ctx(g, g % 2)
                if g >= 1:
                    turn_q(g - 1, (g - 1) % 2)
                if g >= 2:
                    gates(g - 2)
            with pe.Fori(2, GROUPS // 2) as i:
                for k in range(2):
                    turn_ctx(2 * i + k, k)
                    turn_q(2 * i + k - 1, 1 - k)
                    gates(2 * i + k - 2)
            turn_q(GROUPS - 1, (GROUPS - 1) % 2)
            gates(GROUPS - 2)
            gates(GROUPS - 1)

            pe.wait_ge(sc_a, 3)
            for t in range(PAIR_TILES):
                last = nc.tensor.transpose(ps[:, 5, t * P:(t + 1) * P], nm[:, t * S:(t + 1) * S], ident[:])
            last.then_inc(nmT_ps, 1)

            def exponents(b, k):
                pe.wait_ge(pe_ld[k], 112 * ((b - k) // 2) + 112 if isinstance(b, int) else 56 * (b - k) + 112)
                if not isinstance(b, int) or b >= 1:
                    pe.wait_ge(exp_done, b)
                for n in range(2):
                    nc.tensor.matmul(ps[:, n, :], z_lhs[:, k], z_rhs[:, k, n * 512:(n + 1) * 512], start=True, stop=False)
                    last = nc.tensor.matmul(ps[:, n, :], ident_bf[:], mask_bf[:].rearrange("p j s -> p (j s)"), start=False, stop=True)
                last.then_inc(z_ps, 1)

            def scores(b, k):
                if not isinstance(b, int) or b >= 1:
                    pe.wait_ge(cT_done, b)
                for c in range(DC):
                    last = nc.tensor.matmul(ps[:, 2 + c, :], k_st[:, k, c], q_bd[:, k, c], start=True, stop=True)
                last.then_inc(s_ps, 1)

            def head_sums(b, k):
                pe.wait_ge(cT_done, b + 1)
                pe.wait_ge(v_ready, b + 1)
                if not isinstance(b, int) or b >= 1:
                    pe.wait_ge(hn_done, b)
                for h in range(HEADS):
                    last = nc.tensor.matmul(ps[:, 4 + h // 4, (h % 4) * P:(h % 4) * P + VWIN], cT[:, k, h * S:(h + 1) * S],
                                            v_ext[:, k, h * VW:h * VW + VWIN], start=True, stop=True)
                last.then_inc(h_ps, 1)

            def turn_xn(b, k):
                pe.wait_ge(xn_done, b + 1)
                if not isinstance(b, int) or b >= 1:
                    pe.wait_ge(xnT_done, b)
                for c in range(DC):
                    last = nc.tensor.transpose(ps[:, 6, c * S:(c + 1) * S], xn[:, k, c * P:(c + 1) * P], ident[:])
                last.then_inc(xnT_ps, 1)

            def router(b):
                pe.wait_ge(xnT_done, b + 1)
                if not isinstance(b, int) or b >= 1:
                    pe.wait_ge(lg_done, b)
                for c in range(DC):
                    last = nc.tensor.matmul(ps[:, 7, 0:LPAD], xnT[:, c], wg_pad[:, c].rearrange("p r e -> p (r e)"),
                                            start=(c == 0), stop=(c == DC - 1))
                last.then_inc(lg_ps, 1)

            pe.wait_ge(const_v, 1)
            pe.wait_ge(nmT_done, 1)
            for b in range(4):
                exponents(b, b % 2)
                if b >= 3:
                    turn_xn(b - 3, (b - 3) % 2)
                scores(b, b % 2)
                if b >= 3:
                    router(b - 3)
                if b >= 1:
                    head_sums(b - 1, (b - 1) % 2)
            with pe.Fori(2, B // 2) as i:
                for k in range(2):
                    exponents(2 * i + k, k)
                    turn_xn(2 * i + k - 3, 1 - k)
                    scores(2 * i + k, k)
                    router(2 * i + k - 3)
                    head_sums(2 * i + k - 1, 1 - k)
            turn_xn(B - 3, (B - 3) % 2)
            head_sums(B - 1, (B - 1) % 2)
            router(B - 3)
            for b in (B - 2, B - 1):
                turn_xn(b, b % 2)
                router(b)

            pe.wait_ge(rt_v, 21)
            oh = onehot[:].rearrange("p e k b -> p (e k b)")
            nc.tensor.matmul(ps[:, 0, :], ones_bf[:], oh, start=True, stop=True).then_inc(count_ps, 1)
            nc.tensor.matmul(ps[:, 1, :], tri_bf[:], oh, start=True, stop=True).then_inc(count_ps, 1)
            for q in range(4):
                pe.wait_ge(cv_id, q + 1)
                pe.wait_ge(cv_w, q + 1)
                pe.wait_ge(rh_done, q + 1)
                for kt in range(q * KT // 4, (q + 1) * KT // 4):
                    last = nc.tensor.matmul(ps[:, 2, 0:2 * E * SLOT_TILES], rowhot[:, kt], colval[:, kt],
                                            start=(kt == 0), stop=(kt == KT - 1))
            last.then_inc(slot_ps, 1)

            def turn_x(u, k):
                pe.wait_ge(xg_ld[k], 16 * UT * (u // 2 + 1) if isinstance(u, int) else 8 * UT * (u - k) + 16 * UT)
                for c in range(DC):
                    if not isinstance(u, int) or u >= 1:
                        pe.wait_ge(xl_done, DC * (u - 1) + c + 1)
                    for j in range(UT):
                        last = nc.tensor.transpose(ps[:, c, j * P:(j + 1) * P], xg[:, k, j, c * P:(c + 1) * P], ident[:])
                    last.then_inc(xT_ps, 1)

            def hidden(u, k, wk, par):
                if k == 0:
                    pe.wait_ge(w1l_done, u // 2 + 1)
                pe.wait_ge(xl_done, DC * (u + 1))
                for m in range(HC):
                    bank = 2 + (HC * par + m) % 3
                    if not isinstance(u, int) or HC * u + m >= 3:
                        pe.wait_ge(gelu_done, HC * u + m - 2)
                    ms = slice(m * P, (m + 1) * P)
                    for c in range(DC):
                        nc.tensor.matmul(ps[:, bank, :], w1h[:, wk, c, ms], xh[:, k, c], start=(c == 0), stop=False)
                        nc.tensor.matmul(ps[:, bank, :], w1h[:, wk, c, ms], xl[:, k, c], start=False, stop=False)
                        last = nc.tensor.matmul(ps[:, bank, :], w1l[:, wk, c, ms], xh[:, k, c], start=False, stop=(c == DC - 1))
                    last.then_inc(g1_ps, 1)

            def outputs(u, k, wk):
                if k == 0:
                    pe.wait_ge(w2l_done, u // 2 + 1)
                pe.wait_ge(hl_done, HC * (u + 1))
                for j in range(UT):
                    if j % 2 == 0 and (not isinstance(u, int) or u >= 1):
                        pe.wait_ge(yb_done, 2 * (u - 1) + j // 2 + 1)
                    js = slice(j * P, (j + 1) * P)
                    o = ps[:, 5 + j // 2, (j % 2) * D:(j % 2 + 1) * D]
                    for m in range(HC):
                        nc.tensor.matmul(o, hh[:, k, m, js], w2h[:, wk, m], start=(m == 0), stop=False)
                        nc.tensor.matmul(o, hh[:, k, m, js], w2l[:, wk, m], start=False, stop=False)
                        last = nc.tensor.matmul(o, hl[:, k, m, js], w2h[:, wk, m], start=False, stop=(m == HC - 1))
                    if j % 2 == 1:
                        last.then_inc(y_ps, 1)

            pe.wait_ge(slots_done, 3)
            for s in range(UNITS + 2):
                if s < UNITS:
                    turn_x(s, s % 2)
                if 1 <= s <= UNITS:
                    hidden(s - 1, (s - 1) % 2, ((s - 1) // 2) % 2, (s - 1) % 3)
                if s >= 2:
                    outputs(s - 2, s % 2, ((s - 2) // 2) % 2)

        @block.vector
        def _(dve):
            nc.vector.memset(q_bd[:], 0.0)
            nc.vector.memset(decay[:], 0.0)
            nc.vector.memset(ones_bf[:], 1.0)
            nc.vector.memset(ones_row[:], 1.0)
            nc.vector.memset(zero_row[:], 0.0)
            dve.wait_ge(misc_ld, 16 * MISC)
            nc.vector.tensor_copy(wg_pad[:], wg_sb[:].unsqueeze(2).broadcast_to([P, DC, LPAD // E, E])).then_inc(const_v, 1)
            dve.wait_ge(wT_copied, 2)
            nc.vector.tensor_tensor(gate_wk[:], gate_wT[:, DC:2 * DC], gate_wT[:, 2 * DC:3 * DC], ALU.add).then_inc(wk_ready, 1)
            dve.wait_ge(tg_done, 1)
            nc.vector.tensor_scalar(ls_t[:], ls[:], tanh_g[:, 0:1], None, ALU.mult).then_inc(const_v, 1)

            def stats(g, k):
                dve.wait_ge(x_ld[k], 16 * ((g - k) // 2) + 16 if isinstance(g, int) else 8 * (g - k) + 16)
                if not isinstance(g, int) or g >= 1:
                    dve.wait_ge(stats_done, g)
                if not isinstance(g, int) or g >= 2:
                    dve.wait_ge(q_done, GB * (g - 1))
                    dve.wait_ge(rstd_done, g - 1)
                for b in range(GB):
                    last = nc.vector.bn_stats(g_stats[:, b], x_in[:, k, b])
                last.then_inc(g_seq, 1)
                dve.wait_ge(g_seq, g + 1)
                dve.sem_inc(waited, 1)
                for b in range(GB):
                    last = nc.vector.bn_aggr(g_mv[:, k, b], g_stats[:, b])
                last.then_inc(stats_done, 1)

            def normalise(g, k):
                dve.wait_ge(rstd_done, g + 1)
                dve.wait_ge(stats_done, g + 1)
                if not isinstance(g, int) or g >= 2:
                    dve.wait_ge(qT_ps, g - 1)
                for b in range(GB):
                    nc.vector.tensor_scalar(q_rows[:, k, b], x_in[:, k, b], g_mv[:, k, b, 0:1], g_rstd[:, k, b:b + 1],
                                            ALU.subtract, ALU.mult).then_inc(q_done, 1)

            def copy_qT(g):
                dve.wait_ge(qT_ps, g + 1)
                nc.vector.tensor_copy(qT[:, :, bass.ds(g * GW, GW)], ps[:, 2:4, :]).then_inc(qT_done, 1)

            for g in range(4):
                stats(g, g % 2)
                if g >= 1:
                    normalise(g - 1, (g - 1) % 2)
                if g >= 2:
                    copy_qT(g - 2)
            with dve.Fori(2, GROUPS // 2) as i:
                for k in range(2):
                    stats(2 * i + k, k)
                    normalise(2 * i + k - 1, 1 - k)
                    copy_qT(2 * i + k - 2)
            normalise(GROUPS - 1, (GROUPS - 1) % 2)
            copy_qT(GROUPS - 2)
            copy_qT(GROUPS - 1)

            fg = fg_p[:].rearrange("p t s -> p (t s)")
            ig = ig_p[:].rearrange("p t s -> p (t s)")
            dve.wait_ge(pair_ld, 16 * 2 * PAIR_TILES)
            nc.vector.scalar_tensor_tensor(out=fa[:], in0=fg, scalar=-1.0, in1=fg, op0=ALU.mult, op1=ALU.min).then_inc(sc_v, 1)
            dve.wait_ge(sc_a, 2)
            nc.vector.scalar_tensor_tensor(out=logf[:], in0=fg, scalar=0.0, in1=fl[:], op0=ALU.min, op1=ALU.subtract).then_inc(sc_v, 1)
            dve.wait_ge(sc_v, 2)
            for t in range(PAIR_TILES):
                ts = slice(t * S, (t + 1) * S)
                nc.vector.tensor_tensor_scan(cs[:, ts], ones_row[:], logf[:, ts], 0.0, ALU.mult, ALU.add).then_inc(sc_v, 1)
            dve.wait_ge(sc_v, 4)
            nc.vector.tensor_tensor(av[:], ig, cs[:], ALU.subtract).then_inc(sc_v, 1)
            dve.wait_ge(sc_v, 5)
            for t in range(PAIR_TILES):
                ts = slice(t * S, (t + 1) * S)
                nc.vector.tensor_tensor_scan(mv[:, ts], zero_row[:], av[:, ts], LOWEST, ALU.add, ALU.max).then_inc(sc_v, 1)
            dve.wait_ge(sc_v, 7)
            nc.vector.tensor_scalar(negm[:], mv[:], -1.0, None, ALU.mult).then_inc(sc_v, 1)
            nc.vector.tensor_tensor(msum[:], cs[:], mv[:], ALU.add).then_inc(sc_v, 1)
            for n, src in ((0, av), (1, negm)):
                at = 9 + 4 * n
                dve.wait_ge(sc_v, at)
                nc.vector.tensor_copy(parts[:, n, 0], src[:]).then_inc(sc_v, 1)
                dve.wait_ge(sc_v, at + 1)
                nc.vector.tensor_tensor(res1[:, 0], src[:], parts[:, n, 0], ALU.subtract).then_inc(sc_v, 1)
                dve.wait_ge(sc_v, at + 2)
                nc.vector.tensor_copy(parts[:, n, 1], res1[:, 0]).then_inc(sc_v, 1)
                dve.wait_ge(sc_v, at + 3)
                nc.vector.tensor_tensor(parts[:, n, 2], res1[:, 0], parts[:, n, 1], ALU.subtract).then_inc(sc_v, 1)

            dve.wait_ge(nmT_ps, 1)
            nc.vector.tensor_scalar(nmT[:], ps[:, 5, 0:B * HEADS], NORM_EPS, None, ALU.add).then_inc(nmT_done, 1)

            def weigh(b, k):
                dve.wait_ge(exp_done, b + 1)
                dve.wait_ge(s_ps, b + 1)
                if not isinstance(b, int) or b >= 2:
                    dve.wait_ge(h_ps, b - 1)
                nc.vector.scalar_tensor_tensor(out=cT[:, k], in0=ps[:, 2:4, :].rearrange("p a b -> p (a b)"),
                                               scalar=float(DH) ** -0.5, in1=decay[:, k], op0=ALU.mult,
                                               op1=ALU.mult).then_inc(cT_done, 1)

            def heads(b, k):
                hp = ps[:, 4:6, :].rearrange("p a (h w) -> p (a h) w", w=P)
                dve.wait_ge(h_ps, b + 1)
                if not isinstance(b, int) or b >= 1:
                    dve.wait_ge(hsc_done, b)
                if not isinstance(b, int) or b >= 2:
                    dve.wait_ge(h_rs, b - 1)
                    dve.wait_ge(x1_done, b - 1)
                nc.vector.scalar_tensor_tensor(out=den[:].unsqueeze(2), in0=hp[:, :, DH:DH + 1], scalar=NORM_EPS,
                                               in1=nmT[:, bass.ds(b * HEADS, HEADS)].unsqueeze(2),
                                               op0=ALU.subtract, op1=ALU.max, reverse0=True).then_inc(p1_seq, 1)
                dve.wait_ge(p1_seq, 4 * b + 1)
                nc.vector.scalar_tensor_tensor(out=den2[:].unsqueeze(2), in0=hp[:, :, DH:DH + 1], scalar=NORM_EPS,
                                               in1=den[:].unsqueeze(2), op0=ALU.add, op1=ALU.max).then_inc(p1_seq, 1)
                dve.wait_ge(p1_seq, 4 * b + 2)
                nc.vector.reciprocal(rden[:], den2[:]).then_inc(p1_seq, 1)
                dve.wait_ge(p1_seq, 4 * b + 3)
                nc.vector.tensor_tensor(hn[:], hp[:, :, 0:DH], rden[:].unsqueeze(2).broadcast_to([P, HEADS, DH]),
                                        ALU.mult).then_inc(hn_done, 1)
                dve.wait_ge(hn_done, b + 1)
                hrow = hn[:].rearrange("p h e -> p (h e)")
                nc.vector.bn_stats(h_st[:], hrow).then_inc(p1_seq, 1)
                dve.wait_ge(p1_seq, 4 * b + 4)
                dve.sem_inc(waited, 1)
                nc.vector.bn_aggr(h_mv[:, k], h_st[:]).then_inc(h_stat, 1)
                dve.wait_ge(h_stat, b + 1)
                nc.vector.scalar_tensor_tensor(out=h_sc[:, k], in0=hrow, scalar=h_mv[:, k, 0:1], in1=ls_t[:],
                                               op0=ALU.subtract, op1=ALU.mult).then_inc(hsc_done, 1)

            def residual(b, k):
                dve.wait_ge(h_rs, b + 1)
                dve.wait_ge(hsc_done, b + 1)
                if not isinstance(b, int) or b >= 1:
                    dve.wait_ge(x_stat, b)
                if not isinstance(b, int) or b >= 2:
                    dve.wait_ge(x_rs, b - 1)
                    dve.wait_ge(xn_done, b - 1)
                dve.wait_ge(xc_ld[k], 32 * ((b - k) // 2) + 32 if isinstance(b, int) else 16 * (b - k) + 32)
                if not isinstance(b, int) or b >= 2:
                    dve.wait_ge(x1_st[k], 16 * ((b - k) // 2) if isinstance(b, int) else 8 * (b - k))
                nc.vector.scalar_tensor_tensor(out=x1[:, k], in0=h_sc[:, k], scalar=h_rstd[:, k], in1=x_c[:, k],
                                               op0=ALU.mult, op1=ALU.add).then_inc(x1_done, 1)
                dve.wait_ge(x1_done, b + 1)
                nc.vector.bn_stats(x_st[:], x1[:, k]).then_inc(x1_seq, 1)
                dve.wait_ge(x1_seq, b + 1)
                dve.sem_inc(waited, 1)
                nc.vector.bn_aggr(x_mv[:, k], x_st[:]).then_inc(x_stat, 1)

            def norm_rows(b, k):
                dve.wait_ge(x_rs, b + 1)
                dve.wait_ge(x_stat, b + 1)
                if not isinstance(b, int) or b >= 2:
                    dve.wait_ge(xnT_ps, b - 1)
                    dve.wait_ge(xn_st[k], 16 * ((b - k) // 2) if isinstance(b, int) else 8 * (b - k))
                nc.vector.tensor_scalar(xn[:, k], x1[:, k], x_mv[:, k, 0:1], x_rstd[:, k], ALU.subtract, ALU.mult).then_inc(xn_done, 1)

            dve.wait_ge(nmT_done, 1)
            dve.wait_ge(const_v, 2)
            for b in range(4):
                weigh(b, b % 2)
                if b >= 1:
                    heads(b - 1, (b - 1) % 2)
                if b >= 2:
                    norm_rows(b - 2, b % 2)
                if b >= 1:
                    residual(b - 1, (b - 1) % 2)
            with dve.Fori(2, B // 2) as i:
                for k in range(2):
                    weigh(2 * i + k, k)
                    heads(2 * i + k - 1, 1 - k)
                    norm_rows(2 * i + k - 2, k)
                    residual(2 * i + k - 1, 1 - k)
            heads(B - 1, 1)
            norm_rows(B - 2, 0)
            residual(B - 1, 1)
            norm_rows(B - 1, 1)

            def over(t, n=E):
                return t.unsqueeze(2).broadcast_to([P, B, n])

            dve.wait_ge(rt_p, 12 + 4)
            dve.wait_ge(lg_done, B)
            for k in range(2):
                dve.wait_ge(xn_st[k], 16 * (B // 2))
            nc.vector.tensor_reduce(rmax[:], logits[:], AX_X, ALU.max).then_inc(rt_v, 1)
            dve.wait_ge(rt_v, 1)
            nc.vector.tensor_tensor(rz[:], logits[:], over(rmax[:]), ALU.subtract).then_inc(rt_v, 1)
            dve.wait_ge(rt_a, 1)
            nc.vector.tensor_reduce(rsum[:], rexp[:], AX_X, ALU.add).then_inc(rt_v, 1)
            dve.wait_ge(rt_v, 3)
            nc.vector.reciprocal(rrec[:], rsum[:]).then_inc(rt_v, 1)
            dve.wait_ge(rt_v, 4)
            nc.vector.tensor_tensor(score[:], rexp[:], over(rrec[:]), ALU.mult).then_inc(rt_v, 1)
            for k, sc in ((0, score), (1, score2)):
                at = 5 + 7 * k
                dve.wait_ge(rt_v, at)
                nc.vector.tensor_reduce(best[:, k], sc[:], AX_X, ALU.max).then_inc(rt_v, 1)
                dve.wait_ge(rt_v, at + 1)
                nc.vector.tensor_tensor(req[:], sc[:], over(best[:, k]), ALU.is_equal).then_inc(rt_v, 1)
                dve.wait_ge(rt_v, at + 2)
                nc.vector.tensor_tensor(rkey[:], req[:], rank[:], ALU.mult).then_inc(rt_v, 1)
                dve.wait_ge(rt_v, at + 3)
                nc.vector.tensor_reduce(kmax[:, k], rkey[:], AX_X, ALU.max).then_inc(rt_v, 1)
                dve.wait_ge(rt_v, at + 4)
                nc.vector.tensor_tensor(chosen[:], rank[:], over(kmax[:, k]), ALU.is_equal).then_inc(rt_v, 1)
                dve.wait_ge(rt_v, at + 5)
                nc.vector.tensor_copy(onehot[:, :, k].rearrange("p e b -> p b e"), chosen[:]).then_inc(rt_v, 1)
                if k == 0:
                    nc.vector.scalar_tensor_tensor(out=score2[:], in0=chosen[:], scalar=-2.0, in1=score[:],
                                                   op0=ALU.mult, op1=ALU.add).then_inc(rt_v, 1)
            nc.vector.tensor_tensor(gsum[:], best[:, 0], best[:, 1], ALU.add).then_inc(rt_v, 1)
            dve.wait_ge(rt_v, 19)
            nc.vector.tensor_scalar(gclip[:], gsum[:], GATE_EPS, None, ALU.max).then_inc(rt_v, 1)
            dve.wait_ge(rt_v, 20)
            nc.vector.reciprocal(grec[:], gclip[:]).then_inc(rt_v, 1)
            dve.wait_ge(rt_v, 21)
            nc.vector.tensor_tensor(gval[:], best[:], grec[:].unsqueeze(1).broadcast_to([P, TOP, B]), ALU.mult).then_inc(rt_v, 1)
            dve.wait_ge(rt_v, 22)
            nc.vector.tensor_scalar(gw_t[:], gval[:].rearrange("p k b -> p (k b)"), tanh_g[:, 1:2], None, ALU.mult).then_inc(rt_v, 1)
            dve.wait_ge(count_ps, 1)
            nc.vector.tensor_tensor_scan(before[:], reset[:].rearrange("p e k -> p (e k)"), ps[:, 0, :], 0.0,
                                         ALU.mult, ALU.add).then_inc(rt_v, 1)
            dve.wait_ge(rt_v, 24)
            nc.vector.scalar_tensor_tensor(out=loc0[:], in0=before[:], scalar=-1.0, in1=ps[:, 0, :],
                                           op0=ALU.add, op1=ALU.subtract).then_inc(rt_v, 1)
            dve.wait_ge(rt_v, 25)
            dve.wait_ge(count_ps, 2)
            nc.vector.tensor_tensor(loc[:].rearrange("p e k -> p (e k)"), loc0[:], ps[:, 1, :], ALU.add).then_inc(rt_v, 1)
            dve.wait_ge(rt_v, 26)
            nc.vector.tensor_tensor(locsel[:], loc[:], onehot[:].rearrange("p e k b -> p e (k b)"), ALU.mult).then_inc(rt_v, 1)
            dve.wait_ge(rt_v, 27)
            nc.vector.tensor_reduce(pos[:], locsel[:].rearrange("p e k -> p k e"), AX_X, ALU.add).then_inc(rt_v, 1)
            dve.wait_ge(rt_v, 28)
            nc.vector.tensor_copy(pos_i[:], pos[:]).then_inc(rt_v, 1)
            dve.wait_ge(rt_v, 29)
            shift = SLOT_TILES.bit_length() - 1
            nc.vector.tensor_scalar(row_i[:], pos_i[:], shift, None, ALU.arith_shift_right)
            nc.vector.tensor_scalar(col_i[:], pos_i[:], SLOT_TILES - 1, None, ALU.bitwise_and).then_inc(rt_v, 1)
            dve.wait_ge(rt_v, 30)
            nc.vector.tensor_copy(row_f[:], row_i[:])
            nc.vector.tensor_copy(col_f[:], col_i[:])
            nc.vector.tensor_scalar(col_b[:], kmax[:].rearrange("p k b -> p (k b)"), -float(SLOT_TILES), float(E * SLOT_TILES),
                                    ALU.mult, ALU.add).then_inc(rt_v, 1)
            dve.wait_ge(rt_v, 31)
            nc.vector.tensor_tensor(col_s[:], col_f[:], col_b[:], ALU.add).then_inc(rt_v, 1)
            dve.wait_ge(rt_v, 32)
            Q = KT // 4
            W = E * SLOT_TILES
            tok = token1[:].rearrange("p k b -> p (k b)")
            for q in range(4):
                ks = slice(q * Q, (q + 1) * Q)
                nc.vector.tensor_tensor(colhot[:, ks], iota_f[:, 0:W].unsqueeze(1).broadcast_to([P, Q, W]),
                                        col_s[:, ks].unsqueeze(2).broadcast_to([P, Q, W]), ALU.is_equal).then_inc(rt_v, 1)
                nc.vector.tensor_tensor(rowhot[:, ks], iota_f[:].unsqueeze(1).broadcast_to([P, Q, P]),
                                        row_f[:, ks].unsqueeze(2).broadcast_to([P, Q, P]), ALU.is_equal).then_inc(rh_done, 1)
                dve.wait_ge(rt_v, 33 + q)
                nc.vector.tensor_tensor(colval[:, ks, 0:W], colhot[:, ks],
                                        tok[:, ks].unsqueeze(2).broadcast_to([P, Q, W]), ALU.mult).then_inc(cv_id, 1)
            dve.wait_ge(slot_ps, 1)
            nc.vector.tensor_copy(slot_w[:], ps[:, 2, W:2 * W]).then_inc(slots_done, 1)
            nc.vector.tensor_copy(slot_t[:], ps[:, 2, 0:W]).then_inc(rt_v, 1)
            dve.wait_ge(rt_v, 37)
            nc.vector.tensor_scalar(gather_idx[:], slot_t[:], -1.0, 0.0, ALU.add, ALU.max).then_inc(slots_done, 1)
            nc.vector.tensor_scalar(empty[:], slot_t[:], 0.0, None, ALU.is_equal).then_inc(rt_v, 1)
            dve.wait_ge(rt_v, 38)
            nc.vector.tensor_tensor(dumped[:], empty[:], dump[:], ALU.mult).then_inc(rt_v, 1)
            dve.wait_ge(rt_v, 39)
            nc.vector.scalar_tensor_tensor(out=scatter_idx[:], in0=slot_t[:], scalar=-1.0, in1=dumped[:],
                                           op0=ALU.add, op1=ALU.add).then_inc(slots_done, 1)

            def split_w(e, k):
                dve.wait_ge(w1h_done, e + 1)
                nc.vector.tensor_tensor(w1l[:, k], w_raw1[:], w1h[:, k].bitcast(F32), ALU.subtract).then_inc(w1l_done, 1)
                dve.wait_ge(w2h_done, e + 1)
                nc.vector.tensor_tensor(w2l[:, k], w_raw2[:], w2h[:, k].bitcast(F32), ALU.subtract).then_inc(w2l_done, 1)

            def rest_x(u, k):
                for c in range(DC):
                    dve.wait_ge(xh_done, DC * u + c + 1)
                    nc.vector.tensor_tensor(xl[:, k, c], ps[:, c, :], xh[:, k, c].bitcast(F32), ALU.subtract).then_inc(xl_done, 1)

            def split_h(u, k, par):
                if not isinstance(u, int) or u >= 2:
                    dve.wait_ge(y_ps, 2 * (u - 1))
                for m in range(HC):
                    slot = (HC * par + m) % 3
                    dve.wait_ge(gelu_done, HC * u + m + 1)
                    nc.vector.tensor_copy(hh[:, k, m], hf[:, slot]).then_inc(hh_done, 1)
                    dve.wait_ge(hh_done, HC * u + m + 1)
                    nc.vector.tensor_tensor(hl[:, k, m], hf[:, slot], hh[:, k, m].bitcast(F32), ALU.subtract).then_inc(hl_done, 1)

            def bias_y(u, k):
                b2_e = b2_all[:, bass.ds(u // 2, 1)] if isinstance(u, int) else None
                for j in range(UT // 2):
                    dve.wait_ge(y_ps, 2 * u + j + 1)
                    if not isinstance(u, int) or u >= 2:
                        dve.wait_ge(yw_done, UT * (u - 1))
                    nc.vector.tensor_tensor(y_b[:, k, 2 * j:2 * j + 2], ps[:, 5 + j, :].rearrange("p (a d) -> p a d", d=D),
                                            b2_e.broadcast_to([P, 2, D]), ALU.add).then_inc(yb_done, 1)

            for s in range(UNITS + 2):
                if s < UNITS and s % 2 == 0:
                    split_w(s // 2, (s // 2) % 2)
                if s < UNITS:
                    rest_x(s, s % 2)
                if 1 <= s <= UNITS:
                    split_h(s - 1, (s - 1) % 2, (s - 1) % 3)
                if s >= 2:
                    bias_y(s - 2, s % 2)


_INS = ['x', 'ctx_1024', 'g_xattn', 'g_ffn', 'L0_xattn_igate_w', 'L0_xattn_igate_b', 'L0_xattn_fgate_w',
        'L0_xattn_fgate_b', 'L0_xattn_ln_scale', 'L0_ffn_wg', 'L0_ffn_w1', 'L0_ffn_b1', 'L0_ffn_w2', 'L0_ffn_b2']
_OUTS = [((32, 128, 256), 'float32')]


def kernel(**inputs):
    import numpy as _np
    import concourse.bacc as _bacc
    from concourse import mybir as _mybir
    from concourse.bass_utils import run_bass_kernel_spmd as _run

    nc = _bacc.Bacc("TRN2", target_bir_lowering=False, num_devices=1)
    arrays, args = {}, []
    for name in _INS:
        a = _np.ascontiguousarray(inputs[name])
        arrays[f"in_{name}_dram"] = a
        args.append(nc.dram_tensor(f"in_{name}_dram", a.shape, _mybir.dt.from_np(a.dtype), kind="ExternalInput").ap())
    for i, (shape, dtype) in enumerate(_OUTS):
        dt = _mybir.dt.from_np(_np.dtype(dtype))
        args.append(nc.dram_tensor(f"out_{i}_dram", shape, dt, kind="ExternalOutput").ap())
    flamingo_block(nc, *args)
    r = _run(nc, [arrays], core_ids=[0])
    got = tuple(r.results[0][f"out_{i}_dram"] for i in range(len(_OUTS)))
    return got[0]
```

```python
from contextlib import ExitStack

import concourse.bass as bass
from concourse import mybir

F32 = mybir.dt.float32
F32R = mybir.dt.float32r
BF16 = mybir.dt.bfloat16
I32 = mybir.dt.int32
U32 = mybir.dt.uint32
ALU = mybir.AluOpType
ACT = mybir.ActivationFunctionType
AX_X = mybir.AxisListType.X

P = 128
LN_EPS = 1e-5
NORM_EPS = 1e-6
GATE_EPS = 1e-9
MASKED = -1.0e30
LOWEST = -3.0e38


def flamingo_block(nc, x, ctx_in, g_xattn, g_ffn, igate_w, igate_b, fgate_w, fgate_b, ln_scale,
                   wg, w1, b1, w2, b2, out):
    B, S, D = x.shape
    HEADS = igate_w.shape[0]
    DH = D // HEADS
    DC = D // P
    E, _, HID = w1.shape
    HC = HID // P
    TOP = 2
    N = B * S
    CAP = -(-TOP * N // E)
    assert S == P and HEADS * DH == D and CAP % P == 0 and B % 16 == 0

    GB = 4
    GROUPS = B // GB
    GW = GB * S
    PAIR_TILES = B * HEADS // P
    BT = B // PAIR_TILES
    PARTS = 3
    KA = PARTS * HEADS
    VW = DH + 1
    VWIN = 3 * VW
    LPAD = 96
    SLOT_TILES = CAP // P
    KT = TOP * B
    UNITS = 2 * E
    UT = SLOT_TILES // 2
    UW = UT * P

    gates_dram = nc.dram_tensor("gates_scratch", [2 * HEADS, N], F32, kind="Internal").ap()
    a_dram = nc.dram_tensor("a_scratch", [B, HEADS, PARTS, S], BF16, kind="Internal").ap()
    m_dram = nc.dram_tensor("m_scratch", [PARTS, B, HEADS, S], BF16, kind="Internal").ap()
    xn_dram = nc.dram_tensor("xn_scratch", [N, D], F32, kind="Internal").ap()
    acc_dram = nc.dram_tensor("acc_scratch", [N + CAP, D], F32, kind="Internal").ap()

    x_rows = x.rearrange("b s d -> (b s) d")
    ctx_rows = ctx_in.rearrange("b s d -> (b s) d")
    out_rows = out.rearrange("b s d -> (b s) d")

    with ExitStack() as keep:
        def sb(name, shape, dt=F32, stack=keep):
            return stack.enter_context(nc.sbuf_tensor(name, shape, dt))

        def sem(name):
            return keep.enter_context(nc.semaphore(name))

        ident = sb("ident", [P, P])
        ident_bf = sb("ident_bf", [P, P], BF16)
        ones_bf = sb("ones_bf", [P, P], BF16)
        tri_bf = sb("tri_bf", [P, P], BF16)
        w_raw1 = sb("w_raw1", [P, DC, HID])
        w_raw2 = sb("w_raw2", [P, HC, D])
        b1_rows = sb("b1_rows", [E * HC, P])
        b1_cols = sb("b1_cols", [P, E * HC])
        b2_all = sb("b2_all", [P, E, D])
        gx = sb("gx", [P, 2])
        tanh_g = sb("tanh_g", [P, 2])
        logits = sb("logits", [P, B, E])
        slot_w = sb("slot_w", [P, E * SLOT_TILES])
        gather_idx = sb("gather_idx", [P, E * SLOT_TILES], U32)
        scatter_idx = sb("scatter_idx", [P, E * SLOT_TILES], U32)

        att = ExitStack()
        qT = sb("qT", [P, DC, N], stack=att)
        kT = sb("kT", [P, DC, N], stack=att)
        cell = ExitStack()
        q_rows = sb("q_rows", [P, 2, GB, D], stack=cell)
        g_stats = sb("g_stats", [P, GB, 6], stack=cell)
        g_mv = sb("g_mv", [P, 2, GB, 2], stack=cell)
        g_var = sb("g_var", [P, GB], stack=cell)
        g_rstd = sb("g_rstd", [P, 2, GB], stack=cell)
        gate_rows = sb("gate_rows", [2 * HEADS, 3 * D], stack=cell)
        gate_wT = sb("gate_wT", [P, 3 * DC, 2 * HEADS], stack=cell)
        gate_wk = sb("gate_wk", [P, DC, 2 * HEADS], stack=cell)
        gate_b = sb("gate_b", [2 * HEADS, 1], stack=cell)
        gates_sb = sb("gates_sb", [2 * HEADS, 2, GW], stack=cell)
        neg_half = sb("neg_half", [P, GB], stack=cell)
        PW = PAIR_TILES * S
        ig_p = sb("ig_p", [P, PAIR_TILES, S], stack=cell)
        fg_p = sb("fg_p", [P, PAIR_TILES, S], stack=cell)
        fa = sb("fa", [P, PW], stack=cell)
        fe = sb("fe", [P, PW], stack=cell)
        fl = sb("fl", [P, PW], stack=cell)
        logf = sb("logf", [P, PW], stack=cell)
        cs = sb("cs", [P, PW], stack=cell)
        av = sb("av", [P, PW], stack=cell)
        mv = sb("mv", [P, PW], stack=cell)
        msum = sb("msum", [P, PW], stack=cell)
        nm = sb("nm", [P, PW], stack=cell)
        res1 = sb("res1", [P, 2, PW], stack=cell)
        negm = sb("negm", [P, PW], stack=cell)
        parts = sb("parts", [P, 2, PARTS, PW], BF16, stack=cell)
        ones_row = sb("ones_row", [P, S], stack=cell)
        zero_row = sb("zero_row", [P, S], stack=cell)
        nmT = sb("nmT", [P, B * HEADS], stack=cell)
        mask_bf = sb("mask_bf", [P, 4, S], BF16, stack=cell)
        z_lhs = sb("z_lhs", [P, 4, S], BF16, stack=cell)
        z_rhs = sb("z_rhs", [P, 4, HEADS * S], BF16, stack=cell)
        k_st = sb("k_st", [P, 2, DC, 2, S], stack=cell)
        q_bd = sb("q_bd", [P, 2, DC, 4, 2, S], stack=cell)
        v_ext = sb("v_ext", [P, 2, (HEADS + 2) * VW], stack=cell)
        decay = sb("decay", [P, 2, HEADS * S], stack=cell)
        cT = sb("cT", [P, 2, HEADS * S], stack=cell)
        den = sb("den", [P, HEADS], stack=cell)
        den2 = sb("den2", [P, HEADS], stack=cell)
        rden = sb("rden", [P, HEADS], stack=cell)
        hn = sb("hn", [P, HEADS, DH], stack=cell)
        h_st = sb("h_st", [P, 6], stack=cell)
        h_mv = sb("h_mv", [P, 2, 2], stack=cell)
        h_var = sb("h_var", [P, 1], stack=cell)
        h_rstd = sb("h_rstd", [P, 2, 1], stack=cell)
        h_sc = sb("h_sc", [P, 2, D], stack=cell)
        ls = sb("ls", [P, D], stack=cell)
        ls_t = sb("ls_t", [P, D], stack=cell)
        x_st = sb("x_st", [P, 6], stack=cell)
        x_mv = sb("x_mv", [P, 2, 2], stack=cell)
        x_var = sb("x_var", [P, 1], stack=cell)
        x_rstd = sb("x_rstd", [P, 2, 1], stack=cell)
        xnT = sb("xnT", [P, DC, S], stack=cell)
        wg_sb = sb("wg_sb", [P, DC, E], stack=cell)
        wg_pad = sb("wg_pad", [P, DC, LPAD // E, E], stack=cell)
        gates_only = ExitStack()
        x_in = sb("x_in", [P, 2, GB, D], stack=gates_only)
        c_in = sb("c_in", [P, 2, GB, D], stack=gates_only)
        gates_only.close()
        x_c = sb("x_c", [P, 4, D], stack=cell)
        c_c = sb("c_c", [P, 4, D], stack=cell)
        x1 = sb("x1", [P, 4, D], stack=cell)
        xn = sb("xn", [P, 4, D], stack=cell)
        cell.close()
        route = ExitStack()

        def rt(name, shape, dt=F32):
            return sb(name, shape, dt, stack=route)

        rmax = rt("rmax", [P, B])
        rz = rt("rz", [P, B, E])
        rexp = rt("rexp", [P, B, E])
        rsum = rt("rsum", [P, B])
        rrec = rt("rrec", [P, B])
        score = rt("score", [P, B, E])
        best = rt("best", [P, TOP, B])
        req = rt("req", [P, B, E])
        rkey = rt("rkey", [P, B, E])
        kmax = rt("kmax", [P, TOP, B])
        score2 = rt("score2", [P, B, E])
        chosen = rt("chosen", [P, B, E])
        rank = rt("rank", [P, B, E])
        onehot = rt("onehot", [P, E, TOP, B], BF16)
        reset = rt("reset", [P, E, KT])
        gsum = rt("gsum", [P, B])
        gclip = rt("gclip", [P, B])
        grec = rt("grec", [P, B])
        gval = rt("gval", [P, TOP, B])
        gw_t = rt("gw_t", [P, KT])
        before = rt("before", [P, E * KT])
        loc0 = rt("loc0", [P, E * KT])
        loc = rt("loc", [P, E, KT])
        locsel = rt("locsel", [P, E, KT])
        pos = rt("pos", [P, KT])
        pos_i = rt("pos_i", [P, KT], I32)
        row_i = rt("row_i", [P, KT], I32)
        col_i = rt("col_i", [P, KT], I32)
        row_f = rt("row_f", [P, KT])
        col_f = rt("col_f", [P, KT])
        col_b = rt("col_b", [P, KT])
        col_s = rt("col_s", [P, KT])
        token1 = rt("token1", [P, TOP, B])
        token_i = rt("token_i", [P, TOP, B], I32)
        iota_i = rt("iota_i", [P, P], I32)
        iota_f = rt("iota_f", [P, P])
        colhot = rt("colhot", [P, KT, E * SLOT_TILES])
        dump_i = rt("dump_i", [P, E, SLOT_TILES], I32)
        dump = rt("dump", [P, E * SLOT_TILES])
        slot_t = rt("slot_t", [P, E * SLOT_TILES])
        empty = rt("empty", [P, E * SLOT_TILES])
        dumped = rt("dumped", [P, E * SLOT_TILES])
        rowhot = qT[:].rearrange("p c n -> p (c n)").rearrange("p (k r) -> p k r", r=P)
        colval = kT[:].rearrange("p c n -> p (c n)").rearrange("p (k r) -> p k r", r=P)
        route.close()
        att.close()
        w1h = sb("w1h", [P, 2, DC, HID], F32R)
        w1l = sb("w1l", [P, 2, DC, HID], F32R)
        w2h = sb("w2h", [P, 2, HC, D], F32R)
        w2l = sb("w2l", [P, 2, HC, D], F32R)
        xg = sb("xg", [P, 2, UT, D])
        g_ix = sb("g_ix", [P, 2, UT], U32)
        s_ix = sb("s_ix", [P, 2, UT], U32)
        xh = sb("xh", [P, 2, DC, UW], F32R)
        xl = sb("xl", [P, 2, DC, UW], F32R)
        hf = sb("hf", [P, 3, UW])
        hh = sb("hh", [P, 2, HC, UW], F32R)
        hl = sb("hl", [P, 2, HC, UW], F32R)
        y_b = sb("y_b", [P, 2, UT, D])
        y_w = sb("y_w", [P, 2, UT, D])

        ps = keep.enter_context(nc.psum_tensor("ps", [P, 8, 512], F32))

        waited = sem("waited")
        const_ready = sem("const_ready")
        gw_ld = sem("gw_ld")
        misc_ld = sem("misc_ld")
        w_ld = sem("w_ld")
        x_ld = [sem("x_ld0"), sem("x_ld1")]
        c_ld = [sem("c_ld0"), sem("c_ld1")]
        wT_done = sem("wT_done")
        wT_copied = sem("wT_copied")
        wk_ready = sem("wk_ready")
        stats_done = sem("stats_done")
        g_seq = sem("g_seq")
        rstd_seq = sem("rstd_seq")
        rstd_done = sem("rstd_done")
        q_done = sem("q_done")
        kT_ps = sem("kT_ps")
        qT_ps = sem("qT_ps")
        kT_done = sem("kT_done")
        qT_done = sem("qT_done")
        gate_ps = sem("gate_ps")
        gate_done = sem("gate_done")
        gate_st = [sem("gate_st0"), sem("gate_st1")]
        pair_ld = [sem("pair_ld0"), sem("pair_ld1")]
        sc_v = [sem("sc_v0"), sem("sc_v1")]
        sc_a = [sem("sc_a0"), sem("sc_a1")]
        nmT_ps = sem("nmT_ps")
        nmT_done = sem("nmT_done")
        part_st = [sem("part_st0"), sem("part_st1")]
        tg_done = sem("tg_done")
        const_v = sem("const_v")
        pe_ld = [sem("pe_ld0"), sem("pe_ld1")]
        cc_ld = [sem("cc_ld0"), sem("cc_ld1")]
        xc_ld = [sem("xc_ld0"), sem("xc_ld1")]
        v_ready = sem("v_ready")
        z_ps = sem("z_ps")
        s_ps = sem("s_ps")
        exp_done = sem("exp_done")
        cT_done = sem("cT_done")
        h_ps = sem("h_ps")
        p1_seq = sem("p1_seq")
        hn_done = sem("hn_done")
        h_stat = sem("h_stat")
        h_pool = sem("h_pool")
        h_rs = sem("h_rs")
        hsc_done = sem("hsc_done")
        x1_done = sem("x1_done")
        x1_seq = sem("x1_seq")
        x_stat = sem("x_stat")
        x_pool = sem("x_pool")
        x_rs = sem("x_rs")
        xn_done = sem("xn_done")
        xnT_ps = sem("xnT_ps")
        xnT_done = sem("xnT_done")
        lg_ps = sem("lg_ps")
        lg_done = sem("lg_done")
        x1_st = [sem("x1_st0"), sem("x1_st1")]
        xn_st = [sem("xn_st0"), sem("xn_st1")]
        dump_st = sem("dump_st")
        rt_v = sem("rt_v")
        rt_a = sem("rt_a")
        rt_p = sem("rt_p")
        rt_c = sem("rt_c")
        count_ps = sem("count_ps")
        cv_id = sem("cv_id")
        cv_w = sem("cv_w")
        rh_done = sem("rh_done")
        slot_ps = sem("slot_ps")
        slots_done = sem("slots_done")
        w1h_done = sem("w1h_done")
        w1l_done = sem("w1l_done")
        w2h_done = sem("w2h_done")
        w2l_done = sem("w2l_done")
        ix_done = sem("ix_done")
        xg_ld = [sem("xg_ld0"), sem("xg_ld1")]
        xT_ps = sem("xT_ps")
        xh_done = sem("xh_done")
        xl_done = sem("xl_done")
        g1_ps = sem("g1_ps")
        gelu_done = sem("gelu_done")
        hh_done = sem("hh_done")
        hl_done = sem("hl_done")
        y_ps = sem("y_ps")
        yb_done = sem("yb_done")
        yw_done = sem("yw_done")
        six_done = sem("six_done")
        y_st = sem("y_st")
        out_st = sem("out_st")

        LAST_G = GROUPS
        MISC = 6
        A_SPLIT, M_SPLIT = 14, 15
        CONSTS = 10
        NJ = 4
        LOADS = 16 * (NJ + 3)
        LAST_LAG = 5

        def later(step, n):
            return not isinstance(step, int) or step >= n

        def live(step, n):
            return not isinstance(step, int) or 0 <= step < n

        block = keep.enter_context(nc.Block())

        @block.sync
        def _(sp):
            def load_group(g, k):
                if not isinstance(g, int) or g >= 2:
                    sp.wait_ge(kT_ps, 2 * (g - 1))
                    sp.sem_inc(waited, 1)
                sp.dma_start(c_in[:, k], ctx_rows[bass.ds(g * GW, GW)].rearrange("(b p) d -> p b d", p=P)).then_inc(c_ld[k], 16)
                if not isinstance(g, int) or g >= 2:
                    sp.wait_ge(q_done, 4 * (g - 1))
                    sp.sem_inc(waited, 1)
                sp.dma_start(x_in[:, k], x_rows[bass.ds(g * GW, GW)].rearrange("(b p) d -> p b d", p=P)).then_inc(x_ld[k], 16)

            load_group(0, 0)
            sp.dma_start(gate_rows[0:HEADS, :], igate_w).then_inc(gw_ld, 16)
            sp.dma_start(gate_rows[HEADS:2 * HEADS, :], fgate_w).then_inc(gw_ld, 16)
            sp.dma_start(b1_rows[:], b1.rearrange("e (m p) -> (e m) p", p=P)).then_inc(gw_ld, 16)
            load_group(1, 1)
            sp.dma_start(gate_b[0:HEADS, :], igate_b.rearrange("(h a) -> h a", a=1)).then_inc(misc_ld, 16)
            sp.dma_start(gate_b[HEADS:2 * HEADS, :], fgate_b.rearrange("(h a) -> h a", a=1)).then_inc(misc_ld, 16)
            sp.dma_start(ls[:], ln_scale.rearrange("(a d) -> a d", a=1).broadcast_to([P, D])).then_inc(misc_ld, 16)
            sp.dma_start(gx[:, 0:1], g_xattn.rearrange("(a d) -> a d", a=1).broadcast_to([P, 1])).then_inc(misc_ld, 16)
            sp.dma_start(gx[:, 1:2], g_ffn.rearrange("(a d) -> a d", a=1).broadcast_to([P, 1])).then_inc(misc_ld, 16)
            sp.dma_start(wg_sb[:], wg.rearrange("(c p) e -> p c e", p=P)).then_inc(misc_ld, 16)

            load_group(2, 0)
            load_group(3, 1)
            sp.wait_ge(const_v, 1)
            sp.dma_start(acc_dram[N:N + CAP].rearrange("(p j) d -> p (j d)", p=P),
                         q_bd[:, 1].rearrange("p c j b s -> p (c j b s)")).then_inc(dump_st, 16)
            with sp.Fori(2, GROUPS // 2) as i:
                for k in range(2):
                    load_group(2 * i + k, k)

            pairs = gates_dram.rearrange("h (b s) -> b h s", s=S)

            def load_gates(t):
                for k in range(2):
                    sp.wait_ge(gate_st[k], 16 * (t + 1) * GROUPS // (2 * PAIR_TILES))
                sp.dma_start(fg_p[:, t], pairs[t * BT:(t + 1) * BT, HEADS:2 * HEADS]).then_inc(pair_ld[t], 16)
                sp.dma_start(ig_p[:, t], pairs[t * BT:(t + 1) * BT, 0:HEADS]).then_inc(pair_ld[t], 16)

            def store_parts(t):
                ts = slice(t * S, (t + 1) * S)
                sp.wait_ge(sc_v[t], A_SPLIT)
                sp.dma_start(a_dram[t * BT:(t + 1) * BT].rearrange("b h j s -> (b h) j s"), parts[:, 0, :, ts]).then_inc(part_st[t], 16)
                sp.wait_ge(sc_v[t], M_SPLIT)
                sp.dma_start(m_dram[:, t * BT:(t + 1) * BT].rearrange("j b h s -> (b h) j s"), parts[:, 1, :, ts]).then_inc(part_st[t], 16)

            def load_qk(i, r):
                pair, t = 2 * i + r, r % 2
                if later(pair, 2):
                    sp.wait_ge(s_ps, 2 * pair - 2)
                two = bass.ds(2 * pair * S, 2 * S)
                sp.dma_start(k_st[:, t], kT[:, :, two].rearrange("p c (b s) -> p c b s", s=S)).then_inc(pe_ld[t], 16)
                for j in range(NJ):
                    sp.dma_start(q_bd[j * DH:(j + 1) * DH, t, :, j],
                                 qT[j * DH:(j + 1) * DH, :, two].rearrange("p c (b s) -> p c b s", s=S)).then_inc(pe_ld[t], 16)

            def load_z(i, r):
                pair, t = 2 * i + r, r % 2
                slots = slice(2 * t, 2 * t + 2)
                sp.dma_start(z_lhs[PARTS:PARTS + KA, slots],
                             a_dram[bass.ds(2 * pair, 2)].rearrange("b h j s -> (h j) b s")).then_inc(pe_ld[t], 16)
                sp.dma_start(z_rhs[0:PARTS, slots],
                             m_dram[:, bass.ds(2 * pair, 2)].rearrange("j b h s -> j b (h s)")).then_inc(pe_ld[t], 16)

            def pair_rows(rows, pair):
                return rows[bass.ds(2 * pair * S, 2 * S)].rearrange("(b p) d -> p b d", p=P)

            def load_c(i, r):
                pair, t = 2 * i + r, r % 2
                if later(pair, 2):
                    sp.wait_ge(v_ready, 2 * pair - 2)
                sp.dma_start(c_c[:, 2 * t:2 * t + 2], pair_rows(ctx_rows, pair)).then_inc(cc_ld[t], 16)

            def load_x(i, r):
                pair, t = 2 * i + r, r % 2
                if later(pair, 2):
                    sp.wait_ge(x1_done, 2 * pair - 2)
                sp.dma_start(x_c[:, 2 * t:2 * t + 2], pair_rows(x_rows, pair)).then_inc(xc_ld[t], 16)

            def store_rows(i, r):
                pair, t = 2 * i + r, r % 2
                sp.wait_ge(x1_done, 2 * pair + 2)
                sp.dma_start(pair_rows(acc_dram, pair), x1[:, 2 * t:2 * t + 2]).then_inc(x1_st[t], 16)
                sp.wait_ge(xn_done, 2 * pair + 2)
                sp.dma_start(pair_rows(xn_dram, pair), xn[:, 2 * t:2 * t + 2]).then_inc(xn_st[t], 16)

            load_gates(0)
            sp.wait_ge(qT_done, GROUPS)
            sp.wait_ge(kT_done, DC * GROUPS)
            sp.wait_ge(dump_st, 16)
            load_c(0, 0)
            load_qk(0, 0)
            load_c(0, 1)
            load_qk(0, 1)
            load_x(0, 0)
            sp.wait_ge(const_ready, CONSTS)
            store_parts(0)
            load_gates(1)
            sp.wait_ge(part_st[0], 16 * 2)
            load_z(0, 0)
            load_z(0, 1)

            def pair_step(i, r):
                for stage, lag in ((load_qk, 0), (load_z, 0), (load_c, 0), (load_x, 1), (store_rows, 3)):
                    if live(2 * i + r - lag, B // 2):
                        stage(i, r - lag)

            pair_step(0, 2)
            sp.dma_start(b2_all[:], b2.rearrange("(a e) d -> a e d", a=1).broadcast_to([P, E, D])).then_inc(w_ld, 16)
            pair_step(0, 3)
            store_parts(1)
            sp.wait_ge(part_st[1], 16 * 2)
            with sp.Fori(2, B // 4) as i:
                for r in range(2):
                    pair_step(i, r)
            pair_step(0, B // 2)
            sp.dma_start(w_raw1[:], w1[0].rearrange("(c p) h -> p c h", p=P)).then_inc(w_ld, 16)
            pair_step(0, B // 2 + 1)
            sp.dma_start(w_raw2[:], w2[0].rearrange("(k p) d -> p k d", p=P)).then_inc(w_ld, 16)
            pair_step(0, B // 2 + 2)

            with sp.Fori(1, E) as e:
                sp.wait_ge(w1h_done, e)
                sp.wait_ge(w1l_done, e)
                sp.dma_start(w_raw1[:], w1[bass.ds(e, 1)].rearrange("e (c p) h -> p (e c) h", p=P)).then_inc(w_ld, 16)
                sp.wait_ge(w2h_done, e)
                sp.wait_ge(w2l_done, e)
                sp.dma_start(w_raw2[:], w2[bass.ds(e, 1)].rearrange("e (k p) d -> p (e k) d", p=P)).then_inc(w_ld, 16)

            sp.wait_ge(y_st, 16 * E * SLOT_TILES)
            for q in range(4):
                rows = slice(q * N // 4, (q + 1) * N // 4)
                sp.dma_start(out_rows[rows], acc_dram[rows]).then_inc(out_st, 16)
            sp.wait_ge(out_st, 16 * 4)

        @block.gpsimd
        def _(pool):
            nc.gpsimd.memset(ident[:], 0.0).then_inc(rt_c, 1)
            nc.gpsimd.memset(tri_bf[:], 1.0).then_inc(rt_c, 1)
            pool.wait_ge(rt_c, 2)
            nc.gpsimd.affine_select(out=ident[:], in_=ident[:], compare_op=ALU.not_equal, fill=1.0, base=0,
                                    pattern=[[-1, P]], channel_multiplier=1).then_inc(const_ready, 1)
            nc.gpsimd.memset(neg_half[:], -0.5).then_inc(const_ready, 1)

            def group_rstd(g, k):
                pool.wait_ge(stats_done, g + 1)
                if not isinstance(g, int) or g >= 1:
                    pool.wait_ge(rstd_done, g)
                if not isinstance(g, int) or g >= 2:
                    pool.wait_ge(q_done, GB * (g - 1))
                pool.sem_inc(waited, 1)
                nc.gpsimd.tensor_scalar(g_var[:], g_mv[:, k, :, 1], LN_EPS, None, ALU.add).then_inc(rstd_seq, 1)
                pool.wait_ge(rstd_seq, g + 1)
                nc.gpsimd.tensor_tensor(g_rstd[:, k], g_var[:], neg_half[:], ALU.pow).then_inc(rstd_done, 1)

            group_rstd(0, 0)
            nc.gpsimd.memset(z_rhs[:, 0], 0.0).then_inc(rt_c, 1)
            nc.gpsimd.memset(mask_bf[:], 0.0).then_inc(rt_c, 1)
            nc.gpsimd.memset(z_lhs[:], 0.0).then_inc(rt_c, 1)
            nc.gpsimd.memset(v_ext[:], 1.0).then_inc(const_ready, 1)
            pool.wait_ge(const_ready, 2)
            nc.gpsimd.tensor_copy(ident_bf[:], ident[:]).then_inc(const_ready, 1)
            group_rstd(1, 1)
            nc.gpsimd.affine_select(out=tri_bf[:], in_=tri_bf[:], compare_op=ALU.is_ge, fill=0.0, base=0,
                                    pattern=[[1, P]], channel_multiplier=-1).then_inc(const_ready, 1)
            pool.wait_ge(rt_c, 5)
            nc.gpsimd.affine_select(out=mask_bf[:], in_=mask_bf[:], compare_op=ALU.is_ge, fill=MASKED, base=0,
                                    pattern=[[0, 4], [1, S]], channel_multiplier=-1).then_inc(const_ready, 1)
            nc.gpsimd.memset(z_lhs[0:PARTS], 1.0).then_inc(const_ready, 1)
            for g in range(2, 4):
                group_rstd(g, g % 2)
                for j in range(PARTS):
                    if (j < 2) == (g == 2):
                        pool.wait_ge(rt_c, 5 + j)
                        nc.gpsimd.affine_select(out=z_rhs[:, 0].rearrange("p (h s) -> p h s", h=HEADS),
                                                in_=z_rhs[:, 0].rearrange("p (h s) -> p h s", h=HEADS),
                                                compare_op=ALU.not_equal, fill=1.0, base=-(PARTS + j),
                                                pattern=[[-PARTS, HEADS], [0, S]], channel_multiplier=1).then_inc(rt_c, 1)
            with pool.Fori(2, GROUPS // 2) as i:
                for k in range(2):
                    group_rstd(2 * i + k, k)
            pool.wait_ge(rt_c, 8)
            for k in range(1, 4):
                nc.gpsimd.tensor_copy(z_rhs[:, k], z_rhs[:, 0]).then_inc(const_ready, 1)

            def values(i, r):
                b, k = 4 * i + r, r % 2
                pool.wait_ge(cc_ld[r // 2 % 2], 16 * (i + r // 4) + 16)
                if later(b, 2):
                    pool.wait_ge(h_ps, b - 1)
                pool.sem_inc(waited, 1)
                nc.gpsimd.tensor_copy(v_ext[:, k, 0:HEADS * VW].rearrange("p (h e) -> p h e", e=VW)[:, :, 0:DH],
                                      c_c[:, r % 4].rearrange("p (h e) -> p h e", e=DH)).then_inc(v_ready, 1)

            def head_rstd(i, r):
                b, k = 4 * i + r, r % 2
                pool.wait_ge(h_stat, b + 1)
                if later(b, 1):
                    pool.wait_ge(h_rs, b)
                if later(b, 2):
                    pool.wait_ge(x1_done, b - 1)
                pool.sem_inc(waited, 1)
                nc.gpsimd.tensor_scalar(h_var[:], h_mv[:, k, 1:2], LN_EPS, None, ALU.add).then_inc(h_pool, 1)
                pool.wait_ge(h_pool, b + 1)
                nc.gpsimd.tensor_tensor(h_rstd[:, k], h_var[:], neg_half[:, 0:1], ALU.pow).then_inc(h_rs, 1)

            def row_rstd(i, r):
                b, k = 4 * i + r, r % 2
                pool.wait_ge(x_stat, b + 1)
                if later(b, 1):
                    pool.wait_ge(x_rs, b)
                if later(b, 2):
                    pool.wait_ge(xn_done, b - 1)
                pool.sem_inc(waited, 1)
                nc.gpsimd.tensor_scalar(x_var[:], x_mv[:, k, 1:2], LN_EPS, None, ALU.add).then_inc(x_pool, 1)
                pool.wait_ge(x_pool, b + 1)
                nc.gpsimd.tensor_tensor(x_rstd[:, k], x_var[:], neg_half[:, 0:1], ALU.pow).then_inc(x_rs, 1)

            def pool_step(i, r):
                for stage, lag in ((row_rstd, 3), (head_rstd, 2), (values, 0)):
                    if live(4 * i + r - lag, B):
                        stage(i, r - lag)

            for r in range(8):
                pool_step(0, r)
            with pool.Fori(2, B // 4) as i:
                for r in range(4):
                    pool_step(i, r)
            for r in range(B, B + LAST_LAG):
                pool_step(0, r)

            pool.wait_ge(xn_done, B)
            pool.wait_ge(lg_done, B)
            for k in range(2):
                pool.wait_ge(xn_st[k], 16 * (B // 4))
                pool.wait_ge(x1_st[k], 16 * (B // 4))
            nc.gpsimd.iota(iota_i[:], pattern=[[1, P]], base=0, channel_multiplier=0).then_inc(rt_p, 1)
            nc.gpsimd.iota(token_i[:], pattern=[[0, TOP], [S, B]], base=1, channel_multiplier=1).then_inc(rt_p, 1)
            nc.gpsimd.iota(dump_i[:], pattern=[[0, E], [1, SLOT_TILES]], base=N + 1, channel_multiplier=SLOT_TILES).then_inc(rt_p, 1)
            for e in range(E):
                nc.gpsimd.memset(rank[:, :, e:e + 1], float(E - e)).then_inc(rt_p, 1)
            nc.gpsimd.memset(reset[:], 1.0).then_inc(rt_p, 1)
            pool.wait_ge(rt_p, 12)
            nc.gpsimd.memset(reset[:, :, 0:1], 0.0).then_inc(rt_p, 1)
            nc.gpsimd.tensor_copy(iota_f[:], iota_i[:]).then_inc(rt_p, 1)
            nc.gpsimd.tensor_copy(token1[:], token_i[:]).then_inc(rt_p, 1)
            nc.gpsimd.tensor_copy(dump[:], dump_i[:].rearrange("p e j -> p (e j)")).then_inc(rt_p, 1)

            for q in range(4):
                pool.wait_ge(rt_v, 33 + q)
                ks = slice(q * KT // 4, (q + 1) * KT // 4)
                nc.gpsimd.tensor_tensor(colval[:, ks, E * SLOT_TILES:],
                                        colhot[:, ks, :], gw_t[:, ks].unsqueeze(2).broadcast_to([P, KT // 4, E * SLOT_TILES]),
                                        ALU.mult).then_inc(cv_w, 1)

            pool.wait_ge(slots_done, 3)
            for k in range(2):
                pool.wait_ge(xn_st[k], 16 * (B // 4))
            pool.wait_ge(dump_st, 16)

            def gather(u, k):
                if not isinstance(u, int) or u >= 2:
                    pool.wait_ge(xT_ps, 2 * (u - 1))
                    pool.wait_ge(xg_ld[k], 8 * UT * (u - k))
                pool.sem_inc(waited, 1)
                nc.gpsimd.tensor_copy(g_ix[:, k], gather_idx[:, bass.ds(u * UT, UT)]).then_inc(ix_done, 1)
                pool.wait_ge(ix_done, u + 1)
                pool.sem_inc(waited, 1)
                for j in range(UT):
                    nc.gpsimd.indirect_dma_start(xg[:, k, j], None, xn_dram,
                                                 bass.IndirectOffsetOnAxis(ap=g_ix[:, k, j:j + 1], axis=0)).then_inc(xg_ld[k], 16)

            def scatter(u, k):
                if not isinstance(u, int) or u >= 1:
                    pool.wait_ge(y_st, 16 * UT * u)
                pool.sem_inc(waited, 1)
                nc.gpsimd.tensor_copy(s_ix[:, k], scatter_idx[:, bass.ds(u * UT, UT)]).then_inc(six_done, 1)
                pool.wait_ge(six_done, u + 1)
                for j in range(UT):
                    pool.wait_ge(yw_done, UT * u + j + 1)
                    pool.sem_inc(waited, 1)
                    nc.gpsimd.indirect_dma_start(acc_dram, bass.IndirectOffsetOnAxis(ap=s_ix[:, k, j:j + 1], axis=0),
                                                 y_w[:, k, j], None, compute_op=ALU.add).then_inc(y_st, 16)

            for u in range(4):
                gather(u, u % 2)
                if u >= 3:
                    scatter(u - 3, (u - 3) % 2)
            with pool.Fori(2, UNITS // 2) as i:
                for k in range(2):
                    gather(2 * i + k, k)
                    scatter(2 * i + k - 3, 1 - k)
            for u in range(UNITS - 3, UNITS):
                scatter(u, u % 2)
            pool.wait_ge(y_st, 16 * E * SLOT_TILES)

        @block.scalar
        def _(act):
            act.wait_ge(wT_done, 1)
            nc.scalar.copy(gate_wT[:], ps[:, 0, 0:3 * DC * 2 * HEADS].rearrange("p (c g) -> p c g", g=2 * HEADS)).then_inc(wT_copied, 1)
            nc.scalar.copy(b1_cols[:], ps[:, 1, 0:E * HC]).then_inc(wT_copied, 1)
            act.wait_ge(misc_ld, 16 * MISC)
            nc.scalar.activation(tanh_g[:], gx[:], ACT.Tanh).then_inc(tg_done, 1)

            def copy_kT(g):
                for c in range(DC):
                    act.wait_ge(kT_ps, DC * g + c + 1)
                    nc.scalar.copy(kT[:, c, bass.ds(g * GW, GW)], ps[:, c, :]).then_inc(kT_done, 1)

            def copy_gates(g, k):
                act.wait_ge(gate_ps, g + 1)
                if not isinstance(g, int) or g >= 2:
                    act.wait_ge(gate_st[k], 8 * (g - k))
                nc.scalar.activation(gates_sb[:, k], ps[0:2 * HEADS, 4, :], ACT.Identity, bias=gate_b[:, 0:1]).then_inc(gate_done, 1)
                act.wait_ge(gate_done, g + 1)
                act.dma_start(gates_dram[:, bass.ds(g * GW, GW)], gates_sb[:, k]).then_inc(gate_st[k], 16)

            for g in range(4):
                copy_kT(g)
                if g >= 2:
                    copy_gates(g - 2, g % 2)
            with act.Fori(2, GROUPS // 2) as i:
                for k in range(2):
                    copy_kT(2 * i + k)
                    copy_gates(2 * i + k - 2, k)
            copy_gates(GROUPS - 2, 0)

            def softplus(t):
                ts = slice(t * S, (t + 1) * S)
                act.wait_ge(sc_v[t], 1)
                nc.scalar.activation(fe[:, ts], fa[:, ts], ACT.Exp).then_inc(sc_a[t], 1)
                act.wait_ge(sc_a[t], 1)
                nc.scalar.activation(fl[:, ts], fe[:, ts], ACT.Ln, bias=1.0).then_inc(sc_a[t], 1)

            def exp_max(t):
                ts = slice(t * S, (t + 1) * S)
                act.wait_ge(sc_v[t], 7)
                nc.scalar.activation(nm[:, ts], msum[:, ts], ACT.Exp, scale=-1.0).then_inc(sc_a[t], 1)

            softplus(0)
            copy_gates(GROUPS - 1, 1)
            exp_max(0)

            def decays(i, r):
                b, k = 4 * i + r, r % 2
                act.wait_ge(z_ps, b + 1)
                if later(b, 2):
                    act.wait_ge(cT_done, b - 1)
                nc.scalar.activation(decay[:, k], ps[:, 0:2, :].rearrange("p a b -> p (a b)"), ACT.Exp).then_inc(exp_done, 1)

            def copy_xnT(i, r):
                b = 4 * i + r
                act.wait_ge(xnT_ps, b + 1)
                if later(b, 1):
                    act.wait_ge(lg_ps, b)
                nc.scalar.copy(xnT[:], ps[:, 6, 0:DC * S].rearrange("p (c s) -> p c s", s=S)).then_inc(xnT_done, 1)

            def copy_logits(i, r):
                b = 4 * i + r
                act.wait_ge(lg_ps, b + 1)
                nc.scalar.copy(logits[:, bass.ds(b, 1)].rearrange("p a e -> p (a e)"), ps[:, 7, 0:E]).then_inc(lg_done, 1)

            def act_step(i, r):
                for stage, lag in ((copy_xnT, 5), (decays, 0), (copy_logits, 5)):
                    if live(4 * i + r - lag, B):
                        stage(i, r - lag)

            for r in range(8):
                act_step(0, r)
                if r == 2:
                    softplus(1)
                if r == 3:
                    exp_max(1)
            with act.Fori(2, B // 4) as i:
                for r in range(4):
                    act_step(i, r)
            for r in range(B, B + LAST_LAG):
                act_step(0, r)

            act.wait_ge(rt_v, 2)
            nc.scalar.activation(rexp[:], rz[:], ACT.Exp).then_inc(rt_a, 1)

            def split_w(e, k):
                act.wait_ge(w_ld, 32 * e + 48)
                if not isinstance(e, int) or e >= 2:
                    act.wait_ge(g1_ps, 2 * HC * (e - 1))
                nc.scalar.copy(w1h[:, k], w_raw1[:]).then_inc(w1h_done, 1)
                if not isinstance(e, int) or e >= 2:
                    act.wait_ge(y_ps, 2 * 2 * (e - 1))
                nc.scalar.copy(w2h[:, k], w_raw2[:]).then_inc(w2h_done, 1)

            def round_x(u, k):
                for c in range(DC):
                    act.wait_ge(xT_ps, DC * u + c + 1)
                    if not isinstance(u, int) or u >= 2:
                        act.wait_ge(g1_ps, HC * (u - 1))
                    nc.scalar.copy(xh[:, k, c], ps[:, c, :]).then_inc(xh_done, 1)

            def gelu(u, par):
                for m in range(HC):
                    act.wait_ge(g1_ps, HC * u + m + 1)
                    slot = (HC * par + m) % 3
                    if not isinstance(u, int) or HC * u + m >= 3:
                        act.wait_ge(hl_done, HC * u + m - 2)
                    b1_c = HC * (u // 2) + m if isinstance(u, int) else None
                    bias = b1_cols[:, b1_c:b1_c + 1] if b1_c is not None else b1_cols[:, bass.ds(b1_at[0] + m, 1)]
                    nc.scalar.activation(hf[:, slot], ps[:, 2 + (HC * par + m) % 3, :], ACT.Gelu, bias=bias).then_inc(gelu_done, 1)

            def weigh_y(u, k):
                for j in range(UT):
                    if j % 2 == 0:
                        act.wait_ge(yb_done, 2 * u + j // 2 + 1)
                    if not isinstance(u, int) or u >= 2:
                        act.wait_ge(y_st, 16 * UT * (u - 1))
                    scale = slot_w[:, bass.ds(u * UT + j, 1)]
                    nc.scalar.mul(y_w[:, k, j], y_b[:, k, j], scale).then_inc(yw_done, 1)

            b1_at = [0]
            act.wait_ge(slot_ps, 1)
            act.wait_ge(slots_done, 3)
            for s in range(UNITS + 2):
                if s < UNITS and s % 2 == 0:
                    split_w(s // 2, (s // 2) % 2)
                if s < UNITS:
                    round_x(s, s % 2)
                if 1 <= s <= UNITS:
                    gelu(s - 1, (s - 1) % 3)
                if s >= 2:
                    weigh_y(s - 2, s % 2)

        @block.tensor
        def _(pe):
            pe.wait_ge(gw_ld, 16 * 3)
            pe.wait_ge(const_ready, 1)
            for c in range(3 * DC):
                nc.tensor.transpose(ps[:, 0, c * 2 * HEADS:(c + 1) * 2 * HEADS], gate_rows[:, c * P:(c + 1) * P],
                                    ident[0:2 * HEADS, 0:2 * HEADS])
            nc.tensor.transpose(ps[:, 1, 0:E * HC], b1_rows[:], ident[0:E * HC, 0:E * HC]).then_inc(wT_done, 1)
            pe.wait_ge(wT_copied, 2)
            pe.wait_ge(wk_ready, 1)

            def turn_ctx(g, k):
                pe.wait_ge(c_ld[k], 16 * ((g - k) // 2) + 16 if isinstance(g, int) else 8 * (g - k) + 16)
                for c in range(DC):
                    if not isinstance(g, int) or g >= 1:
                        pe.wait_ge(kT_done, DC * (g - 1) + c + 1)
                    for b in range(GB):
                        last = nc.tensor.transpose(ps[:, c, b * S:(b + 1) * S], c_in[:, k, b, c * P:(c + 1) * P], ident[:])
                    last.then_inc(kT_ps, 1)

            def turn_q(g, k):
                pe.wait_ge(q_done, GB * (g + 1))
                if not isinstance(g, int) or g >= 1:
                    pe.wait_ge(qT_done, g)
                for c in range(DC):
                    for b in range(GB):
                        last = nc.tensor.transpose(ps[:, 2 + c, b * S:(b + 1) * S], q_rows[:, k, b, c * P:(c + 1) * P], ident[:])
                last.then_inc(qT_ps, 1)

            def gates(g):
                pe.wait_ge(qT_done, g + 1)
                pe.wait_ge(kT_done, DC * (g + 1))
                if not isinstance(g, int) or g >= 1:
                    pe.wait_ge(gate_done, g)
                for c in range(DC):
                    nc.tensor.matmul(ps[0:2 * HEADS, 4, :], gate_wT[:, c], qT[:, c, bass.ds(g * GW, GW)], start=(c == 0), stop=False)
                for c in range(DC):
                    last = nc.tensor.matmul(ps[0:2 * HEADS, 4, :], gate_wk[:, c], kT[:, c, bass.ds(g * GW, GW)], start=False, stop=(c == DC - 1))
                last.then_inc(gate_ps, 1)

            for g in range(4):
                turn_ctx(g, g % 2)
                if g >= 1:
                    turn_q(g - 1, (g - 1) % 2)
                if g >= 2:
                    gates(g - 2)
            with pe.Fori(2, GROUPS // 2) as i:
                for k in range(2):
                    turn_ctx(2 * i + k, k)
                    turn_q(2 * i + k - 1, 1 - k)
                    gates(2 * i + k - 2)
            turn_q(GROUPS - 1, (GROUPS - 1) % 2)
            gates(GROUPS - 2)
            gates(GROUPS - 1)

            def turn_max(t):
                pe.wait_ge(sc_a[t], 3)
                nc.tensor.transpose(ps[:, 7, t * P:(t + 1) * P], nm[:, t * S:(t + 1) * S], ident[:]).then_inc(nmT_ps, 1)

            def exponents(i, r):
                b, t = 4 * i + r, r % 4
                pe.wait_ge(pe_ld[t // 2], LOADS * (i + r // 4) + LOADS)
                if later(b, 1):
                    pe.wait_ge(exp_done, b)
                for n in range(2):
                    nc.tensor.matmul(ps[:, n, :], z_lhs[:, t], z_rhs[:, t, n * 512:(n + 1) * 512], start=True, stop=False)
                    last = nc.tensor.matmul(ps[:, n, :], ident_bf[:], mask_bf[:].rearrange("p j s -> p (j s)"), start=False, stop=True)
                last.then_inc(z_ps, 1)

            def scores(i, r):
                b, t = 4 * i + r, r % 4
                if later(b, 1):
                    pe.wait_ge(cT_done, b)
                for c in range(DC):
                    last = nc.tensor.matmul(ps[:, 2 + c, :].rearrange("p (j s) -> p j s", s=S), k_st[:, t // 2, c, t % 2],
                                            q_bd[:, t // 2, c, :, t % 2], start=True, stop=True)
                last.then_inc(s_ps, 1)

            def head_sums(i, r):
                b, k = 4 * i + r, r % 2
                pe.wait_ge(cT_done, b + 1)
                pe.wait_ge(v_ready, b + 1)
                if later(b, 1):
                    pe.wait_ge(hn_done, b)
                for h in range(HEADS):
                    last = nc.tensor.matmul(ps[:, 4 + h // 4, (h % 4) * P:(h % 4) * P + VWIN], cT[:, k, h * S:(h + 1) * S],
                                            v_ext[:, k, h * VW:h * VW + VWIN], start=True, stop=True)
                last.then_inc(h_ps, 1)

            def turn_xn(i, r):
                b = 4 * i + r
                pe.wait_ge(xn_done, b + 1)
                if later(b, 1):
                    pe.wait_ge(xnT_done, b)
                for c in range(DC):
                    last = nc.tensor.transpose(ps[:, 6, c * S:(c + 1) * S], xn[:, r % 4, c * P:(c + 1) * P], ident[:])
                last.then_inc(xnT_ps, 1)

            def router(i, r):
                b = 4 * i + r
                pe.wait_ge(xnT_done, b + 1)
                if later(b, 1):
                    pe.wait_ge(lg_done, b)
                for c in range(DC):
                    last = nc.tensor.matmul(ps[:, 7, 0:LPAD], xnT[:, c], wg_pad[:, c].rearrange("p r e -> p (r e)"),
                                            start=(c == 0), stop=(c == DC - 1))
                last.then_inc(lg_ps, 1)

            def pe_step(i, r):
                for stage, lag in ((turn_xn, 5), (exponents, 0), (scores, 0), (router, 5), (head_sums, 1)):
                    if live(4 * i + r - lag, B):
                        stage(i, r - lag)

            pe.wait_ge(const_ready, CONSTS)
            pe.wait_ge(const_v, 3)
            for r in range(8):
                if r == 1:
                    turn_max(0)
                if r == 5:
                    turn_max(1)
                    pe.wait_ge(nmT_done, 2)
                pe_step(0, r)
            with pe.Fori(2, B // 4) as i:
                for r in range(4):
                    pe_step(i, r)
            for r in range(B, B + LAST_LAG):
                pe_step(0, r)

            pe.wait_ge(rt_v, 21)
            oh = onehot[:].rearrange("p e k b -> p (e k b)")
            nc.tensor.matmul(ps[:, 0, :], ones_bf[:], oh, start=True, stop=True).then_inc(count_ps, 1)
            nc.tensor.matmul(ps[:, 1, :], tri_bf[:], oh, start=True, stop=True).then_inc(count_ps, 1)
            for q in range(4):
                pe.wait_ge(cv_id, q + 1)
                pe.wait_ge(cv_w, q + 1)
                pe.wait_ge(rh_done, q + 1)
                for kt in range(q * KT // 4, (q + 1) * KT // 4):
                    last = nc.tensor.matmul(ps[:, 2, 0:2 * E * SLOT_TILES], rowhot[:, kt], colval[:, kt],
                                            start=(kt == 0), stop=(kt == KT - 1))
            last.then_inc(slot_ps, 1)

            def turn_x(u, k):
                pe.wait_ge(xg_ld[k], 16 * UT * (u // 2 + 1) if isinstance(u, int) else 8 * UT * (u - k) + 16 * UT)
                for c in range(DC):
                    if not isinstance(u, int) or u >= 1:
                        pe.wait_ge(xl_done, DC * (u - 1) + c + 1)
                    for j in range(UT):
                        last = nc.tensor.transpose(ps[:, c, j * P:(j + 1) * P], xg[:, k, j, c * P:(c + 1) * P], ident[:])
                    last.then_inc(xT_ps, 1)

            def hidden(u, k, wk, par):
                if k == 0:
                    pe.wait_ge(w1l_done, u // 2 + 1)
                pe.wait_ge(xl_done, DC * (u + 1))
                for m in range(HC):
                    bank = 2 + (HC * par + m) % 3
                    if not isinstance(u, int) or HC * u + m >= 3:
                        pe.wait_ge(gelu_done, HC * u + m - 2)
                    ms = slice(m * P, (m + 1) * P)
                    for c in range(DC):
                        nc.tensor.matmul(ps[:, bank, :], w1h[:, wk, c, ms], xh[:, k, c], start=(c == 0), stop=False)
                        nc.tensor.matmul(ps[:, bank, :], w1h[:, wk, c, ms], xl[:, k, c], start=False, stop=False)
                        last = nc.tensor.matmul(ps[:, bank, :], w1l[:, wk, c, ms], xh[:, k, c], start=False, stop=(c == DC - 1))
                    last.then_inc(g1_ps, 1)

            def outputs(u, k, wk):
                if k == 0:
                    pe.wait_ge(w2l_done, u // 2 + 1)
                pe.wait_ge(hl_done, HC * (u + 1))
                for j in range(UT):
                    if j % 2 == 0 and (not isinstance(u, int) or u >= 1):
                        pe.wait_ge(yb_done, 2 * (u - 1) + j // 2 + 1)
                    js = slice(j * P, (j + 1) * P)
                    o = ps[:, 5 + j // 2, (j % 2) * D:(j % 2 + 1) * D]
                    for m in range(HC):
                        nc.tensor.matmul(o, hh[:, k, m, js], w2h[:, wk, m], start=(m == 0), stop=False)
                        nc.tensor.matmul(o, hh[:, k, m, js], w2l[:, wk, m], start=False, stop=False)
                        last = nc.tensor.matmul(o, hl[:, k, m, js], w2h[:, wk, m], start=False, stop=(m == HC - 1))
                    if j % 2 == 1:
                        last.then_inc(y_ps, 1)

            pe.wait_ge(slots_done, 3)
            for s in range(UNITS + 2):
                if s < UNITS:
                    turn_x(s, s % 2)
                if 1 <= s <= UNITS:
                    hidden(s - 1, (s - 1) % 2, ((s - 1) // 2) % 2, (s - 1) % 3)
                if s >= 2:
                    outputs(s - 2, s % 2, ((s - 2) // 2) % 2)

        @block.vector
        def _(dve):
            nc.vector.memset(q_bd[:], 0.0).then_inc(const_v, 1)
            dve.wait_ge(wT_copied, 2)
            nc.vector.tensor_tensor(gate_wk[:], gate_wT[:, DC:2 * DC], gate_wT[:, 2 * DC:3 * DC], ALU.add).then_inc(wk_ready, 1)

            def stats(g, k):
                dve.wait_ge(x_ld[k], 16 * ((g - k) // 2) + 16 if isinstance(g, int) else 8 * (g - k) + 16)
                if not isinstance(g, int) or g >= 1:
                    dve.wait_ge(stats_done, g)
                if not isinstance(g, int) or g >= 2:
                    dve.wait_ge(q_done, GB * (g - 1))
                    dve.wait_ge(rstd_done, g - 1)
                for b in range(GB):
                    last = nc.vector.bn_stats(g_stats[:, b], x_in[:, k, b])
                last.then_inc(g_seq, 1)
                dve.wait_ge(g_seq, g + 1)
                dve.sem_inc(waited, 1)
                for b in range(GB):
                    last = nc.vector.bn_aggr(g_mv[:, k, b], g_stats[:, b])
                last.then_inc(stats_done, 1)

            def normalise(g, k):
                dve.wait_ge(rstd_done, g + 1)
                dve.wait_ge(stats_done, g + 1)
                if not isinstance(g, int) or g >= 2:
                    dve.wait_ge(qT_ps, g - 1)
                for b in range(GB):
                    nc.vector.tensor_scalar(q_rows[:, k, b], x_in[:, k, b], g_mv[:, k, b, 0:1], g_rstd[:, k, b:b + 1],
                                            ALU.subtract, ALU.mult).then_inc(q_done, 1)

            def copy_qT(g):
                dve.wait_ge(qT_ps, g + 1)
                nc.vector.tensor_copy(qT[:, :, bass.ds(g * GW, GW)], ps[:, 2:4, :]).then_inc(qT_done, 1)

            stats(0, 0)
            for g in range(1, 4):
                if g >= 2:
                    copy_qT(g - 2)
                normalise(g - 1, (g - 1) % 2)
                stats(g, g % 2)
            with dve.Fori(2, GROUPS // 2) as i:
                for k in range(2):
                    copy_qT(2 * i + k - 2)
                    normalise(2 * i + k - 1, 1 - k)
                    stats(2 * i + k, k)
            copy_qT(GROUPS - 2)
            normalise(GROUPS - 1, (GROUPS - 1) % 2)
            copy_qT(GROUPS - 1)

            nc.vector.memset(ones_bf[:], 1.0)
            nc.vector.memset(ones_row[:], 1.0)
            nc.vector.memset(zero_row[:], 0.0)
            dve.wait_ge(misc_ld, 16 * MISC)
            nc.vector.tensor_copy(wg_pad[:], wg_sb[:].unsqueeze(2).broadcast_to([P, DC, LPAD // E, E])).then_inc(const_v, 1)
            dve.wait_ge(tg_done, 1)
            nc.vector.tensor_scalar(ls_t[:], ls[:], tanh_g[:, 0:1], None, ALU.mult).then_inc(const_v, 1)

            def fgate_abs(t):
                dve.wait_ge(pair_ld[t], 16 * 2)
                nc.vector.scalar_tensor_tensor(out=fa[:, t * S:(t + 1) * S], in0=fg_p[:, t], scalar=-1.0, in1=fg_p[:, t], op0=ALU.mult,
                                               op1=ALU.min).then_inc(sc_v[t], 1)

            def scans(t):
                ts = slice(t * S, (t + 1) * S)
                dve.wait_ge(sc_a[t], 2)
                nc.vector.scalar_tensor_tensor(out=logf[:, ts], in0=fg_p[:, t], scalar=0.0, in1=fl[:, ts], op0=ALU.min,
                                               op1=ALU.subtract).then_inc(sc_v[t], 1)
                dve.wait_ge(sc_v[t], 2)
                nc.vector.tensor_tensor_scan(cs[:, ts], ones_row[:], logf[:, ts], 0.0, ALU.mult, ALU.add).then_inc(sc_v[t], 1)
                dve.wait_ge(sc_v[t], 3)
                nc.vector.tensor_tensor(av[:, ts], ig_p[:, t], cs[:, ts], ALU.subtract).then_inc(sc_v[t], 1)
                dve.wait_ge(sc_v[t], 4)
                nc.vector.tensor_tensor_scan(mv[:, ts], zero_row[:], av[:, ts], LOWEST, ALU.add, ALU.max).then_inc(sc_v[t], 1)
                dve.wait_ge(sc_v[t], 5)
                nc.vector.tensor_scalar(negm[:, ts], mv[:, ts], -1.0, None, ALU.mult).then_inc(sc_v[t], 1)
                nc.vector.tensor_tensor(msum[:, ts], cs[:, ts], mv[:, ts], ALU.add).then_inc(sc_v[t], 1)

            def split_scans(t):
                ts = slice(t * S, (t + 1) * S)
                dve.wait_ge(sc_v[t], 6)
                for n, src in ((0, av), (1, negm)):
                    nc.vector.tensor_copy(parts[:, n, 0, ts], src[:, ts]).then_inc(sc_v[t], 1)
                for n, src in ((0, av), (1, negm)):
                    dve.wait_ge(sc_v[t], 8 + n)
                    nc.vector.tensor_tensor(res1[:, n, ts], src[:, ts], parts[:, n, 0, ts], ALU.subtract).then_inc(sc_v[t], 1)
                for n in range(2):
                    dve.wait_ge(sc_v[t], 10 + n)
                    nc.vector.tensor_copy(parts[:, n, 1, ts], res1[:, n, ts]).then_inc(sc_v[t], 1)
                for n in range(2):
                    dve.wait_ge(sc_v[t], 12 + n)
                    nc.vector.tensor_tensor(parts[:, n, 2, ts], res1[:, n, ts], parts[:, n, 1, ts], ALU.subtract).then_inc(sc_v[t], 1)

            def keep_max(t):
                dve.wait_ge(nmT_ps, t + 1)
                nc.vector.tensor_scalar(nmT[:, t * P:(t + 1) * P], ps[:, 7, t * P:(t + 1) * P], NORM_EPS, None, ALU.add).then_inc(nmT_done, 1)

            fgate_abs(0)
            scans(0)
            split_scans(0)

            def weigh(i, r):
                b, k = 4 * i + r, r % 2
                dve.wait_ge(exp_done, b + 1)
                dve.wait_ge(s_ps, b + 1)
                if later(b, 2):
                    dve.wait_ge(h_ps, b - 1)
                nc.vector.scalar_tensor_tensor(out=cT[:, k], in0=ps[:, 2:4, :].rearrange("p a b -> p (a b)"),
                                               scalar=float(DH) ** -0.5, in1=decay[:, k], op0=ALU.mult,
                                               op1=ALU.mult).then_inc(cT_done, 1)

            hp = ps[:, 4:6, :].rearrange("p a (h w) -> p (a h) w", w=P)
            hrow = hn[:].rearrange("p h e -> p (h e)")

            def head_den(i, r):
                b = 4 * i + r
                dve.wait_ge(h_ps, b + 1)
                if later(b, 1):
                    dve.wait_ge(hsc_done, b)
                nc.vector.scalar_tensor_tensor(out=den[:].unsqueeze(2), in0=hp[:, :, DH:DH + 1], scalar=NORM_EPS,
                                               in1=nmT[:, bass.ds(b * HEADS, HEADS)].unsqueeze(2),
                                               op0=ALU.subtract, op1=ALU.max, reverse0=True).then_inc(p1_seq, 1)

            def head_den2(i, r):
                dve.wait_ge(p1_seq, 4 * (4 * i + r) + 1)
                nc.vector.scalar_tensor_tensor(out=den2[:].unsqueeze(2), in0=hp[:, :, DH:DH + 1], scalar=NORM_EPS,
                                               in1=den[:].unsqueeze(2), op0=ALU.add, op1=ALU.max).then_inc(p1_seq, 1)

            def head_rden(i, r):
                dve.wait_ge(p1_seq, 4 * (4 * i + r) + 2)
                nc.vector.reciprocal(rden[:], den2[:]).then_inc(p1_seq, 1)

            def head_scale(i, r):
                dve.wait_ge(p1_seq, 4 * (4 * i + r) + 3)
                nc.vector.tensor_tensor(hn[:], hp[:, :, 0:DH], rden[:].unsqueeze(2).broadcast_to([P, HEADS, DH]),
                                        ALU.mult).then_inc(hn_done, 1)

            def head_stats(i, r):
                dve.wait_ge(hn_done, 4 * i + r + 1)
                nc.vector.bn_stats(h_st[:], hrow).then_inc(p1_seq, 1)

            def head_mean(i, r):
                b, k = 4 * i + r, r % 2
                if later(b, 2):
                    dve.wait_ge(h_rs, b - 1)
                dve.wait_ge(p1_seq, 4 * b + 4)
                dve.sem_inc(waited, 1)
                nc.vector.bn_aggr(h_mv[:, k], h_st[:]).then_inc(h_stat, 1)

            def head_center(i, r):
                b, k = 4 * i + r, r % 2
                dve.wait_ge(h_stat, b + 1)
                if later(b, 2):
                    dve.wait_ge(x1_done, b - 1)
                nc.vector.scalar_tensor_tensor(out=h_sc[:, k], in0=hrow, scalar=h_mv[:, k, 0:1], in1=ls_t[:],
                                               op0=ALU.subtract, op1=ALU.mult).then_inc(hsc_done, 1)

            def residual(i, r):
                b, k, t = 4 * i + r, r % 2, r % 4
                dve.wait_ge(h_rs, b + 1)
                dve.wait_ge(hsc_done, b + 1)
                dve.wait_ge(xc_ld[t // 2], 16 * (i + r // 4) + 16)
                if later(b, 4):
                    dve.wait_ge(xn_done, b - 3)
                    dve.wait_ge(x1_st[t // 2], 16 * (i + r // 4))
                nc.vector.scalar_tensor_tensor(out=x1[:, t], in0=h_sc[:, k], scalar=h_rstd[:, k], in1=x_c[:, t],
                                               op0=ALU.mult, op1=ALU.add).then_inc(x1_done, 1)

            def row_stats(i, r):
                b = 4 * i + r
                dve.wait_ge(x1_done, b + 1)
                if later(b, 1):
                    dve.wait_ge(x_stat, b)
                nc.vector.bn_stats(x_st[:], x1[:, r % 4]).then_inc(x1_seq, 1)

            def row_mean(i, r):
                b, k = 4 * i + r, r % 2
                if later(b, 2):
                    dve.wait_ge(x_rs, b - 1)
                    dve.wait_ge(xn_done, b - 1)
                dve.wait_ge(x1_seq, b + 1)
                dve.sem_inc(waited, 1)
                nc.vector.bn_aggr(x_mv[:, k], x_st[:]).then_inc(x_stat, 1)

            def norm_rows(i, r):
                b, k, t = 4 * i + r, r % 2, r % 4
                dve.wait_ge(x_rs, b + 1)
                dve.wait_ge(x_stat, b + 1)
                if later(b, 4):
                    dve.wait_ge(xnT_ps, b - 3)
                    dve.wait_ge(xn_st[t // 2], 16 * (i + r // 4))
                nc.vector.tensor_scalar(xn[:, t], x1[:, t], x_mv[:, k, 0:1], x_rstd[:, k], ALU.subtract, ALU.mult).then_inc(xn_done, 1)

            def dve_step(i, r):
                for stage, lag in ((head_den, 2), (residual, 3), (head_den2, 2), (row_stats, 3), (head_rden, 2), (row_mean, 3),
                                   (head_scale, 2), (weigh, 0), (head_stats, 2), (norm_rows, 4), (head_mean, 2),
                                   (head_center, 2)):
                    if live(4 * i + r - lag, B):
                        stage(i, r - lag)

            dve.wait_ge(const_v, 3)
            for r in range(8):
                dve_step(0, r)
                if r == 1:
                    keep_max(0)
                    dve.wait_ge(nmT_done, 1)
                    fgate_abs(1)
                if r == 2:
                    scans(1)
                if r == 3:
                    split_scans(1)
                if r == 4:
                    keep_max(1)
            with dve.Fori(2, B // 4) as i:
                for r in range(4):
                    dve_step(i, r)
            for r in range(B, B + LAST_LAG):
                dve_step(0, r)

            def over(t, n=E):
                return t.unsqueeze(2).broadcast_to([P, B, n])

            dve.wait_ge(rt_p, 12 + 4)
            dve.wait_ge(lg_done, B)
            for k in range(2):
                dve.wait_ge(xn_st[k], 16 * (B // 4))
            nc.vector.tensor_reduce(rmax[:], logits[:], AX_X, ALU.max).then_inc(rt_v, 1)
            dve.wait_ge(rt_v, 1)
            nc.vector.tensor_tensor(rz[:], logits[:], over(rmax[:]), ALU.subtract).then_inc(rt_v, 1)
            dve.wait_ge(rt_a, 1)
            nc.vector.tensor_reduce(rsum[:], rexp[:], AX_X, ALU.add).then_inc(rt_v, 1)
            dve.wait_ge(rt_v, 3)
            nc.vector.reciprocal(rrec[:], rsum[:]).then_inc(rt_v, 1)
            dve.wait_ge(rt_v, 4)
            nc.vector.tensor_tensor(score[:], rexp[:], over(rrec[:]), ALU.mult).then_inc(rt_v, 1)
            for k, sc in ((0, score), (1, score2)):
                at = 5 + 7 * k
                dve.wait_ge(rt_v, at)
                nc.vector.tensor_reduce(best[:, k], sc[:], AX_X, ALU.max).then_inc(rt_v, 1)
                dve.wait_ge(rt_v, at + 1)
                nc.vector.tensor_tensor(req[:], sc[:], over(best[:, k]), ALU.is_equal).then_inc(rt_v, 1)
                dve.wait_ge(rt_v, at + 2)
                nc.vector.tensor_tensor(rkey[:], req[:], rank[:], ALU.mult).then_inc(rt_v, 1)
                dve.wait_ge(rt_v, at + 3)
                nc.vector.tensor_reduce(kmax[:, k], rkey[:], AX_X, ALU.max).then_inc(rt_v, 1)
                dve.wait_ge(rt_v, at + 4)
                nc.vector.tensor_tensor(chosen[:], rank[:], over(kmax[:, k]), ALU.is_equal).then_inc(rt_v, 1)
                dve.wait_ge(rt_v, at + 5)
                nc.vector.tensor_copy(onehot[:, :, k].rearrange("p e b -> p b e"), chosen[:]).then_inc(rt_v, 1)
                if k == 0:
                    nc.vector.scalar_tensor_tensor(out=score2[:], in0=chosen[:], scalar=-2.0, in1=score[:],
                                                   op0=ALU.mult, op1=ALU.add).then_inc(rt_v, 1)
            nc.vector.tensor_tensor(gsum[:], best[:, 0], best[:, 1], ALU.add).then_inc(rt_v, 1)
            dve.wait_ge(rt_v, 19)
            nc.vector.tensor_scalar(gclip[:], gsum[:], GATE_EPS, None, ALU.max).then_inc(rt_v, 1)
            dve.wait_ge(rt_v, 20)
            nc.vector.reciprocal(grec[:], gclip[:]).then_inc(rt_v, 1)
            dve.wait_ge(rt_v, 21)
            nc.vector.tensor_tensor(gval[:], best[:], grec[:].unsqueeze(1).broadcast_to([P, TOP, B]), ALU.mult).then_inc(rt_v, 1)
            dve.wait_ge(rt_v, 22)
            nc.vector.tensor_scalar(gw_t[:], gval[:].rearrange("p k b -> p (k b)"), tanh_g[:, 1:2], None, ALU.mult).then_inc(rt_v, 1)
            dve.wait_ge(count_ps, 1)
            nc.vector.tensor_tensor_scan(before[:], reset[:].rearrange("p e k -> p (e k)"), ps[:, 0, :], 0.0,
                                         ALU.mult, ALU.add).then_inc(rt_v, 1)
            dve.wait_ge(rt_v, 24)
            nc.vector.scalar_tensor_tensor(out=loc0[:], in0=before[:], scalar=-1.0, in1=ps[:, 0, :],
                                           op0=ALU.add, op1=ALU.subtract).then_inc(rt_v, 1)
            dve.wait_ge(rt_v, 25)
            dve.wait_ge(count_ps, 2)
            nc.vector.tensor_tensor(loc[:].rearrange("p e k -> p (e k)"), loc0[:], ps[:, 1, :], ALU.add).then_inc(rt_v, 1)
            dve.wait_ge(rt_v, 26)
            nc.vector.tensor_tensor(locsel[:], loc[:], onehot[:].rearrange("p e k b -> p e (k b)"), ALU.mult).then_inc(rt_v, 1)
            dve.wait_ge(rt_v, 27)
            nc.vector.tensor_reduce(pos[:], locsel[:].rearrange("p e k -> p k e"), AX_X, ALU.add).then_inc(rt_v, 1)
            dve.wait_ge(rt_v, 28)
            nc.vector.tensor_copy(pos_i[:], pos[:]).then_inc(rt_v, 1)
            dve.wait_ge(rt_v, 29)
            shift = SLOT_TILES.bit_length() - 1
            nc.vector.tensor_scalar(row_i[:], pos_i[:], shift, None, ALU.arith_shift_right)
            nc.vector.tensor_scalar(col_i[:], pos_i[:], SLOT_TILES - 1, None, ALU.bitwise_and).then_inc(rt_v, 1)
            dve.wait_ge(rt_v, 30)
            nc.vector.tensor_copy(row_f[:], row_i[:])
            nc.vector.tensor_copy(col_f[:], col_i[:])
            nc.vector.tensor_scalar(col_b[:], kmax[:].rearrange("p k b -> p (k b)"), -float(SLOT_TILES), float(E * SLOT_TILES),
                                    ALU.mult, ALU.add).then_inc(rt_v, 1)
            dve.wait_ge(rt_v, 31)
            nc.vector.tensor_tensor(col_s[:], col_f[:], col_b[:], ALU.add).then_inc(rt_v, 1)
            dve.wait_ge(rt_v, 32)
            Q = KT // 4
            W = E * SLOT_TILES
            tok = token1[:].rearrange("p k b -> p (k b)")
            for q in range(4):
                ks = slice(q * Q, (q + 1) * Q)
                nc.vector.tensor_tensor(colhot[:, ks], iota_f[:, 0:W].unsqueeze(1).broadcast_to([P, Q, W]),
                                        col_s[:, ks].unsqueeze(2).broadcast_to([P, Q, W]), ALU.is_equal).then_inc(rt_v, 1)
                nc.vector.tensor_tensor(rowhot[:, ks], iota_f[:].unsqueeze(1).broadcast_to([P, Q, P]),
                                        row_f[:, ks].unsqueeze(2).broadcast_to([P, Q, P]), ALU.is_equal).then_inc(rh_done, 1)
                dve.wait_ge(rt_v, 33 + q)
                nc.vector.tensor_tensor(colval[:, ks, 0:W], colhot[:, ks],
                                        tok[:, ks].unsqueeze(2).broadcast_to([P, Q, W]), ALU.mult).then_inc(cv_id, 1)
            dve.wait_ge(slot_ps, 1)
            nc.vector.tensor_copy(slot_w[:], ps[:, 2, W:2 * W]).then_inc(slots_done, 1)
            nc.vector.tensor_copy(slot_t[:], ps[:, 2, 0:W]).then_inc(rt_v, 1)
            dve.wait_ge(rt_v, 37)
            nc.vector.tensor_scalar(gather_idx[:], slot_t[:], -1.0, 0.0, ALU.add, ALU.max).then_inc(slots_done, 1)
            nc.vector.tensor_scalar(empty[:], slot_t[:], 0.0, None, ALU.is_equal).then_inc(rt_v, 1)
            dve.wait_ge(rt_v, 38)
            nc.vector.tensor_tensor(dumped[:], empty[:], dump[:], ALU.mult).then_inc(rt_v, 1)
            dve.wait_ge(rt_v, 39)
            nc.vector.scalar_tensor_tensor(out=scatter_idx[:], in0=slot_t[:], scalar=-1.0, in1=dumped[:],
                                           op0=ALU.add, op1=ALU.add).then_inc(slots_done, 1)

            def split_w(e, k):
                dve.wait_ge(w1h_done, e + 1)
                nc.vector.tensor_tensor(w1l[:, k], w_raw1[:], w1h[:, k].bitcast(F32), ALU.subtract).then_inc(w1l_done, 1)
                dve.wait_ge(w2h_done, e + 1)
                nc.vector.tensor_tensor(w2l[:, k], w_raw2[:], w2h[:, k].bitcast(F32), ALU.subtract).then_inc(w2l_done, 1)

            def rest_x(u, k):
                for c in range(DC):
                    dve.wait_ge(xh_done, DC * u + c + 1)
                    nc.vector.tensor_tensor(xl[:, k, c], ps[:, c, :], xh[:, k, c].bitcast(F32), ALU.subtract).then_inc(xl_done, 1)

            def split_h(u, k, par):
                if not isinstance(u, int) or u >= 2:
                    dve.wait_ge(y_ps, 2 * (u - 1))
                for m in range(HC):
                    slot = (HC * par + m) % 3
                    dve.wait_ge(gelu_done, HC * u + m + 1)
                    nc.vector.tensor_copy(hh[:, k, m], hf[:, slot]).then_inc(hh_done, 1)
                    dve.wait_ge(hh_done, HC * u + m + 1)
                    nc.vector.tensor_tensor(hl[:, k, m], hf[:, slot], hh[:, k, m].bitcast(F32), ALU.subtract).then_inc(hl_done, 1)

            def bias_y(u, k):
                b2_e = b2_all[:, bass.ds(u // 2, 1)] if isinstance(u, int) else None
                for j in range(UT // 2):
                    dve.wait_ge(y_ps, 2 * u + j + 1)
                    if not isinstance(u, int) or u >= 2:
                        dve.wait_ge(yw_done, UT * (u - 1))
                    nc.vector.tensor_tensor(y_b[:, k, 2 * j:2 * j + 2], ps[:, 5 + j, :].rearrange("p (a d) -> p a d", d=D),
                                            b2_e.broadcast_to([P, 2, D]), ALU.add).then_inc(yb_done, 1)

            for s in range(UNITS + 2):
                if s < UNITS and s % 2 == 0:
                    split_w(s // 2, (s // 2) % 2)
                if s < UNITS:
                    rest_x(s, s % 2)
                if 1 <= s <= UNITS:
                    split_h(s - 1, (s - 1) % 2, (s - 1) % 3)
                if s >= 2:
                    bias_y(s - 2, s % 2)


_INS = ['x', 'ctx_1024', 'g_xattn', 'g_ffn', 'L0_xattn_igate_w', 'L0_xattn_igate_b', 'L0_xattn_fgate_w',
        'L0_xattn_fgate_b', 'L0_xattn_ln_scale', 'L0_ffn_wg', 'L0_ffn_w1', 'L0_ffn_b1', 'L0_ffn_w2', 'L0_ffn_b2']
_OUTS = [((32, 128, 256), 'float32')]


def kernel(**inputs):
    import numpy as _np
    import concourse.bacc as _bacc
    from concourse import mybir as _mybir
    from concourse.bass_utils import run_bass_kernel_spmd as _run

    nc = _bacc.Bacc("TRN2", target_bir_lowering=False, num_devices=1)
    arrays, args = {}, []
    for name in _INS:
        a = _np.ascontiguousarray(inputs[name])
        arrays[f"in_{name}_dram"] = a
        args.append(nc.dram_tensor(f"in_{name}_dram", a.shape, _mybir.dt.from_np(a.dtype), kind="ExternalInput").ap())
    for i, (shape, dtype) in enumerate(_OUTS):
        dt = _mybir.dt.from_np(_np.dtype(dtype))
        args.append(nc.dram_tensor(f"out_{i}_dram", shape, dt, kind="ExternalOutput").ap())
    flamingo_block(nc, *args)
    r = _run(nc, [arrays], core_ids=[0])
    got = tuple(r.results[0][f"out_{i}_dram"] for i in range(len(_OUTS)))
    return got[0]
```

```python
from contextlib import ExitStack

import concourse.bass as bass
from concourse import mybir

F32 = mybir.dt.float32
F32R = mybir.dt.float32r
BF16 = mybir.dt.bfloat16
I32 = mybir.dt.int32
U32 = mybir.dt.uint32
ALU = mybir.AluOpType
ACT = mybir.ActivationFunctionType
AX_X = mybir.AxisListType.X

P = 128
LN_EPS = 1e-5
NORM_EPS = 1e-6
GATE_EPS = 1e-9
MASKED = -1.0e30
LOWEST = -3.0e38


def flamingo_block(nc, x, ctx_in, g_xattn, g_ffn, igate_w, igate_b, fgate_w, fgate_b, ln_scale,
                   wg, w1, b1, w2, b2, out):
    B, S, D = x.shape
    HEADS = igate_w.shape[0]
    DH = D // HEADS
    DC = D // P
    E, _, HID = w1.shape
    HC = HID // P
    TOP = 2
    N = B * S
    CAP = -(-TOP * N // E)
    assert out.shape[0] == N + CAP
    assert S == P and HEADS * DH == D and CAP % P == 0 and B % 16 == 0

    GB = 4
    GROUPS = B // GB
    GW = GB * S
    PAIR_TILES = B * HEADS // P
    BT = B // PAIR_TILES
    PARTS = 3
    KA = PARTS * HEADS
    VW = DH + 1
    VWIN = 3 * VW
    LPAD = 96
    SLOT_TILES = CAP // P
    W = E * SLOT_TILES
    KT = TOP * B
    UNITS = 2 * E
    UT = SLOT_TILES // 2
    UW = UT * P

    gates_dram = nc.dram_tensor("gates_scratch", [2 * HEADS, N], F32, kind="Internal").ap()
    a_dram = nc.dram_tensor("a_scratch", [B, HEADS, PARTS, S], BF16, kind="Internal").ap()
    m_dram = nc.dram_tensor("m_scratch", [PARTS, B, HEADS, S], BF16, kind="Internal").ap()
    xn_dram = nc.dram_tensor("xn_scratch", [N, D + E], F32, kind="Internal").ap()

    x_rows = x.rearrange("b s d -> (b s) d")
    ctx_rows = ctx_in.rearrange("b s d -> (b s) d")

    with ExitStack() as keep:
        def sb(name, shape, dt=F32, stack=keep):
            return stack.enter_context(nc.sbuf_tensor(name, shape, dt))

        def sem(name):
            return keep.enter_context(nc.semaphore(name))

        ident = sb("ident", [P, P])
        ident_bf = sb("ident_bf", [P, P], BF16)
        ones_bf = sb("ones_bf", [P, P], BF16)
        later_bf = sb("later_bf", [P, P], BF16)
        w_raw1 = sb("w_raw1", [P, DC, HID])
        w_raw2 = sb("w_raw2", [P, HC, D])
        b1_rows = sb("b1_rows", [E * HC, P])
        b1_cols = sb("b1_cols", [P, E * HC])
        b2_all = sb("b2_all", [P, E, D])
        gx = sb("gx", [P, 2])
        tanh_g = sb("tanh_g", [P, 2])
        logits = sb("logits", [P, B, E])
        gather_idx = sb("gather_idx", [P, E * SLOT_TILES], U32)
        scatter_idx = sb("scatter_idx", [P, E * SLOT_TILES], U32)

        att = ExitStack()
        rank = sb("rank", [P, B, E], stack=att)
        reset = sb("reset", [P, E, B], stack=att)
        iota_i = sb("iota_i", [P, P], I32, stack=att)
        iota_bf = sb("iota_bf", [P, P], BF16, stack=att)
        tile_i = sb("tile_i", [P, TOP, B], I32, stack=att)
        tile1 = sb("tile1", [P, KT], BF16, stack=att)
        part_i = sb("part_i", [P, 1], I32, stack=att)
        part_f = sb("part_f", [P, 1], stack=att)
        dump_i = sb("dump_i", [P, E, SLOT_TILES], I32, stack=att)
        dump = sb("dump", [P, W], stack=att)
        qT = sb("qT", [P, DC, N], stack=att)
        kT = sb("kT", [P, DC, N], stack=att)
        cell = ExitStack()
        q_rows = sb("q_rows", [P, 2, GB, D], stack=cell)
        g_stats = sb("g_stats", [P, GB, 6], stack=cell)
        g_mv = sb("g_mv", [P, 2, GB, 2], stack=cell)
        g_var = sb("g_var", [P, GB], stack=cell)
        g_rstd = sb("g_rstd", [P, 2, GB], stack=cell)
        gate_rows = sb("gate_rows", [2 * HEADS, 3 * D], stack=cell)
        gate_wT = sb("gate_wT", [P, 3 * DC, 2 * HEADS], stack=cell)
        gate_wk = sb("gate_wk", [P, DC, 2 * HEADS], stack=cell)
        gate_b = sb("gate_b", [2 * HEADS, 1], stack=cell)
        gates_sb = sb("gates_sb", [2 * HEADS, 2, GW], stack=cell)
        neg_half = sb("neg_half", [P, GB], stack=cell)
        PW = PAIR_TILES * S
        ig_p = sb("ig_p", [P, PAIR_TILES, S], stack=cell)
        fg_p = sb("fg_p", [P, PAIR_TILES, S], stack=cell)
        fa = sb("fa", [P, PW], stack=cell)
        fe = sb("fe", [P, PW], stack=cell)
        fl = sb("fl", [P, PW], stack=cell)
        logf = sb("logf", [P, PW], stack=cell)
        cs = sb("cs", [P, PW], stack=cell)
        av = sb("av", [P, PW], stack=cell)
        mv = sb("mv", [P, PW], stack=cell)
        msum = sb("msum", [P, PW], stack=cell)
        nm = sb("nm", [P, PW], stack=cell)
        res1 = sb("res1", [P, 2, PW], stack=cell)
        negm = sb("negm", [P, PW], stack=cell)
        parts = sb("parts", [P, 2, PARTS, PW], BF16, stack=cell)
        ones_row = sb("ones_row", [P, S], stack=cell)
        zero_row = sb("zero_row", [P, S], stack=cell)
        nmT = sb("nmT", [P, B * HEADS], stack=cell)
        mask_bf = sb("mask_bf", [P, 4, S], BF16, stack=cell)
        z_lhs = sb("z_lhs", [P, 4, S], BF16, stack=cell)
        z_rhs = sb("z_rhs", [P, 4, HEADS * S], BF16, stack=cell)
        k_st = sb("k_st", [P, 2, DC, 2, S], stack=cell)
        q_st = sb("q_st", [P, 2, DC, 2, S], stack=cell)
        zero_rows = sb("zero_rows", [P, CAP * D // P], stack=cell)
        v_ext = sb("v_ext", [P, 2, (HEADS + 2) * VW], stack=cell)
        decay = sb("decay", [P, 2, HEADS * S], stack=cell)
        cT = sb("cT", [P, 2, HEADS * S], stack=cell)
        den = sb("den", [P, 2, HEADS], stack=cell)
        den2 = sb("den2", [P, 2, HEADS], stack=cell)
        rden = sb("rden", [P, 2, HEADS], stack=cell)
        hn = sb("hn", [P, 2, HEADS, DH], stack=cell)
        h_st = sb("h_st", [P, 2, 6], stack=cell)
        h_mv = sb("h_mv", [P, 2, 2], stack=cell)
        h_var = sb("h_var", [P, 1], stack=cell)
        h_rstd = sb("h_rstd", [P, 2, 1], stack=cell)
        h_sc = sb("h_sc", [P, 2, D], stack=cell)
        ls = sb("ls", [P, D], stack=cell)
        ls_t = sb("ls_t", [P, D], stack=cell)
        x_st = sb("x_st", [P, 6], stack=cell)
        x_mv = sb("x_mv", [P, 2, 2], stack=cell)
        x_var = sb("x_var", [P, 1], stack=cell)
        x_rstd = sb("x_rstd", [P, 2, 1], stack=cell)
        x_bias = sb("x_bias", [P, 2, 1], stack=cell)
        xnT = sb("xnT", [P, DC, S], stack=cell)
        wg_sb = sb("wg_sb", [P, DC, E], stack=cell)
        wg_pad = sb("wg_pad", [P, DC, LPAD // E, E], stack=cell)
        gates_only = ExitStack()
        x_in = sb("x_in", [P, 2, GB, D], stack=gates_only)
        c_in = sb("c_in", [P, 2, GB, D], stack=gates_only)
        gates_only.close()
        x_c = sb("x_c", [P, 4, D], stack=cell)
        c_c = sb("c_c", [P, 4, D], stack=cell)
        x1 = sb("x1", [P, 4, D], stack=cell)
        xn = sb("xn", [P, 4, D], stack=cell)
        cell.close()
        route = ExitStack()

        def rt(name, shape, dt=F32):
            return sb(name, shape, dt, stack=route)

        rmax = rt("rmax", [P, B])
        rz = rt("rz", [P, B, E])
        rexp = rt("rexp", [P, B, E])
        rsum = rt("rsum", [P, B])
        rrec = rt("rrec", [P, B])
        score = rt("score", [P, B, E])
        best = rt("best", [P, TOP, B])
        req = rt("req", [P, B, E])
        rkey = rt("rkey", [P, TOP, B, E])
        kmax = rt("kmax", [P, TOP, B])
        chosen = rt("chosen", [P, TOP, B, E])
        onehot = rt("onehot", [P, TOP, E, B], BF16)
        probs = rt("probs", [P, TOP, B])
        gsum = rt("gsum", [P, B])
        gclip = rt("gclip", [P, B])
        grec = rt("grec", [P, B])
        gval = rt("gval", [P, TOP, B])
        gw_t = rt("gw_t", [P, TOP, B])
        gw_e = rt("gw_e", [P, TOP, B, E])
        gw_all = rt("gw_all", [P, B, E])
        before = rt("before", [P, TOP, E, B])
        after = rt("after", [P, E, B])
        loc = rt("loc", [P, TOP, E, B])
        locsel = rt("locsel", [P, TOP, E, B])
        pos_i = rt("pos_i", [P, KT], I32)
        row_i = rt("row_i", [P, KT], I32)
        col_i = rt("col_i", [P, KT], I32)
        col_b = rt("col_b", [P, KT])
        col_s = rt("col_s", [P, KT])
        QK = KT // 4
        iota_rep = rt("iota_rep", [P, QK, P], BF16)
        row_rep = rt("row_rep", [P, 4, QK, P], BF16)
        rowhot = rt("rowhot", [P, KT, P], BF16)
        colhot = rt("colhot", [P, KT, W], BF16)
        colval = rt("colval", [P, KT, 2, W], BF16)
        slot_n = rt("slot_n", [P, 2, W])
        slot_t = rt("slot_t", [P, W])
        empty = rt("empty", [P, W])
        dumped = rt("dumped", [P, W])
        route.close()
        att.close()
        w1h = sb("w1h", [P, 2, DC, HID], F32R)
        w1l = sb("w1l", [P, 2, DC, HID], F32R)
        w2h = sb("w2h", [P, 2, HC, D], F32R)
        w2l = sb("w2l", [P, 2, HC, D], F32R)
        xg = sb("xg", [P, 2, UT, D + E])
        w_u = sb("w_u", [P, 4, UT])
        g_ix = sb("g_ix", [P, 2, UT], U32)
        s_ix = sb("s_ix", [P, 2, UT], U32)
        xh = sb("xh", [P, 2, DC, UW], F32R)
        xl = sb("xl", [P, 2, DC, UW], F32R)
        hf = sb("hf", [P, 3, UW])
        hh = sb("hh", [P, 2, HC, UW], F32R)
        hl = sb("hl", [P, 2, HC, UW], F32R)
        y_b = sb("y_b", [P, 2, UT, D])
        y_w = sb("y_w", [P, 2, UT, D])

        ps = keep.enter_context(nc.psum_tensor("ps", [P, 8, 512], F32))

        waited = sem("waited")
        const_ready = sem("const_ready")
        gw_ld = sem("gw_ld")
        misc_ld = sem("misc_ld")
        w_ld = sem("w_ld")
        x_ld = [sem("x_ld0"), sem("x_ld1")]
        c_ld = [sem("c_ld0"), sem("c_ld1")]
        wT_done = sem("wT_done")
        wT_copied = sem("wT_copied")
        wk_ready = sem("wk_ready")
        stats_done = sem("stats_done")
        g_seq = sem("g_seq")
        rstd_seq = sem("rstd_seq")
        rstd_done = sem("rstd_done")
        q_done = sem("q_done")
        kT_ps = sem("kT_ps")
        qT_ps = sem("qT_ps")
        kT_done = sem("kT_done")
        qT_done = sem("qT_done")
        gate_ps = sem("gate_ps")
        gate_done = sem("gate_done")
        gate_st = [sem("gate_st0"), sem("gate_st1")]
        pair_ld = [sem("pair_ld0"), sem("pair_ld1")]
        sc_v = [sem("sc_v0"), sem("sc_v1")]
        sc_a = [sem("sc_a0"), sem("sc_a1")]
        nmT_ps = sem("nmT_ps")
        nmT_done = sem("nmT_done")
        part_st = [sem("part_st0"), sem("part_st1")]
        tg_done = sem("tg_done")
        const_v = sem("const_v")
        pe_ld = [sem("pe_ld0"), sem("pe_ld1")]
        cc_ld = [sem("cc_ld0"), sem("cc_ld1")]
        xc_ld = [sem("xc_ld0"), sem("xc_ld1")]
        v_ready = sem("v_ready")
        z_ps = sem("z_ps")
        s_ps = sem("s_ps")
        exp_done = sem("exp_done")
        cT_done = sem("cT_done")
        h_ps = sem("h_ps")
        p1_seq = sem("p1_seq")
        hn_done = sem("hn_done")
        h_stat = sem("h_stat")
        h_pool = sem("h_pool")
        h_rs = sem("h_rs")
        hsc_done = sem("hsc_done")
        x1_done = sem("x1_done")
        x1_seq = sem("x1_seq")
        x_stat = sem("x_stat")
        x_pool = sem("x_pool")
        x_rs = sem("x_rs")
        xn_done = sem("xn_done")
        xnT_ps = sem("xnT_ps")
        xnT_done = sem("xnT_done")
        lg_ps = sem("lg_ps")
        lg_done = sem("lg_done")
        x1_st = [sem("x1_st0"), sem("x1_st1")]
        xn_st = [sem("xn_st0"), sem("xn_st1")]
        dump_st = sem("dump_st")
        top_v = sem("top_v")
        gw_v = sem("gw_v")
        gw_p = sem("gw_p")
        pos_v = [sem("pos_v0"), sem("pos_v1")]
        oh_done = sem("oh_done")
        hot_v = sem("hot_v")
        row_done = sem("row_done")
        rep_done = sem("rep_done")
        gw_st = sem("gw_st")
        wu_done = sem("wu_done")
        rt_v = sem("rt_v")
        rt_a = sem("rt_a")
        rt_p = sem("rt_p")
        rt_c = sem("rt_c")
        count_ps = sem("count_ps")
        cv_id = sem("cv_id")
        cv_w = sem("cv_w")
        rh_done = sem("rh_done")
        slot_ps = sem("slot_ps")
        slots_done = sem("slots_done")
        w1h_done = sem("w1h_done")
        w1l_done = sem("w1l_done")
        w2h_done = sem("w2h_done")
        w2l_done = sem("w2l_done")
        ix_done = sem("ix_done")
        xg_ld = [sem("xg_ld0"), sem("xg_ld1")]
        xT_ps = sem("xT_ps")
        xh_done = sem("xh_done")
        xl_done = sem("xl_done")
        g1_ps = sem("g1_ps")
        gelu_done = sem("gelu_done")
        hh_done = sem("hh_done")
        hl_done = sem("hl_done")
        y_ps = sem("y_ps")
        yb_done = sem("yb_done")
        yw_done = sem("yw_done")
        six_done = sem("six_done")
        y_st = sem("y_st")

        MISC = 6
        A_SPLIT, M_SPLIT = 14, 15
        CONSTS = 10
        NJ = 4
        LOADS = 16 * 4
        LAST_LAG = 5

        def later(step, n):
            return not isinstance(step, int) or step >= n

        def last_use(m):
            return 3 if m >= 3 else m + HC - max(n for n in range(HC) if n % 3 == m)

        def place(h):
            return h % NJ * DC + h // NJ

        def live(step, n):
            return not isinstance(step, int) or 0 <= step < n

        block = keep.enter_context(nc.Block())

        @block.sync
        def _(sp):
            def load_group(g, k):
                if later(g, 2):
                    sp.wait_ge(kT_ps, 2 * (g - 1))
                    sp.sem_inc(waited, 1)
                sp.dma_start(c_in[:, k], ctx_rows[bass.ds(g * GW, GW)].rearrange("(b p) d -> p b d", p=P)).then_inc(c_ld[k], 16)
                if later(g, 2):
                    sp.wait_ge(q_done, 4 * (g - 1))
                    sp.sem_inc(waited, 1)
                sp.dma_start(x_in[:, k], x_rows[bass.ds(g * GW, GW)].rearrange("(b p) d -> p b d", p=P)).then_inc(x_ld[k], 16)

            load_group(0, 0)
            sp.dma_start(gate_rows[0:HEADS, :], igate_w).then_inc(gw_ld, 16)
            sp.dma_start(gate_rows[HEADS:2 * HEADS, :], fgate_w).then_inc(gw_ld, 16)
            sp.dma_start(b1_rows[:], b1.rearrange("e (m p) -> (e m) p", p=P)).then_inc(gw_ld, 16)
            load_group(1, 1)
            sp.dma_start(gate_b[0:HEADS, :], igate_b.rearrange("(h a) -> h a", a=1)).then_inc(misc_ld, 16)
            sp.dma_start(gate_b[HEADS:2 * HEADS, :], fgate_b.rearrange("(h a) -> h a", a=1)).then_inc(misc_ld, 16)
            sp.dma_start(ls[:], ln_scale.rearrange("(a d) -> a d", a=1).broadcast_to([P, D])).then_inc(misc_ld, 16)
            sp.dma_start(gx[:, 0:1], g_xattn.rearrange("(a d) -> a d", a=1).broadcast_to([P, 1])).then_inc(misc_ld, 16)
            sp.dma_start(gx[:, 1:2], g_ffn.rearrange("(a d) -> a d", a=1).broadcast_to([P, 1])).then_inc(misc_ld, 16)
            sp.dma_start(wg_sb[:], wg.rearrange("(c p) e -> p c e", p=P)).then_inc(misc_ld, 16)

            load_group(2, 0)
            load_group(3, 1)
            for g in range(4, GROUPS):
                load_group(g, g % 2)
                if g == 5:
                    sp.wait_ge(const_v, 2)
                    sp.dma_start(out[N:N + CAP].rearrange("(p j) d -> p (j d)", p=P),
                                 zero_rows[:]).then_inc(dump_st, 16)

            pairs = gates_dram.rearrange("h (b s) -> b h s", s=S)

            def load_gates(t):
                for k in range(2):
                    sp.wait_ge(gate_st[k], 16 * (t + 1) * GROUPS // (2 * PAIR_TILES))
                sp.dma_start(fg_p[:, t], pairs[t * BT:(t + 1) * BT, HEADS:2 * HEADS]).then_inc(pair_ld[t], 16)
                sp.dma_start(ig_p[:, t], pairs[t * BT:(t + 1) * BT, 0:HEADS]).then_inc(pair_ld[t], 16)

            def store_parts(t):
                ts = slice(t * S, (t + 1) * S)
                sp.wait_ge(sc_v[t], A_SPLIT)
                sp.dma_start(a_dram[t * BT:(t + 1) * BT].rearrange("b h j s -> (b h) j s"), parts[:, 0, :, ts]).then_inc(part_st[t], 16)
                sp.wait_ge(sc_v[t], M_SPLIT)
                sp.dma_start(m_dram[:, t * BT:(t + 1) * BT].rearrange("j b h s -> (b h) j s"), parts[:, 1, :, ts]).then_inc(part_st[t], 16)

            def load_qk(i, r):
                pair, t = 2 * i + r, r % 2
                if later(pair, 2):
                    sp.wait_ge(s_ps, 2 * pair - 2)
                two = bass.ds(2 * pair * S, 2 * S)
                sp.dma_start(k_st[:, t], kT[:, :, two].rearrange("p c (b s) -> p c b s", s=S)).then_inc(pe_ld[t], 16)
                sp.dma_start(q_st[:, t], qT[:, :, two].rearrange("p c (b s) -> p c b s", s=S)).then_inc(pe_ld[t], 16)

            def load_z(i, r):
                pair, t = 2 * i + r, r % 2
                slots = slice(2 * t, 2 * t + 2)
                sp.dma_start(z_lhs[PARTS:PARTS + KA, slots],
                             a_dram[bass.ds(2 * pair, 2)].rearrange("b h j s -> (h j) b s")).then_inc(pe_ld[t], 16)
                sp.dma_start(z_rhs[0:PARTS, slots],
                             m_dram[:, bass.ds(2 * pair, 2)].rearrange("j b h s -> j b (h s)")).then_inc(pe_ld[t], 16)

            def pair_rows(rows, pair):
                return rows[bass.ds(2 * pair * S, 2 * S)].rearrange("(b p) d -> p b d", p=P)

            def load_c(i, r):
                pair, t = 2 * i + r, r % 2
                if later(pair, 2):
                    sp.wait_ge(v_ready, 2 * pair - 2)
                sp.dma_start(c_c[:, 2 * t:2 * t + 2], pair_rows(ctx_rows, pair)).then_inc(cc_ld[t], 16)

            def load_x(i, r):
                pair, t = 2 * i + r, r % 2
                if later(pair, 2):
                    sp.wait_ge(x1_done, 2 * pair - 2)
                sp.dma_start(x_c[:, 2 * t:2 * t + 2], pair_rows(x_rows, pair)).then_inc(xc_ld[t], 16)

            def store_rows(i, r):
                pair, t = 2 * i + r, r % 2
                sp.wait_ge(x1_done, 2 * pair + 2)
                sp.dma_start(pair_rows(out, pair), x1[:, 2 * t:2 * t + 2]).then_inc(x1_st[t], 16)
                sp.wait_ge(xn_done, 2 * pair + 2)
                sp.dma_start(pair_rows(xn_dram, pair)[:, :, 0:D], xn[:, 2 * t:2 * t + 2]).then_inc(xn_st[t], 16)

            load_gates(0)
            sp.wait_ge(dump_st, 16)
            sp.wait_ge(qT_done, 1)
            sp.wait_ge(kT_done, DC)
            load_qk(0, 0)
            load_qk(0, 1)
            sp.wait_ge(const_ready, CONSTS)
            store_parts(0)
            sp.wait_ge(q_done, GB * GROUPS)
            sp.wait_ge(kT_ps, DC * GROUPS)
            load_c(0, 0)
            load_c(0, 1)
            load_x(0, 0)
            sp.wait_ge(part_st[0], 16 * 2)
            load_z(0, 0)
            load_z(0, 1)
            sp.wait_ge(qT_done, GROUPS)
            sp.wait_ge(kT_done, DC * GROUPS)
            load_gates(1)

            def pair_step(i, r):
                for stage, lag in ((load_qk, 0), (load_z, 0), (load_c, 0), (load_x, 1), (store_rows, 3)):
                    if live(2 * i + r - lag, B // 2):
                        stage(i, r - lag)

            pair_step(0, 2)
            sp.dma_start(b2_all[:], b2.rearrange("(a e) d -> a e d", a=1).broadcast_to([P, E, D])).then_inc(w_ld, 16)
            pair_step(0, 3)
            store_parts(1)
            sp.wait_ge(part_st[1], 16 * 2)
            with sp.Fori(2, B // 4) as i:
                for r in range(2):
                    pair_step(i, r)
            pair_step(0, B // 2)
            sp.dma_start(w_raw1[:], w1[0].rearrange("(c p) h -> p c h", p=P)).then_inc(w_ld, 16)
            pair_step(0, B // 2 + 1)
            pair_step(0, B // 2 + 2)
            sp.dma_start(w_raw2[:], w2[0].rearrange("(k p) d -> p k d", p=P)).then_inc(w_ld, 16)

            sp.wait_ge(gw_p, 4)
            sp.dma_start(xn_dram[:, D:D + E].rearrange("(b p) e -> p b e", p=P), gw_all[:]).then_inc(gw_st, 16)

            with sp.Fori(1, E) as e:
                sp.wait_ge(xT_ps, 2 * DC * e)
                sp.wait_ge(w1h_done, e)
                sp.wait_ge(w1l_done, e)
                sp.dma_start(w_raw1[:], w1[bass.ds(e, 1)].rearrange("e (c p) h -> p (e c) h", p=P)).then_inc(w_ld, 16)
                sp.wait_ge(w2h_done, e)
                sp.wait_ge(w2l_done, e)
                sp.dma_start(w_raw2[:], w2[bass.ds(e, 1)].rearrange("e (k p) d -> p (e k) d", p=P)).then_inc(w_ld, 16)

            sp.wait_ge(y_st, 16 * E * SLOT_TILES)

        @block.gpsimd
        def _(pool):
            nc.gpsimd.memset(ident[:], 0.0).then_inc(rt_c, 1)
            nc.gpsimd.memset(later_bf[:], 0.0).then_inc(rt_c, 1)
            pool.wait_ge(rt_c, 2)
            nc.gpsimd.affine_select(out=ident[:], in_=ident[:], compare_op=ALU.not_equal, fill=1.0, base=0,
                                    pattern=[[-1, P]], channel_multiplier=1).then_inc(const_ready, 1)
            nc.gpsimd.memset(neg_half[:], -0.5).then_inc(const_ready, 1)

            def group_rstd(g, k):
                pool.wait_ge(stats_done, g + 1)
                if later(g, 1):
                    pool.wait_ge(rstd_done, g)
                if later(g, 2):
                    pool.wait_ge(q_done, GB * (g - 1))
                pool.sem_inc(waited, 1)
                nc.gpsimd.tensor_scalar(g_var[:], g_mv[:, k, :, 1], LN_EPS, None, ALU.add).then_inc(rstd_seq, 1)
                pool.wait_ge(rstd_seq, g + 1)
                nc.gpsimd.tensor_tensor(g_rstd[:, k], g_var[:], neg_half[:], ALU.pow).then_inc(rstd_done, 1)

            group_rstd(0, 0)
            nc.gpsimd.memset(z_rhs[:, 0], 0.0).then_inc(rt_c, 1)
            nc.gpsimd.memset(mask_bf[:], 0.0).then_inc(rt_c, 1)
            nc.gpsimd.memset(z_lhs[:], 0.0).then_inc(rt_c, 1)
            nc.gpsimd.memset(v_ext[:], 1.0).then_inc(const_ready, 1)
            pool.wait_ge(const_ready, 2)
            nc.gpsimd.tensor_copy(ident_bf[:], ident[:]).then_inc(const_ready, 1)
            group_rstd(1, 1)
            nc.gpsimd.affine_select(out=later_bf[:], in_=later_bf[:], compare_op=ALU.is_ge, fill=-1.0, base=0,
                                    pattern=[[1, P]], channel_multiplier=-1).then_inc(const_ready, 1)
            pool.wait_ge(rt_c, 5)
            nc.gpsimd.affine_select(out=mask_bf[:], in_=mask_bf[:], compare_op=ALU.is_ge, fill=MASKED, base=0,
                                    pattern=[[0, 4], [1, S]], channel_multiplier=-1).then_inc(const_ready, 1)
            nc.gpsimd.memset(z_lhs[0:PARTS], 1.0).then_inc(const_ready, 1)
            for g in range(2, 4):
                group_rstd(g, g % 2)
                for j in range(PARTS):
                    if (j < 2) == (g == 2):
                        pool.wait_ge(rt_c, 5 + j)
                        nc.gpsimd.affine_select(out=z_rhs[:, 0].rearrange("p (h s) -> p h s", h=HEADS),
                                                in_=z_rhs[:, 0].rearrange("p (h s) -> p h s", h=HEADS),
                                                compare_op=ALU.not_equal, fill=1.0, base=-(PARTS + j),
                                                pattern=[[-PARTS, HEADS], [0, S]], channel_multiplier=1).then_inc(rt_c, 1)
            with pool.Fori(2, GROUPS // 2) as i:
                for k in range(2):
                    group_rstd(2 * i + k, k)
            nc.gpsimd.iota(iota_i[:], pattern=[[1, P]], base=0, channel_multiplier=0).then_inc(rt_p, 1)
            nc.gpsimd.iota(tile_i[:], pattern=[[0, TOP], [1, B]], base=1, channel_multiplier=0).then_inc(rt_p, 1)
            nc.gpsimd.iota(part_i[:], pattern=[[0, 1]], base=0, channel_multiplier=1).then_inc(rt_p, 1)
            nc.gpsimd.iota(dump_i[:], pattern=[[0, E], [1, SLOT_TILES]], base=N + P, channel_multiplier=SLOT_TILES).then_inc(rt_p, 1)
            for e in range(E):
                nc.gpsimd.memset(rank[:, :, e:e + 1], float(E - e)).then_inc(rt_p, 1)
            nc.gpsimd.memset(reset[:], 1.0).then_inc(rt_p, 1)
            pool.wait_ge(rt_p, 5 + E)
            nc.gpsimd.memset(reset[:, :, 0:1], 0.0).then_inc(rt_p, 1)
            nc.gpsimd.tensor_copy(iota_bf[:], iota_i[:]).then_inc(rt_p, 1)
            nc.gpsimd.tensor_copy(tile1[:], tile_i[:].rearrange("p k b -> p (k b)")).then_inc(rt_p, 1)
            nc.gpsimd.tensor_copy(part_f[:], part_i[:]).then_inc(rt_p, 1)
            nc.gpsimd.tensor_copy(dump[:], dump_i[:].rearrange("p e j -> p (e j)")).then_inc(rt_p, 1)

            def head_rstd(i, r):
                b, k = 4 * i + r, r % 2
                if later(b, 1):
                    pool.wait_ge(h_rs, b)
                if later(b, 2):
                    pool.wait_ge(x1_done, b - 1)
                pool.wait_ge(h_stat, b + 1)
                pool.sem_inc(waited, 1)
                nc.gpsimd.tensor_scalar(h_var[:], h_mv[:, k, 1:2], LN_EPS, None, ALU.add).then_inc(h_pool, 1)
                pool.wait_ge(h_pool, b + 1)
                nc.gpsimd.tensor_tensor(h_rstd[:, k], h_var[:], neg_half[:, 0:1], ALU.pow).then_inc(h_rs, 1)

            def row_rstd(i, r):
                b, k = 4 * i + r, r % 2
                if later(b, 1):
                    pool.wait_ge(x_rs, b)
                if later(b, 2):
                    pool.wait_ge(xn_done, b - 1)
                pool.wait_ge(x_stat, b + 1)
                pool.sem_inc(waited, 1)
                nc.gpsimd.tensor_scalar(x_var[:], x_mv[:, k, 1:2], LN_EPS, None, ALU.add).then_inc(x_pool, 1)
                pool.wait_ge(x_pool, 2 * b + 1)
                nc.gpsimd.tensor_tensor(x_rstd[:, k], x_var[:], neg_half[:, 0:1], ALU.pow).then_inc(x_pool, 1)
                pool.wait_ge(x_pool, 2 * b + 2)
                pool.sem_inc(waited, 1)
                nc.gpsimd.tensor_scalar(x_bias[:, k], x_mv[:, k, 0:1], x_rstd[:, k], -1.0, ALU.mult, ALU.mult).then_inc(x_rs, 1)

            def pool_step(i, r):
                for stage, lag in ((row_rstd, 3), (head_rstd, 2)):
                    if live(4 * i + r - lag, B):
                        stage(i, r - lag)

            for r in range(8):
                pool_step(0, r)
            with pool.Fori(2, B // 4) as i:
                for r in range(4):
                    pool_step(i, r)
            for r in range(B, B + LAST_LAG):
                pool_step(0, r)

            pool.wait_ge(xn_done, B)
            pool.wait_ge(lg_done, B)
            for k in range(2):
                pool.wait_ge(xn_st[k], 16 * (B // 4))
                pool.wait_ge(x1_st[k], 16 * (B // 4))
            nc.gpsimd.tensor_copy(iota_rep[:], iota_bf[:].unsqueeze(1).broadcast_to([P, QK, P])).then_inc(rep_done, 1)
            for q in range(4):
                if q == 2:
                    pool.wait_ge(gw_v, 7)
                    nc.gpsimd.tensor_tensor(gval[:], probs[:], grec[:].unsqueeze(1).broadcast_to([P, TOP, B]), ALU.mult).then_inc(gw_p, 1)
                    pool.wait_ge(gw_p, 1)
                    nc.gpsimd.tensor_scalar(gw_t[:], gval[:], tanh_g[:, 1:2], None, ALU.mult).then_inc(gw_p, 1)
                    pool.wait_ge(gw_p, 2)
                    nc.gpsimd.tensor_tensor(gw_e[:].rearrange("p k b e -> p (k b) e"), chosen[:].rearrange("p k b e -> p (k b) e"),
                                            gw_t[:].rearrange("p k b -> p (k b)").unsqueeze(2).broadcast_to([P, KT, E]),
                                            ALU.mult).then_inc(gw_p, 1)
                    pool.wait_ge(gw_p, 3)
                    nc.gpsimd.tensor_tensor(gw_all[:], gw_e[:, 0], gw_e[:, 1], ALU.add).then_inc(gw_p, 1)
                pool.wait_ge(hot_v, q + 1)
                ks = slice(q * QK, (q + 1) * QK)
                nc.gpsimd.tensor_tensor(colval[:, ks, 0], colhot[:, ks], tile1[:, ks].unsqueeze(2).broadcast_to([P, QK, W]),
                                        ALU.mult).then_inc(cv_id, 1)

            pool.wait_ge(slots_done, 1)
            pool.wait_ge(gw_st, 16)
            for k in range(2):
                pool.wait_ge(xn_st[k], 16 * (B // 4))
            pool.wait_ge(dump_st, 16)

            def gather(u, k):
                if later(u, 2):
                    pool.wait_ge(xT_ps, 2 * (u - 1))
                    pool.wait_ge(wu_done, u - 1)
                    pool.wait_ge(xg_ld[k], 8 * UT * (u - k))
                pool.sem_inc(waited, 1)
                nc.gpsimd.tensor_copy(g_ix[:, k], gather_idx[:, bass.ds(u * UT, UT)]).then_inc(ix_done, 1)
                pool.wait_ge(ix_done, u + 1)
                pool.sem_inc(waited, 1)
                for j in range(UT):
                    nc.gpsimd.indirect_dma_start(xg[:, k, j], None, xn_dram,
                                                 bass.IndirectOffsetOnAxis(ap=g_ix[:, k, j:j + 1], axis=0)).then_inc(xg_ld[k], 16)

            def scatter(u, k):
                if later(u, 1):
                    pool.wait_ge(y_st, 16 * UT * u)
                pool.sem_inc(waited, 1)
                nc.gpsimd.tensor_copy(s_ix[:, k], scatter_idx[:, bass.ds(u * UT, UT)]).then_inc(six_done, 1)
                pool.wait_ge(six_done, u + 1)
                for j in range(UT):
                    pool.wait_ge(yw_done, UT * u + j + 1)
                    pool.sem_inc(waited, 1)
                    nc.gpsimd.indirect_dma_start(out, bass.IndirectOffsetOnAxis(ap=s_ix[:, k, j:j + 1], axis=0),
                                                 y_w[:, k, j], None, compute_op=ALU.add).then_inc(y_st, 16)

            for u in range(4):
                gather(u, u % 2)
                if u == 2:
                    pool.wait_ge(slots_done, 2)
                if u >= 3:
                    scatter(u - 3, (u - 3) % 2)
            with pool.Fori(2, UNITS // 2) as i:
                for k in range(2):
                    gather(2 * i + k, k)
                    scatter(2 * i + k - 3, 1 - k)
            for u in range(UNITS - 3, UNITS):
                scatter(u, u % 2)
            pool.wait_ge(y_st, 16 * E * SLOT_TILES)

        @block.scalar
        def _(act):
            def copy_kT(g):
                for c in range(DC):
                    act.wait_ge(kT_ps, DC * g + c + 1)
                    nc.scalar.copy(kT[:, c, bass.ds(g * GW, GW)], ps[:, c, :]).then_inc(kT_done, 1)

            def copy_gates(g, k):
                act.wait_ge(gate_ps, g + 1)
                if later(g, 2):
                    act.wait_ge(gate_st[k], 8 * (g - k))
                nc.scalar.activation(gates_sb[:, k], ps[0:2 * HEADS, 4, :], ACT.Identity, bias=gate_b[:, 0:1]).then_inc(gate_done, 1)
                act.wait_ge(gate_done, g + 1)
                act.dma_start(gates_dram[:, bass.ds(g * GW, GW)], gates_sb[:, k]).then_inc(gate_st[k], 16)

            def softplus(t):
                ts = slice(t * S, (t + 1) * S)
                act.wait_ge(sc_v[t], 1)
                nc.scalar.activation(fe[:, ts], fa[:, ts], ACT.Exp).then_inc(sc_a[t], 1)
                act.wait_ge(sc_a[t], 1)
                nc.scalar.activation(fl[:, ts], fe[:, ts], ACT.Ln, bias=1.0).then_inc(sc_a[t], 1)

            def exp_max(t):
                ts = slice(t * S, (t + 1) * S)
                act.wait_ge(sc_v[t], 7)
                nc.scalar.activation(nm[:, ts], msum[:, ts], ACT.Exp, scale=-1.0).then_inc(sc_a[t], 1)

            for g in range(GROUPS):
                copy_kT(g)
                if g == 0:
                    act.wait_ge(wT_done, 1)
                    nc.scalar.copy(gate_wT[:], ps[:, 5, 0:3 * DC * 2 * HEADS].rearrange("p (c g) -> p c g", g=2 * HEADS)).then_inc(wT_copied, 1)
                    nc.scalar.copy(b1_cols[:], ps[:, 6, 0:E * HC]).then_inc(wT_copied, 1)
                    act.wait_ge(misc_ld, 16 * MISC)
                    nc.scalar.activation(tanh_g[:], gx[:], ACT.Tanh).then_inc(tg_done, 1)
                if g == GROUPS - 1:
                    softplus(0)
                if g >= 2:
                    copy_gates(g - 2, g % 2)
                if g == 4:
                    act.wait_ge(rt_c, 8)
                    for k in range(1, 4):
                        nc.scalar.copy(z_rhs[:, k], z_rhs[:, 0]).then_inc(const_ready, 1)
            copy_gates(GROUPS - 2, 0)
            exp_max(0)
            copy_gates(GROUPS - 1, 1)

            def decays(i, r):
                b, k = 4 * i + r, r % 2
                if later(b, 2):
                    act.wait_ge(cT_done, b - 1)
                act.wait_ge(z_ps, b + 1)
                nc.scalar.activation(decay[:, k].rearrange("p (j c s) -> p c j s", j=NJ, s=S),
                                     ps[:, 0:2, :].rearrange("p c (j s) -> p c j s", s=S), ACT.Exp).then_inc(exp_done, 1)

            def values(i, r):
                b, k = 4 * i + r, r % 2
                if later(b, 2):
                    act.wait_ge(h_ps, b - 1)
                act.wait_ge(cc_ld[r // 2 % 2], 16 * (i + r // 4) + 16)
                nc.scalar.copy(v_ext[:, k, 0:HEADS * VW].rearrange("p (h e) -> p h e", e=VW)[:, :, 0:DH],
                                      c_c[:, r % 4].rearrange("p (h e) -> p h e", e=DH)).then_inc(v_ready, 1)

            def norm_rows(i, r):
                b, k, t = 4 * i + r, r % 2, r % 4
                if later(b, 4):
                    act.wait_ge(xnT_ps, b - 3)
                    act.wait_ge(xn_st[t // 2], 16 * (i + r // 4))
                act.wait_ge(x_rs, b + 1)
                nc.scalar.activation(xn[:, t], x1[:, t], ACT.Identity, bias=x_bias[:, k, 0:1],
                                     scale=x_rstd[:, k, 0:1]).then_inc(xn_done, 1)

            def copy_xnT(i, r):
                b = 4 * i + r
                if later(b, 1):
                    act.wait_ge(lg_ps, b)
                act.wait_ge(xnT_ps, b + 1)
                nc.scalar.copy(xnT[:], ps[:, 7, 0:DC * S].rearrange("p (c s) -> p c s", s=S)).then_inc(xnT_done, 1)

            def copy_logits(i, r):
                b = 4 * i + r
                act.wait_ge(lg_ps, b + 1)
                nc.scalar.copy(logits[:, bass.ds(b, 1)].rearrange("p a e -> p (a e)"), ps[:, 7, DC * S:DC * S + E]).then_inc(lg_done, 1)

            def act_step(i, r):
                for stage, lag in ((copy_xnT, 5), (decays, 0), (copy_logits, 5), (norm_rows, 4), (values, 0)):
                    if live(4 * i + r - lag, B):
                        stage(i, r - lag)

            for r in range(8):
                act_step(0, r)
                if r == 1:
                    softplus(1)
                if r == 3:
                    exp_max(1)
            with act.Fori(2, B // 4) as i:
                for r in range(4):
                    act_step(i, r)
            for r in range(B, B + LAST_LAG):
                act_step(0, r)

            act.wait_ge(top_v, 2)
            nc.scalar.activation(rexp[:], rz[:], ACT.Exp).then_inc(rt_a, 1)
            for q in range(4):
                ks = slice(q * QK, (q + 1) * QK)
                act.wait_ge(pos_v[q // 2], 5 + q // 2)
                nc.scalar.copy(row_rep[:, q], row_i[:, ks].unsqueeze(2).broadcast_to([P, QK, P])).then_inc(row_done, 1)
                act.wait_ge(hot_v, q + 1)
                nc.scalar.mul(colval[:, ks, 1], colhot[:, ks], part_f[:, 0:1]).then_inc(cv_w, 1)

            def split_w(i, r):
                e, k = 2 * i + r // 2, r // 2 % 2
                act.wait_ge(w_ld, 32 * e + 48)
                if later(e, 2):
                    act.wait_ge(g1_ps, 2 * HC * (e - 1))
                nc.scalar.copy(w1h[:, k], w_raw1[:]).then_inc(w1h_done, 1)
                if later(e, 2):
                    act.wait_ge(y_ps, 2 * 2 * (e - 1))
                nc.scalar.copy(w2h[:, k], w_raw2[:]).then_inc(w2h_done, 1)

            def keep_weights(i, r):
                u, k = 4 * i + r, r % 2
                act.wait_ge(xg_ld[k], 16 * UT * (2 * i + r // 2 + 1))
                if later(u, 4):
                    act.wait_ge(yw_done, UT * (u - 3))
                nc.scalar.copy(w_u[:, r % 4].unsqueeze(2), xg[:, k, :, bass.ds(D + 2 * i + r // 2, 1)]).then_inc(wu_done, 1)

            def round_x(i, r):
                u, k = 4 * i + r, r % 2
                for c in range(DC):
                    act.wait_ge(xT_ps, DC * u + c + 1)
                    if later(u, 2):
                        act.wait_ge(g1_ps, HC * (u - 1))
                    nc.scalar.copy(xh[:, k, c], ps[:, c, :]).then_inc(xh_done, 1)

            def gelu(i, r):
                u = 4 * i + r
                for m in range(HC):
                    act.wait_ge(g1_ps, HC * u + m + 1)
                    if later(u, 1) or m >= 3:
                        act.wait_ge(hl_done, HC * u + m + 1 - last_use(m))
                    act.sem_inc(waited, 1)
                    nc.scalar.activation(hf[:, m % 3], ps[:, 2 + m % 3, :], ACT.Gelu,
                                         bias=b1_cols[:, bass.ds(HC * (2 * i + r // 2) + m, 1)]).then_inc(gelu_done, 1)

            def weigh_y(i, r):
                u, k = 4 * i + r, r % 2
                for j in range(UT):
                    if j % 2 == 0:
                        act.wait_ge(yb_done, 2 * u + j // 2 + 1)
                    if later(u, 2):
                        act.wait_ge(y_st, 16 * UT * (u - 1))
                    nc.scalar.mul(y_w[:, k, j], y_b[:, k, j], w_u[:, r % 4, j:j + 1]).then_inc(yw_done, 1)

            def act_unit(i, r):
                for stage, lag in ((gelu, 1), (keep_weights, 0), (round_x, 0), (split_w, 0), (weigh_y, 2)):
                    if live(4 * i + r - lag, UNITS) and (stage is not split_w or later(4 * i + r, 1) and r % 2 == 0):
                        stage(i, r - lag)

            act.wait_ge(slot_ps, 1)
            act.wait_ge(slots_done, 2)
            act.wait_ge(gw_st, 16)
            split_w(0, 0)
            for r in range(4):
                act_unit(0, r)
            with act.Fori(1, UNITS // 4) as i:
                for r in range(4):
                    act_unit(i, r)
            for r in range(UNITS, UNITS + 2):
                act_unit(0, r)

        @block.tensor
        def _(pe):
            def keep_clock(n, bank=7):
                for _ in range(n):
                    nc.tensor.matmul(ps[:, bank, 0:P], ident[:], ident[:], start=True, stop=True)

            pe.wait_ge(const_ready, 1)
            keep_clock(6)
            def turn_ctx(g, k):
                pe.wait_ge(c_ld[k], 8 * (g - k) + 16)
                for c in range(DC):
                    if later(g, 1):
                        pe.wait_ge(kT_done, DC * (g - 1) + c + 1)
                    for b in range(GB):
                        last = nc.tensor.transpose(ps[:, c, b * S:(b + 1) * S], c_in[:, k, b, c * P:(c + 1) * P], ident[:])
                    last.then_inc(kT_ps, 1)

            def turn_q(g, k):
                pe.wait_ge(q_done, GB * (g + 1))
                if later(g, 1):
                    pe.wait_ge(qT_done, g)
                for c in range(DC):
                    for b in range(GB):
                        last = nc.tensor.transpose(ps[:, 2 + c, b * S:(b + 1) * S], q_rows[:, k, b, c * P:(c + 1) * P], ident[:])
                last.then_inc(qT_ps, 1)

            def gates(g):
                pe.wait_ge(qT_done, g + 1)
                pe.wait_ge(kT_done, DC * (g + 1))
                if later(g, 1):
                    pe.wait_ge(gate_done, g)
                for c in range(DC):
                    nc.tensor.matmul(ps[0:2 * HEADS, 4, :], gate_wT[:, c], qT[:, c, bass.ds(g * GW, GW)], start=(c == 0), stop=False)
                for c in range(DC):
                    last = nc.tensor.matmul(ps[0:2 * HEADS, 4, :], gate_wk[:, c], kT[:, c, bass.ds(g * GW, GW)], start=False, stop=(c == DC - 1))
                last.then_inc(gate_ps, 1)

            for g in range(GROUPS):
                turn_ctx(g, g % 2)
                if g == 1:
                    keep_clock(2)
                if g == 2:
                    keep_clock(3)
                if g == 0:
                    pe.wait_ge(gw_ld, 16 * 3)
                    for c in range(3 * DC):
                        nc.tensor.transpose(ps[:, 5, c * 2 * HEADS:(c + 1) * 2 * HEADS], gate_rows[:, c * P:(c + 1) * P],
                                            ident[0:2 * HEADS, 0:2 * HEADS])
                    nc.tensor.transpose(ps[:, 6, 0:E * HC], b1_rows[:], ident[0:E * HC, 0:E * HC]).then_inc(wT_done, 1)
                if g == 2:
                    pe.wait_ge(wT_copied, 1)
                    pe.wait_ge(wk_ready, 1)
                if g >= 1:
                    turn_q(g - 1, (g - 1) % 2)
                if g >= 2:
                    gates(g - 2)
            gates(GROUPS - 2)
            turn_q(GROUPS - 1, (GROUPS - 1) % 2)
            gates(GROUPS - 1)

            def turn_max(t):
                pe.wait_ge(sc_a[t], 3)
                nc.tensor.transpose(ps[:, 7, t * P:(t + 1) * P], nm[:, t * S:(t + 1) * S], ident[:]).then_inc(nmT_ps, 1)

            def exponents(i, r):
                b, t = 4 * i + r, r % 4
                pe.wait_ge(pe_ld[t // 2], LOADS * (i + r // 4) + LOADS)
                if later(b, 1):
                    pe.wait_ge(exp_done, b)
                for n in range(2):
                    nc.tensor.matmul(ps[:, n, :], z_lhs[:, t], z_rhs[:, t, n * 512:(n + 1) * 512], start=True, stop=False)
                    last = nc.tensor.matmul(ps[:, n, :], ident_bf[:], mask_bf[:].rearrange("p j s -> p (j s)"), start=False, stop=True)
                last.then_inc(z_ps, 1)

            def scores(i, r):
                b, t = 4 * i + r, r % 4
                if later(b, 1):
                    pe.wait_ge(cT_done, b)
                for c in range(DC):
                    for j in range(NJ):
                        js = slice(j * DH, (j + 1) * DH)
                        last = nc.tensor.matmul(ps[:, 2 + j, c * S:(c + 1) * S], k_st[js, t // 2, c, t % 2],
                                                q_st[js, t // 2, c, t % 2], start=True, stop=True)
                last.then_inc(s_ps, 1)

            def head_sums(i, r):
                b, k = 4 * i + r, r % 2
                pe.wait_ge(cT_done, b + 1)
                pe.wait_ge(v_ready, b + 1)
                if later(b, 1):
                    pe.wait_ge(hn_done, b)
                for h in range(HEADS):
                    last = nc.tensor.matmul(ps[:, 6, h * VW:h * VW + VWIN], cT[:, k, place(h) * S:(place(h) + 1) * S],
                                            v_ext[:, k, h * VW:h * VW + VWIN], start=True, stop=True)
                last.then_inc(h_ps, 1)

            def turn_xn(i, r):
                b = 4 * i + r
                if later(b, 1):
                    pe.wait_ge(lg_done, b)
                pe.wait_ge(xn_done, b + 1)
                for c in range(DC):
                    last = nc.tensor.transpose(ps[:, 7, c * S:(c + 1) * S], xn[:, r % 4, c * P:(c + 1) * P], ident[:])
                last.then_inc(xnT_ps, 1)

            def router(i, r):
                b = 4 * i + r
                pe.wait_ge(xnT_done, b + 1)
                for c in range(DC):
                    last = nc.tensor.matmul(ps[:, 7, DC * S:DC * S + LPAD], xnT[:, c], wg_pad[:, c].rearrange("p r e -> p (r e)"),
                                            start=(c == 0), stop=(c == DC - 1))
                last.then_inc(lg_ps, 1)

            def pe_step(i, r):
                for stage, lag in ((turn_xn, 5), (exponents, 0), (scores, 0), (router, 5), (head_sums, 1)):
                    if live(4 * i + r - lag, B):
                        stage(i, r - lag)

            pe.wait_ge(const_ready, CONSTS)
            pe.wait_ge(gate_done, GROUPS)
            pe.wait_ge(const_v, 4)
            for r in range(8):
                if r == 1:
                    turn_max(0)
                if r == 5:
                    turn_max(1)
                    pe.wait_ge(nmT_done, 2)
                pe_step(0, r)
            with pe.Fori(2, B // 4) as i:
                for r in range(4):
                    pe_step(i, r)
            for r in range(B, B + LAST_LAG):
                pe_step(0, r)

            for k in range(TOP):
                pe.wait_ge(oh_done, k + 1)
                oh = onehot[:, k].rearrange("p e b -> p (e b)")
                nc.tensor.matmul(ps[:, 2 * k, 0:E * B], ones_bf[:], oh, start=True, stop=True)
                nc.tensor.matmul(ps[:, 2 * k + 1, 0:E * B], later_bf[:], oh, start=True, stop=True).then_inc(count_ps, 1)
            pe.wait_ge(lg_done, B)
            for q in range(4):
                if q == 2:
                    keep_clock(8)
                pe.wait_ge(cv_id, q + 1)
                pe.wait_ge(cv_w, q + 1)
                pe.wait_ge(rh_done, q + 1)
                for kt in range(q * QK, (q + 1) * QK):
                    last = nc.tensor.matmul(ps[:, 4, 0:2 * W], rowhot[:, kt], colval[:, kt].rearrange("p a w -> p (a w)"),
                                            start=(kt == 0), stop=(kt == KT - 1))
            last.then_inc(slot_ps, 1)

            def turn_x(i, r):
                u, k = 4 * i + r, r % 2
                pe.wait_ge(xg_ld[k], 16 * UT * (2 * i + r // 2 + 1))
                for c in range(DC):
                    if later(u, 1):
                        pe.wait_ge(xl_done, DC * (u - 1) + c + 1)
                    for j in range(UT):
                        last = nc.tensor.transpose(ps[:, c, j * P:(j + 1) * P], xg[:, k, j, c * P:(c + 1) * P], ident[:])
                    last.then_inc(xT_ps, 1)

            def hidden(i, r):
                u, k, wk = 4 * i + r, r % 2, r // 2 % 2
                if k == 0:
                    pe.wait_ge(w1l_done, 2 * i + r // 2 + 1)
                for m in range(HC):
                    bank = 2 + m % 3
                    if later(u, 1) or m >= 3:
                        pe.wait_ge(gelu_done, HC * u + m + 1 - last_use(m))
                    ms = slice(m * P, (m + 1) * P)
                    for c in range(DC):
                        if m == 0:
                            pe.wait_ge(xl_done, DC * u + c + 1)
                        nc.tensor.matmul(ps[:, bank, :], w1h[:, wk, c, ms], xh[:, k, c], start=(c == 0), stop=False)
                        nc.tensor.matmul(ps[:, bank, :], w1h[:, wk, c, ms], xl[:, k, c], start=False, stop=False)
                        last = nc.tensor.matmul(ps[:, bank, :], w1l[:, wk, c, ms], xh[:, k, c], start=False, stop=(c == DC - 1))
                    last.then_inc(g1_ps, 1)

            def outputs(i, r):
                u, k, wk = 4 * i + r, r % 2, r // 2 % 2
                if k == 0:
                    pe.wait_ge(w2l_done, 2 * i + r // 2 + 1)
                pe.wait_ge(hl_done, HC * (u + 1))
                for j in range(UT):
                    if j % 2 == 0 and later(u, 1):
                        pe.wait_ge(yb_done, 2 * (u - 1) + j // 2 + 1)
                    js = slice(j * P, (j + 1) * P)
                    o = ps[:, 5 + j // 2, (j % 2) * D:(j % 2 + 1) * D]
                    for m in range(HC):
                        nc.tensor.matmul(o, hh[:, k, m, js], w2h[:, wk, m], start=(m == 0), stop=False)
                        nc.tensor.matmul(o, hh[:, k, m, js], w2l[:, wk, m], start=False, stop=False)
                        last = nc.tensor.matmul(o, hl[:, k, m, js], w2h[:, wk, m], start=False, stop=(m == HC - 1))
                    if j % 2 == 1:
                        last.then_inc(y_ps, 1)

            def pe_unit(i, r):
                for stage, lag in ((hidden, 1), (turn_x, 0), (outputs, 2)):
                    if live(4 * i + r - lag, UNITS):
                        stage(i, r - lag)

            pe.wait_ge(slots_done, 2)
            keep_clock(14)
            for r in range(4):
                pe_unit(0, r)
            with pe.Fori(1, UNITS // 4) as i:
                for r in range(4):
                    pe_unit(i, r)
            for r in range(UNITS, UNITS + 2):
                pe_unit(0, r)

        @block.vector
        def _(dve):
            nc.vector.memset(zero_rows[:, 0:CAP * D // P // 2], 0.0).then_inc(const_v, 1)

            def stats(g, k):
                dve.wait_ge(x_ld[k], 8 * (g - k) + 16)
                if later(g, 1):
                    dve.wait_ge(stats_done, g)
                if later(g, 2):
                    dve.wait_ge(q_done, GB * (g - 1))
                    dve.wait_ge(rstd_done, g - 1)
                for b in range(GB):
                    last = nc.vector.bn_stats(g_stats[:, b], x_in[:, k, b])
                last.then_inc(g_seq, 1)
                dve.wait_ge(g_seq, g + 1)
                dve.sem_inc(waited, 1)
                for b in range(GB):
                    last = nc.vector.bn_aggr(g_mv[:, k, b], g_stats[:, b])
                last.then_inc(stats_done, 1)

            def normalise(g, k):
                dve.wait_ge(rstd_done, g + 1)
                dve.wait_ge(stats_done, g + 1)
                if later(g, 2):
                    dve.wait_ge(qT_ps, g - 1)
                for b in range(GB):
                    nc.vector.tensor_scalar(q_rows[:, k, b], x_in[:, k, b], g_mv[:, k, b, 0:1], g_rstd[:, k, b:b + 1],
                                            ALU.subtract, ALU.mult).then_inc(q_done, 1)

            def copy_qT(g):
                dve.wait_ge(qT_ps, g + 1)
                nc.vector.tensor_copy(qT[:, :, bass.ds(g * GW, GW)], ps[:, 2:4, :]).then_inc(qT_done, 1)

            def fgate_abs(t):
                dve.wait_ge(pair_ld[t], 16 * 2)
                nc.vector.scalar_tensor_tensor(out=fa[:, t * S:(t + 1) * S], in0=fg_p[:, t], scalar=-1.0, in1=fg_p[:, t], op0=ALU.mult,
                                               op1=ALU.min).then_inc(sc_v[t], 1)

            def scans(t):
                ts = slice(t * S, (t + 1) * S)
                dve.wait_ge(sc_a[t], 2)
                nc.vector.scalar_tensor_tensor(out=logf[:, ts], in0=fg_p[:, t], scalar=0.0, in1=fl[:, ts], op0=ALU.min,
                                               op1=ALU.subtract).then_inc(sc_v[t], 1)
                dve.wait_ge(sc_v[t], 2)
                nc.vector.tensor_tensor_scan(cs[:, ts], ones_row[:], logf[:, ts], 0.0, ALU.mult, ALU.add).then_inc(sc_v[t], 1)
                dve.wait_ge(sc_v[t], 3)
                nc.vector.tensor_tensor(av[:, ts], ig_p[:, t], cs[:, ts], ALU.subtract).then_inc(sc_v[t], 1)

            def scan_max(t):
                ts = slice(t * S, (t + 1) * S)
                dve.wait_ge(sc_v[t], 4)
                nc.vector.tensor_tensor_scan(mv[:, ts], zero_row[:], av[:, ts], LOWEST, ALU.add, ALU.max).then_inc(sc_v[t], 1)
                dve.wait_ge(sc_v[t], 5)
                nc.vector.tensor_scalar(negm[:, ts], mv[:, ts], -1.0, None, ALU.mult).then_inc(sc_v[t], 1)
                nc.vector.tensor_tensor(msum[:, ts], cs[:, ts], mv[:, ts], ALU.add).then_inc(sc_v[t], 1)

            def split_scans(t):
                ts = slice(t * S, (t + 1) * S)
                dve.wait_ge(sc_v[t], 6)
                for n, src in ((0, av), (1, negm)):
                    nc.vector.tensor_copy(parts[:, n, 0, ts], src[:, ts]).then_inc(sc_v[t], 1)
                for n, src in ((0, av), (1, negm)):
                    dve.wait_ge(sc_v[t], 8 + n)
                    nc.vector.tensor_tensor(res1[:, n, ts], src[:, ts], parts[:, n, 0, ts], ALU.subtract).then_inc(sc_v[t], 1)
                for n in range(2):
                    dve.wait_ge(sc_v[t], 10 + n)
                    nc.vector.tensor_copy(parts[:, n, 1, ts], res1[:, n, ts]).then_inc(sc_v[t], 1)
                for n in range(2):
                    dve.wait_ge(sc_v[t], 12 + n)
                    nc.vector.tensor_tensor(parts[:, n, 2, ts], res1[:, n, ts], parts[:, n, 1, ts], ALU.subtract).then_inc(sc_v[t], 1)

            def keep_max(t):
                dve.wait_ge(nmT_ps, t + 1)
                nc.vector.tensor_scalar(nmT[:, t * P:(t + 1) * P], ps[:, 7, t * P:(t + 1) * P], NORM_EPS, None, ALU.add).then_inc(nmT_done, 1)

            stats(0, 0)
            dve.wait_ge(wT_copied, 1)
            nc.vector.tensor_tensor(gate_wk[:], gate_wT[:, DC:2 * DC], gate_wT[:, 2 * DC:3 * DC], ALU.add).then_inc(wk_ready, 1)
            for g in range(1, GROUPS):
                if g >= 2:
                    copy_qT(g - 2)
                normalise(g - 1, (g - 1) % 2)
                if g == GROUPS - 1:
                    fgate_abs(0)
                stats(g, g % 2)
                if g == 3:
                    nc.vector.memset(zero_rows[:, CAP * D // P // 2:], 0.0).then_inc(const_v, 1)
                if g == 4:
                    nc.vector.memset(ones_bf[:], 1.0)
                    nc.vector.memset(ones_row[:], 1.0)
                    nc.vector.memset(zero_row[:], 0.0)
                    dve.wait_ge(misc_ld, 16 * MISC)
                    nc.vector.tensor_copy(wg_pad[:], wg_sb[:].unsqueeze(2).broadcast_to([P, DC, LPAD // E, E])).then_inc(const_v, 1)
                    dve.wait_ge(tg_done, 1)
                    nc.vector.tensor_scalar(ls_t[:], ls[:], tanh_g[:, 0:1], None, ALU.mult).then_inc(const_v, 1)
            copy_qT(GROUPS - 2)
            scans(0)
            scan_max(0)
            normalise(GROUPS - 1, (GROUPS - 1) % 2)
            split_scans(0)
            copy_qT(GROUPS - 1)

            def weigh(i, r):
                b, k = 4 * i + r, r % 2
                if later(b, 2):
                    dve.wait_ge(h_ps, b - 1)
                dve.wait_ge(exp_done, b + 1)
                dve.wait_ge(s_ps, b + 1)
                nc.vector.scalar_tensor_tensor(out=cT[:, k].rearrange("p (j x) -> p j x", j=NJ), in0=ps[:, 2:6, 0:DC * S],
                                               scalar=float(DH) ** -0.5,
                                               in1=decay[:, k].rearrange("p (j x) -> p j x", j=NJ), op0=ALU.mult,
                                               op1=ALU.mult).then_inc(cT_done, 1)

            hp = ps[:, 6, 0:HEADS * VW].rearrange("p (h w) -> p h w", w=VW)
            hrow = hn[:].rearrange("p k h e -> p k (h e)")

            def head_den(i, r):
                b, k = 4 * i + r, r % 2
                if later(b, 2):
                    dve.wait_ge(hsc_done, b - 1)
                dve.wait_ge(h_ps, b + 1)
                nc.vector.scalar_tensor_tensor(out=den[:, k].unsqueeze(2), in0=hp[:, :, DH:DH + 1], scalar=NORM_EPS,
                                               in1=nmT[:, bass.ds(b * HEADS, HEADS)].unsqueeze(2),
                                               op0=ALU.subtract, op1=ALU.max, reverse0=True).then_inc(p1_seq, 1)

            def head_den2(i, r):
                k = r % 2
                dve.wait_ge(p1_seq, 4 * (4 * i + r) + 1)
                nc.vector.scalar_tensor_tensor(out=den2[:, k].unsqueeze(2), in0=hp[:, :, DH:DH + 1], scalar=NORM_EPS,
                                               in1=den[:, k].unsqueeze(2), op0=ALU.add, op1=ALU.max).then_inc(p1_seq, 1)

            def head_rden(i, r):
                k = r % 2
                dve.wait_ge(p1_seq, 4 * (4 * i + r) + 2)
                nc.vector.reciprocal(rden[:, k], den2[:, k]).then_inc(p1_seq, 1)

            def head_scale(i, r):
                k = r % 2
                dve.wait_ge(p1_seq, 4 * (4 * i + r) + 3)
                nc.vector.tensor_tensor(hn[:, k], hp[:, :, 0:DH], rden[:, k].unsqueeze(2).broadcast_to([P, HEADS, DH]),
                                        ALU.mult).then_inc(hn_done, 1)

            def head_stats(i, r):
                dve.wait_ge(hn_done, 4 * i + r + 1)
                nc.vector.bn_stats(h_st[:, r % 2], hrow[:, r % 2]).then_inc(p1_seq, 1)

            def head_mean(i, r):
                b, k = 4 * i + r, r % 2
                if later(b, 2):
                    dve.wait_ge(h_rs, b - 1)
                dve.wait_ge(p1_seq, 4 * b + 4)
                dve.sem_inc(waited, 1)
                nc.vector.bn_aggr(h_mv[:, k], h_st[:, k]).then_inc(h_stat, 1)

            def head_center(i, r):
                b, k = 4 * i + r, r % 2
                if later(b, 2):
                    dve.wait_ge(x1_done, b - 1)
                dve.wait_ge(h_stat, b + 1)
                nc.vector.scalar_tensor_tensor(out=h_sc[:, k], in0=hrow[:, k], scalar=h_mv[:, k, 0:1], in1=ls_t[:],
                                               op0=ALU.subtract, op1=ALU.mult).then_inc(hsc_done, 1)

            def residual(i, r):
                b, k, t = 4 * i + r, r % 2, r % 4
                dve.wait_ge(hsc_done, b + 1)
                dve.wait_ge(xc_ld[t // 2], 16 * (i + r // 4) + 16)
                if later(b, 4):
                    dve.wait_ge(xn_done, b - 3)
                    dve.wait_ge(x1_st[t // 2], 16 * (i + r // 4))
                dve.wait_ge(h_rs, b + 1)
                nc.vector.scalar_tensor_tensor(out=x1[:, t], in0=h_sc[:, k], scalar=h_rstd[:, k], in1=x_c[:, t],
                                               op0=ALU.mult, op1=ALU.add).then_inc(x1_done, 1)

            def row_stats(i, r):
                b = 4 * i + r
                if later(b, 1):
                    dve.wait_ge(x_stat, b)
                dve.wait_ge(x1_done, b + 1)
                nc.vector.bn_stats(x_st[:], x1[:, r % 4]).then_inc(x1_seq, 1)

            def row_mean(i, r):
                b, k = 4 * i + r, r % 2
                if later(b, 2):
                    dve.wait_ge(x_rs, b - 1)
                    dve.wait_ge(xn_done, b - 1)
                dve.wait_ge(x1_seq, b + 1)
                dve.sem_inc(waited, 1)
                nc.vector.bn_aggr(x_mv[:, k], x_st[:]).then_inc(x_stat, 1)

            def dve_step(i, r):
                for stage, lag in ((head_den, 2), (head_den2, 2), (head_rden, 2), (head_scale, 2), (residual, 3), (weigh, 0),
                                   (row_stats, 3), (head_stats, 2), (row_mean, 3), (head_mean, 2), (head_center, 2)):
                    if live(4 * i + r - lag, B):
                        stage(i, r - lag)

            dve.wait_ge(const_v, 4)
            for r in range(8):
                dve_step(0, r)
                if r == 0:
                    fgate_abs(1)
                if r == 1:
                    keep_max(0)
                    dve.wait_ge(nmT_done, 1)
                    scans(1)
                if r == 2:
                    scan_max(1)
                if r == 4:
                    keep_max(1)
                    split_scans(1)
            with dve.Fori(2, B // 4) as i:
                for r in range(4):
                    dve_step(i, r)
            for r in range(B, B + LAST_LAG):
                dve_step(0, r)

            def over(t, n=E):
                return t.unsqueeze(2).broadcast_to([P, B, n])

            dve.wait_ge(rt_p, E + 10)
            for k in range(2):
                dve.wait_ge(xn_st[k], 16 * (B // 4))
                dve.wait_ge(x1_st[k], 16 * (B // 4))
            dve.wait_ge(lg_done, B)
            nc.vector.tensor_reduce(rmax[:], logits[:], AX_X, ALU.max).then_inc(top_v, 1)
            dve.wait_ge(top_v, 1)
            nc.vector.tensor_tensor(rz[:], logits[:], over(rmax[:]), ALU.subtract).then_inc(top_v, 1)

            def first_key():
                dve.wait_ge(top_v, 2)
                nc.vector.scalar_tensor_tensor(out=rkey[:, 0], in0=rz[:], scalar=0.0, in1=rank[:], op0=ALU.is_ge,
                                               op1=ALU.mult).then_inc(top_v, 1)

            def top_rank(k):
                dve.wait_ge(top_v, (3, 9)[k])
                nc.vector.tensor_reduce(kmax[:, k], rkey[:, k], AX_X, ALU.max).then_inc(top_v, 1)

            def top_chosen(k):
                dve.wait_ge(top_v, (4, 10)[k])
                nc.vector.tensor_tensor(chosen[:, k], rank[:], over(kmax[:, k]), ALU.is_equal).then_inc(top_v, 1)

            def top_onehot(k):
                dve.wait_ge(top_v, (5, 11)[k])
                nc.vector.tensor_copy(onehot[:, k].rearrange("p e b -> p b e"), chosen[:, k]).then_inc(oh_done, 1)

            def drop_first():
                dve.wait_ge(rt_a, 1)
                nc.vector.scalar_tensor_tensor(out=score[:], in0=chosen[:, 0], scalar=-2.0, in1=rexp[:],
                                               op0=ALU.mult, op1=ALU.add).then_inc(top_v, 1)

            def second_best():
                dve.wait_ge(top_v, 6)
                nc.vector.tensor_reduce(best[:, 1], score[:], AX_X, ALU.max).then_inc(top_v, 1)

            def second_equal():
                dve.wait_ge(top_v, 7)
                nc.vector.tensor_tensor(req[:], score[:], over(best[:, 1]), ALU.is_equal).then_inc(top_v, 1)

            def second_key():
                dve.wait_ge(top_v, 8)
                nc.vector.tensor_tensor(rkey[:, 1], req[:], rank[:], ALU.mult).then_inc(top_v, 1)

            def pos_before(k):
                dve.wait_ge(count_ps, k + 1)
                nc.vector.tensor_tensor_scan(before[:, k].rearrange("p e b -> p (e b)"), reset[:].rearrange("p e b -> p (e b)"),
                                             ps[:, 2 * k, 0:E * B], 0.0, ALU.mult, ALU.add).then_inc(pos_v[k], 1)

            def pos_after():
                dve.wait_ge(pos_v[1], 1)
                nc.vector.scalar_tensor_tensor(out=after[:], in0=before[:, 1], scalar=-1.0,
                                               in1=before[:, 0, :, B - 1:B].broadcast_to([P, E, B]),
                                               op0=ALU.add, op1=ALU.add).then_inc(pos_v[1], 1)

            def pos_first():
                dve.wait_ge(pos_v[0], 1)
                nc.vector.scalar_tensor_tensor(out=loc[:, 0], in0=before[:, 0], scalar=-1.0,
                                               in1=ps[:, 1, 0:E * B].rearrange("p (e b) -> p e b", b=B),
                                               op0=ALU.add, op1=ALU.add).then_inc(pos_v[0], 1)

            def pos_second():
                dve.wait_ge(pos_v[1], 2)
                nc.vector.tensor_tensor(loc[:, 1], after[:], ps[:, 3, 0:E * B].rearrange("p (e b) -> p e b", b=B),
                                        ALU.add).then_inc(pos_v[1], 1)

            def pos_own(k):
                dve.wait_ge(pos_v[k], 2 + k)
                nc.vector.tensor_tensor(locsel[:, k], loc[:, k], onehot[:, k], ALU.mult).then_inc(pos_v[k], 1)

            def pos_sum(k):
                dve.wait_ge(pos_v[k], 3 + k)
                with nc.allow_low_precision(reason="whole numbers below 2 ** 24"):
                    nc.vector.tensor_reduce(pos_i[:, k * B:(k + 1) * B], locsel[:, k].rearrange("p e b -> p b e"), AX_X,
                                            ALU.add).then_inc(pos_v[k], 1)

            def pos_cut(k):
                kb = slice(k * B, (k + 1) * B)
                dve.wait_ge(pos_v[k], 4 + k)
                nc.vector.tensor_scalar(row_i[:, kb], pos_i[:, kb], SLOT_TILES.bit_length() - 1, None,
                                        ALU.arith_shift_right).then_inc(pos_v[k], 1)
                nc.vector.tensor_scalar(col_i[:, kb], pos_i[:, kb], SLOT_TILES - 1, None, ALU.bitwise_and)
                nc.vector.tensor_scalar(col_b[:, kb], kmax[:, k], -float(SLOT_TILES), float(W), ALU.mult, ALU.add).then_inc(pos_v[k], 1)

            def pos_column(k):
                kb = slice(k * B, (k + 1) * B)
                dve.wait_ge(pos_v[k], 6 + k)
                nc.vector.tensor_tensor(col_s[:, kb], col_i[:, kb], col_b[:, kb], ALU.add).then_inc(pos_v[k], 1)

            def hot_columns(q):
                ks = slice(q * QK, (q + 1) * QK)
                dve.wait_ge(pos_v[q // 2], 7 + q // 2)
                nc.vector.tensor_tensor(colhot[:, ks], iota_bf[:, 0:W].unsqueeze(1).broadcast_to([P, QK, W]),
                                        col_s[:, ks].unsqueeze(2).broadcast_to([P, QK, W]), ALU.is_equal).then_inc(hot_v, 1)

            def hot_rows(q):
                dve.wait_ge(rep_done, 1)
                dve.wait_ge(row_done, q + 1)
                nc.vector.tensor_tensor(rowhot[:, q * QK:(q + 1) * QK], iota_rep[:], row_rep[:, q], ALU.is_equal).then_inc(rh_done, 1)

            def soft_sum():
                dve.wait_ge(rt_a, 1)
                nc.vector.tensor_reduce(rsum[:], rexp[:], AX_X, ALU.add).then_inc(gw_v, 1)

            def first_best():
                nc.vector.tensor_reduce(best[:, 0], rexp[:], AX_X, ALU.max).then_inc(gw_v, 1)

            def soft_rec():
                dve.wait_ge(gw_v, 1)
                nc.vector.reciprocal(rrec[:], rsum[:]).then_inc(gw_v, 1)

            def soft_best():
                dve.wait_ge(gw_v, 3)
                nc.vector.tensor_tensor(probs[:], best[:], rrec[:].unsqueeze(1).broadcast_to([P, TOP, B]), ALU.mult).then_inc(gw_v, 1)

            def weight_sum():
                dve.wait_ge(gw_v, 4)
                nc.vector.tensor_tensor(gsum[:], probs[:, 0], probs[:, 1], ALU.add).then_inc(gw_v, 1)

            def weight_clip():
                dve.wait_ge(gw_v, 5)
                nc.vector.tensor_scalar(gclip[:], gsum[:], GATE_EPS, None, ALU.max).then_inc(gw_v, 1)

            def weight_rec():
                dve.wait_ge(gw_v, 6)
                nc.vector.reciprocal(grec[:], gclip[:]).then_inc(gw_v, 1)

            first_key()
            top_rank(0)
            top_chosen(0)
            top_onehot(0)
            drop_first()
            second_best()
            second_equal()
            pos_before(0)
            second_key()
            top_rank(1)
            pos_first()
            top_chosen(1)
            pos_own(0)
            top_onehot(1)
            pos_sum(0)
            soft_sum()
            pos_cut(0)
            first_best()
            pos_column(0)
            soft_rec()
            pos_before(1)
            hot_columns(0)
            soft_best()
            hot_columns(1)
            pos_after()
            weight_sum()
            hot_rows(0)
            pos_second()
            weight_clip()
            hot_rows(1)
            pos_own(1)
            weight_rec()
            pos_sum(1)
            pos_cut(1)
            pos_column(1)
            for q in range(2, 4):
                hot_columns(q)
                hot_rows(q)
            dve.wait_ge(slot_ps, 1)
            nc.vector.tensor_copy(slot_n[:].rearrange("p a w -> p (a w)"), ps[:, 4, 0:2 * W]).then_inc(rt_v, 1)
            dve.wait_ge(rt_v, 1)
            nc.vector.scalar_tensor_tensor(out=slot_t[:], in0=slot_n[:, 0], scalar=float(S), in1=slot_n[:, 1], op0=ALU.mult,
                                           op1=ALU.add).then_inc(rt_v, 1)
            nc.vector.tensor_scalar(empty[:], slot_n[:, 0], 0.0, None, ALU.is_equal).then_inc(rt_v, 1)
            dve.wait_ge(rt_v, 2)
            nc.vector.tensor_scalar(gather_idx[:], slot_t[:], -float(P), 0.0, ALU.add, ALU.max).then_inc(slots_done, 1)
            dve.wait_ge(rt_v, 3)
            nc.vector.tensor_tensor(dumped[:], empty[:], dump[:], ALU.mult).then_inc(rt_v, 1)
            dve.wait_ge(rt_v, 4)
            nc.vector.scalar_tensor_tensor(out=scatter_idx[:], in0=slot_t[:], scalar=-float(P), in1=dumped[:],
                                           op0=ALU.add, op1=ALU.add).then_inc(slots_done, 1)

            def rest_w(i, r):
                e, k = 2 * i + r // 2, r // 2 % 2
                dve.wait_ge(w1h_done, e + 1)
                nc.vector.tensor_tensor(w1l[:, k], w_raw1[:], w1h[:, k].bitcast(F32), ALU.subtract).then_inc(w1l_done, 1)
                dve.wait_ge(w2h_done, e + 1)
                nc.vector.tensor_tensor(w2l[:, k], w_raw2[:], w2h[:, k].bitcast(F32), ALU.subtract).then_inc(w2l_done, 1)

            def rest_x(i, r):
                u, k = 4 * i + r, r % 2
                for c in range(DC):
                    dve.wait_ge(xh_done, DC * u + c + 1)
                    nc.vector.tensor_tensor(xl[:, k, c], ps[:, c, :], xh[:, k, c].bitcast(F32), ALU.subtract).then_inc(xl_done, 1)

            def split_h(i, r):
                u, k = 4 * i + r, r % 2
                if later(u, 2):
                    dve.wait_ge(y_ps, 2 * (u - 1))
                for m in range(HC):
                    dve.wait_ge(gelu_done, HC * u + m + 1)
                    nc.vector.tensor_copy(hh[:, k, m], hf[:, m % 3]).then_inc(hh_done, 1)
                    dve.wait_ge(hh_done, HC * u + m + 1)
                    nc.vector.tensor_tensor(hl[:, k, m], hf[:, m % 3], hh[:, k, m].bitcast(F32), ALU.subtract).then_inc(hl_done, 1)

            def bias_y(i, r):
                u, k = 4 * i + r, r % 2
                for j in range(UT // 2):
                    dve.wait_ge(y_ps, 2 * u + j + 1)
                    if later(u, 2):
                        dve.wait_ge(yw_done, UT * (u - 1))
                    nc.vector.tensor_tensor(y_b[:, k, 2 * j:2 * j + 2], ps[:, 5 + j, :].rearrange("p (a d) -> p a d", d=D),
                                            b2_all[:, bass.ds(2 * i + r // 2, 1)].broadcast_to([P, 2, D]), ALU.add).then_inc(yb_done, 1)

            def dve_unit(i, r):
                for stage, lag in ((split_h, 1), (rest_x, 0), (rest_w, 0), (bias_y, 2)):
                    if live(4 * i + r - lag, UNITS) and (stage is not rest_w or later(4 * i + r, 1) and r % 2 == 0):
                        stage(i, r - lag)

            rest_w(0, 0)
            for r in range(4):
                dve_unit(0, r)
            with dve.Fori(1, UNITS // 4) as i:
                for r in range(4):
                    dve_unit(i, r)
            for r in range(UNITS, UNITS + 2):
                dve_unit(0, r)


_INS = ['x', 'ctx_1024', 'g_xattn', 'g_ffn', 'L0_xattn_igate_w', 'L0_xattn_igate_b', 'L0_xattn_fgate_w',
        'L0_xattn_fgate_b', 'L0_xattn_ln_scale', 'L0_ffn_wg', 'L0_ffn_w1', 'L0_ffn_b1', 'L0_ffn_w2', 'L0_ffn_b2']
SHAPE = (32, 128, 256)
SPARE = 1024
_OUTS = [((SHAPE[0] * SHAPE[1] + SPARE, SHAPE[2]), 'float32')]


def kernel(**inputs):
    import numpy as _np
    import concourse.bacc as _bacc
    from concourse import mybir as _mybir
    from concourse.bass_utils import run_bass_kernel_spmd as _run

    nc = _bacc.Bacc("TRN2", target_bir_lowering=False, num_devices=1)
    arrays, args = {}, []
    for name in _INS:
        a = _np.ascontiguousarray(inputs[name])
        arrays[f"in_{name}_dram"] = a
        args.append(nc.dram_tensor(f"in_{name}_dram", a.shape, _mybir.dt.from_np(a.dtype), kind="ExternalInput").ap())
    for i, (shape, dtype) in enumerate(_OUTS):
        dt = _mybir.dt.from_np(_np.dtype(dtype))
        args.append(nc.dram_tensor(f"out_{i}_dram", shape, dt, kind="ExternalOutput").ap())
    flamingo_block(nc, *args)
    r = _run(nc, [arrays], core_ids=[0])
    got = tuple(r.results[0][f"out_{i}_dram"] for i in range(len(_OUTS)))
    return got[0][:SHAPE[0] * SHAPE[1]].reshape(SHAPE)
```
